# Optimizing a Trainium2 kernel written in Bass

```python
import numpy as np
import jax
import jax.numpy as jnp

def _softmax(x, axis=-1):
    return jax.nn.softmax(x, axis=axis)

def _gelu(x):
    return jax.nn.gelu(x, approximate=True)

def _silu(x):
    return jax.nn.silu(x)

def _sigmoid(x):
    return jax.nn.sigmoid(x)

def _layernorm(x, axis=-1, eps=1e-05):
    m = jnp.mean(x, axis=axis, keepdims=True)
    v = jnp.var(x, axis=axis, keepdims=True)
    return (x - m) / jnp.sqrt(v + eps)

def _scatter_add(tgt, idx, src, axis=0):
    return tgt.at[idx].add(src)

def _segment_sum(src, seg, n):
    return jax.ops.segment_sum(src, seg, n)
kernel_name = 'mk_conv_attn_hybrid_d2_conv_nhwc256_r2_70dcaf'

def setup_inputs(seed: int=0):
    np.random.seed(seed)
    _w = jnp.asarray

    def _rec_inputs():
        import jax
        import jax.numpy as jnp
        _gk = jax.random.key(seed)
        x = -0.000125 + 0.9999 * jax.random.normal(jax.random.fold_in(_gk, 1), (32, 32, 32, 128), jnp.float32)
        return x
    x = _rec_inputs()

    def _L0_conv_setup():
        import jax, jax.numpy as jnp
        import numpy as np
        WS, SS, HEADS = (8, 4, 8)

        def _static_consts(H, W):
            ws, ss = (WS, SS)
            r = np.arange(-(ws - 1), ws, dtype=np.float32)
            tbl = np.stack(np.meshgrid(r, r, indexing='ij'), axis=-1)
            tbl = tbl / (ws - 1) * 8.0
            tbl = np.sign(tbl) * np.log2(np.abs(tbl) + 1.0) / np.log2(8.0)
            tbl = tbl.reshape(-1, 2)
            c = np.stack(np.meshgrid(np.arange(ws), np.arange(ws), indexing='ij')).reshape(2, -1)
            rel = (c[:, :, None] - c[:, None, :]).transpose(1, 2, 0).copy()
            rel[..., 0] += ws - 1
            rel[..., 1] += ws - 1
            rel[..., 0] *= 2 * ws - 1
            idx = rel.sum(-1)
            img = np.zeros((H, W), dtype=np.int32)
            cnt = 0
            for hs in (slice(0, -ws), slice(-ws, -ss), slice(-ss, None)):
                for wsl in (slice(0, -ws), slice(-ws, -ss), slice(-ss, None)):
                    img[hs, wsl] = cnt
                    cnt += 1
            mw = img.reshape(H // ws, ws, W // ws, ws).transpose(0, 2, 1, 3).reshape(-1, ws * ws)
            mask = np.where(mw[:, None, :] != mw[:, :, None], -100.0, 0.0).astype(np.float32)
            return (jnp.asarray(tbl), jnp.asarray(idx), jnp.asarray(mask))

        def _fwd(x, Wq, bq, Wk, bk, Wv, bv, Wo, bo, logit_scale, cpb_w1, cpb_b1, cpb_w2):
            B, H, W, C = x.shape
            ws, ss, h = (WS, SS, HEADS)
            N, dh = (ws * ws, C // HEADS)
            tbl, idx, mask = _static_consts(H, W)
            xs = jnp.roll(x, (-ss, -ss), axis=(1, 2))
            nh, nw = (H // ws, W // ws)
            xw = xs.reshape(B, nh, ws, nw, ws, C).transpose(0, 1, 3, 2, 4, 5).reshape(B * nh * nw, N, C)

            def proj(t, Wm, bm):
                return (t @ Wm.T + bm).reshape(-1, N, h, dh).transpose(0, 2, 1, 3)
            q, k, v = (proj(xw, Wq, bq), proj(xw, Wk, bk), proj(xw, Wv, bv))
            qn = q / jnp.maximum(jnp.linalg.norm(q, axis=-1, keepdims=True), 1e-12)
            kn = k / jnp.maximum(jnp.linalg.norm(k, axis=-1, keepdims=True), 1e-12)
            scale = jnp.exp(jnp.minimum(logit_scale, jnp.log(100.0)))
            attn = jnp.einsum('whnd,whmd->whnm', qn, kn) * scale[None]
            bias = 16.0 * jax.nn.sigmoid(jax.nn.relu(tbl @ cpb_w1.T + cpb_b1) @ cpb_w2.T)
            attn = attn + bias[idx].transpose(2, 0, 1)[None]
            attn = attn.reshape(B, nh * nw, h, N, N) + mask[None, :, None]
            attn = jax.nn.softmax(attn, axis=-1).reshape(B * nh * nw, h, N, N)
            out = jnp.einsum('whnm,whmd->whnd', attn, v).transpose(0, 2, 1, 3).reshape(-1, N, C)
            out = out @ Wo.T + bo
            out = out.reshape(B, nh, nw, ws, ws, C).transpose(0, 1, 3, 2, 4, 5).reshape(B, H, W, C)
            return jnp.roll(out, (ss, ss), axis=(1, 2))
        key = jax.random.key(seed)
        ks = jax.random.split(key, 12)
        B, H, W, C = (32, 32, 32, 128)
        p = lambda i, shp, s=0.05: jax.random.normal(ks[i], shp, dtype=jnp.float32) * s
        return {'x': p(0, (B, H, W, C), 1.0), 'Wq': p(1, (C, C)), 'bq': p(2, (C,)), 'Wk': p(3, (C, C)), 'bk': p(4, (C,)), 'Wv': p(5, (C, C)), 'bv': p(6, (C,)), 'Wo': p(7, (C, C)), 'bo': p(8, (C,)), 'logit_scale': jnp.full((HEADS, 1, 1), jnp.log(10.0), dtype=jnp.float32), 'cpb_w1': p(9, (256, 2)), 'cpb_b1': p(10, (256,)), 'cpb_w2': p(11, (HEADS, 256))}
    _L0_conv_all = _L0_conv_setup()
    _L0_conv_in = {k: v for k, v in _L0_conv_all.items() if k in ('Wq', 'bq', 'Wk', 'bk', 'Wv', 'bv', 'Wo', 'bo', 'logit_scale', 'cpb_w1', 'cpb_b1', 'cpb_w2')}
    del _L0_conv_all

    def _L1_attn_setup():
        import jax, jax.numpy as jnp
        import numpy as np
        DIM = 128
        HEADS = 4
        WIN = 128
        RADIUS = 32
        HEAD_DIM = DIM // HEADS
        SCALE = HEAD_DIM ** (-0.5)
        NEG_INF = -1e+30

        def _band_mask(T, radius):
            i = jnp.arange(T)[:, None]
            j = jnp.arange(T)[None, :]
            d = i - j
            return jnp.where((d >= 0) & (d <= radius), 0.0, -jnp.inf).astype(jnp.float32)
        key = jax.random.key(seed)
        k1, k2, k3 = jax.random.split(key, 3)
        B, T, C = (16, 2048, DIM)
        x = jax.random.normal(k1, (B, T, C), dtype=jnp.float32)
        Wqkv = jax.random.normal(k2, (C, 3 * C), dtype=jnp.float32) * 0.02
        Wproj = jax.random.normal(k3, (C, C), dtype=jnp.float32) * 0.02
        bproj = jnp.zeros((C,), dtype=jnp.float32)
        return {'x': x, 'Wqkv': Wqkv, 'Wproj': Wproj, 'bproj': bproj}
    _L1_attn_all = _L1_attn_setup()
    _L1_attn_in = {k: v for k, v in _L1_attn_all.items() if k in ('Wqkv', 'Wproj', 'bproj')}
    del _L1_attn_all

    def _L1_ffn_setup():
        import jax, jax.numpy as jnp
        import numpy as np
        B, T, D, H, E = (16, 2048, 128, 256, 8)
        key = jax.random.key(seed)
        ks = jax.random.split(key, 5)
        x = jax.random.normal(ks[0], (B, T, D), dtype=jnp.float32)
        gate_w = jax.random.normal(ks[1], (D, E), dtype=jnp.float32) * 0.02
        gate_b = jnp.zeros((E,), dtype=jnp.float32)
        W1 = jax.random.normal(ks[2], (E, D, H), dtype=jnp.float32) * 0.02
        b1 = jnp.zeros((E, H), dtype=jnp.float32)
        W2 = jax.random.normal(ks[3], (E, H, D), dtype=jnp.float32) * 0.02
        b2 = jnp.zeros((E, D), dtype=jnp.float32)
        return {'x': x, 'gate_w': gate_w, 'gate_b': gate_b, 'W1': W1, 'b1': b1, 'W2': W2, 'b2': b2}
    _L1_ffn_all = _L1_ffn_setup()
    _L1_ffn_in = {k: v for k, v in _L1_ffn_all.items() if k in ('gate_w', 'gate_b', 'W1', 'b1', 'W2', 'b2')}
    del _L1_ffn_all
    return {'x': x, 'L0_conv_Wq': _L0_conv_in['Wq'], 'L0_conv_bq': _L0_conv_in['bq'], 'L0_conv_Wk': _L0_conv_in['Wk'], 'L0_conv_bk': _L0_conv_in['bk'], 'L0_conv_Wv': _L0_conv_in['Wv'], 'L0_conv_bv': _L0_conv_in['bv'], 'L0_conv_Wo': _L0_conv_in['Wo'], 'L0_conv_bo': _L0_conv_in['bo'], 'L0_conv_logit_scale': _L0_conv_in['logit_scale'], 'L0_conv_cpb_w1': _L0_conv_in['cpb_w1'], 'L0_conv_cpb_b1': _L0_conv_in['cpb_b1'], 'L0_conv_cpb_w2': _L0_conv_in['cpb_w2'], 'L1_attn_Wqkv': _L1_attn_in['Wqkv'], 'L1_attn_Wproj': _L1_attn_in['Wproj'], 'L1_attn_bproj': _L1_attn_in['bproj'], 'L1_ffn_gate_w': _L1_ffn_in['gate_w'], 'L1_ffn_gate_b': _L1_ffn_in['gate_b'], 'L1_ffn_W1': _L1_ffn_in['W1'], 'L1_ffn_b1': _L1_ffn_in['b1'], 'L1_ffn_W2': _L1_ffn_in['W2'], 'L1_ffn_b2': _L1_ffn_in['b2']}

def reference(x, L0_conv_Wq, L0_conv_bq, L0_conv_Wk, L0_conv_bk, L0_conv_Wv, L0_conv_bv, L0_conv_Wo, L0_conv_bo, L0_conv_logit_scale, L0_conv_cpb_w1, L0_conv_cpb_b1, L0_conv_cpb_w2, L1_attn_Wqkv, L1_attn_Wproj, L1_attn_bproj, L1_ffn_gate_w, L1_ffn_gate_b, L1_ffn_W1, L1_ffn_b1, L1_ffn_W2, L1_ffn_b2):
    import jax
    import jax.numpy as jnp

    def _L0_conv_ref(x, Wq, bq, Wk, bk, Wv, bv, Wo, bo, logit_scale, cpb_w1, cpb_b1, cpb_w2):
        import jax, jax.numpy as jnp
        import numpy as np
        WS, SS, HEADS = (8, 4, 8)

        def _static_consts(H, W):
            ws, ss = (WS, SS)
            r = np.arange(-(ws - 1), ws, dtype=np.float32)
            tbl = np.stack(np.meshgrid(r, r, indexing='ij'), axis=-1)
            tbl = tbl / (ws - 1) * 8.0
            tbl = np.sign(tbl) * np.log2(np.abs(tbl) + 1.0) / np.log2(8.0)
            tbl = tbl.reshape(-1, 2)
            c = np.stack(np.meshgrid(np.arange(ws), np.arange(ws), indexing='ij')).reshape(2, -1)
            rel = (c[:, :, None] - c[:, None, :]).transpose(1, 2, 0).copy()
            rel[..., 0] += ws - 1
            rel[..., 1] += ws - 1
            rel[..., 0] *= 2 * ws - 1
            idx = rel.sum(-1)
            img = np.zeros((H, W), dtype=np.int32)
            cnt = 0
            for hs in (slice(0, -ws), slice(-ws, -ss), slice(-ss, None)):
                for wsl in (slice(0, -ws), slice(-ws, -ss), slice(-ss, None)):
                    img[hs, wsl] = cnt
                    cnt += 1
            mw = img.reshape(H // ws, ws, W // ws, ws).transpose(0, 2, 1, 3).reshape(-1, ws * ws)
            mask = np.where(mw[:, None, :] != mw[:, :, None], -100.0, 0.0).astype(np.float32)
            return (jnp.asarray(tbl), jnp.asarray(idx), jnp.asarray(mask))

        def _fwd(x, Wq, bq, Wk, bk, Wv, bv, Wo, bo, logit_scale, cpb_w1, cpb_b1, cpb_w2):
            B, H, W, C = x.shape
            ws, ss, h = (WS, SS, HEADS)
            N, dh = (ws * ws, C // HEADS)
            tbl, idx, mask = _static_consts(H, W)
            xs = jnp.roll(x, (-ss, -ss), axis=(1, 2))
            nh, nw = (H // ws, W // ws)
            xw = xs.reshape(B, nh, ws, nw, ws, C).transpose(0, 1, 3, 2, 4, 5).reshape(B * nh * nw, N, C)

            def proj(t, Wm, bm):
                return (t @ Wm.T + bm).reshape(-1, N, h, dh).transpose(0, 2, 1, 3)
            q, k, v = (proj(xw, Wq, bq), proj(xw, Wk, bk), proj(xw, Wv, bv))
            qn = q / jnp.maximum(jnp.linalg.norm(q, axis=-1, keepdims=True), 1e-12)
            kn = k / jnp.maximum(jnp.linalg.norm(k, axis=-1, keepdims=True), 1e-12)
            scale = jnp.exp(jnp.minimum(logit_scale, jnp.log(100.0)))
            attn = jnp.einsum('whnd,whmd->whnm', qn, kn) * scale[None]
            bias = 16.0 * jax.nn.sigmoid(jax.nn.relu(tbl @ cpb_w1.T + cpb_b1) @ cpb_w2.T)
            attn = attn + bias[idx].transpose(2, 0, 1)[None]
            attn = attn.reshape(B, nh * nw, h, N, N) + mask[None, :, None]
            attn = jax.nn.softmax(attn, axis=-1).reshape(B * nh * nw, h, N, N)
            out = jnp.einsum('whnm,whmd->whnd', attn, v).transpose(0, 2, 1, 3).reshape(-1, N, C)
            out = out @ Wo.T + bo
            out = out.reshape(B, nh, nw, ws, ws, C).transpose(0, 1, 3, 2, 4, 5).reshape(B, H, W, C)
            return jnp.roll(out, (ss, ss), axis=(1, 2))
        return _fwd(x, Wq, bq, Wk, bk, Wv, bv, Wo, bo, logit_scale, cpb_w1, cpb_b1, cpb_w2)

    def _L1_attn_ref(x, Wqkv, Wproj, bproj):
        import jax, jax.numpy as jnp
        import numpy as np
        DIM = 128
        HEADS = 4
        WIN = 128
        RADIUS = 32
        HEAD_DIM = DIM // HEADS
        SCALE = HEAD_DIM ** (-0.5)
        NEG_INF = -1e+30

        def _band_mask(T, radius):
            i = jnp.arange(T)[:, None]
            j = jnp.arange(T)[None, :]
            d = i - j
            return jnp.where((d >= 0) & (d <= radius), 0.0, -jnp.inf).astype(jnp.float32)
        B_prev, T_prev, C = x.shape
        xw = x.reshape(-1, WIN, C)
        Bw = xw.shape[0]
        qkv = xw @ Wqkv
        qkv = qkv.reshape(Bw, WIN, 3, HEADS, HEAD_DIM)
        qkv = qkv.transpose(2, 0, 3, 1, 4)
        q, k, v = (qkv[0], qkv[1], qkv[2])
        attn = jnp.einsum('bhid,bhjd->bhij', q, k) * SCALE
        attn = attn + _band_mask(WIN, RADIUS)[None, None]
        attn = jax.nn.softmax(attn, axis=-1)
        out = jnp.einsum('bhij,bhjd->bhid', attn, v)
        out = out.transpose(0, 2, 1, 3).reshape(Bw, WIN, C)
        out = out @ Wproj + bproj
        return out.reshape(B_prev, T_prev, C)

    def _L1_ffn_ref(x, gate_w, gate_b, W1, b1, W2, b2):
        import jax, jax.numpy as jnp
        import numpy as np
        B, T, D, H, E = (16, 2048, 128, 256, 8)
        Bb, Tt, Dd = x.shape
        Ee = gate_w.shape[1]
        xf = x.reshape(-1, Dd)
        N = xf.shape[0]
        logits = xf @ gate_w + gate_b
        probs = jax.nn.softmax(logits, axis=-1)
        top2_vals, top2_idx = jax.lax.top_k(probs, 2)
        cw = jnp.zeros((N, Ee), dtype=xf.dtype).at[jnp.arange(N)[:, None], top2_idx].add(top2_vals)

        def step(acc, params):
            w1, bb1, w2, bb2, we = params
            h = jax.nn.gelu(xf @ w1 + bb1, approximate=False)
            y = h @ w2 + bb2
            return (acc + we[:, None] * y, None)
        out, _ = jax.lax.scan(step, jnp.zeros_like(xf), (W1, b1, W2, b2, cw.T))
        return out.reshape(Bb, Tt, Dd)

    def _gn(v, G=32, eps=1e-05):
        B_, H_, W_, C_ = v.shape
        g = v.reshape(B_, H_, W_, G, C_ // G)
        m = jnp.mean(g, axis=(1, 2, 4), keepdims=True)
        s = jnp.var(g, axis=(1, 2, 4), keepdims=True)
        return ((g - m) / jnp.sqrt(s + eps)).reshape(v.shape)

    def _ln_c(v, eps=1e-06):
        m = jnp.mean(v, axis=-1, keepdims=True)
        s = jnp.var(v, axis=-1, keepdims=True)
        return (v - m) / jnp.sqrt(s + eps)

    def _ln_t(v, eps=1e-05):
        m = jnp.mean(v, axis=-1, keepdims=True)
        s = jnp.var(v, axis=-1, keepdims=True)
        return (v - m) / jnp.sqrt(s + eps)

    def _to_tokens(v):
        B_, H_, W_, C_ = v.shape
        return v.reshape(B_, H_ * W_, C_)

    def _from_tokens(t, like):
        return t.reshape(like.shape)
    x = x + _L0_conv_ref(_gn(x), L0_conv_Wq, L0_conv_bq, L0_conv_Wk, L0_conv_bk, L0_conv_Wv, L0_conv_bv, L0_conv_Wo, L0_conv_bo, L0_conv_logit_scale, L0_conv_cpb_w1, L0_conv_cpb_b1, L0_conv_cpb_w2)
    t = _to_tokens(x)
    t = t + _L1_attn_ref(_ln_t(t), L1_attn_Wqkv, L1_attn_Wproj, L1_attn_bproj)
    t = t + _L1_ffn_ref(_ln_t(t), L1_ffn_gate_w, L1_ffn_gate_b, L1_ffn_W1, L1_ffn_b1, L1_ffn_W2, L1_ffn_b2)
    x = _from_tokens(t, x)
    return x

_drawn_inputs = setup_inputs


def setup_inputs(seed=0):
    import zlib

    import numpy as np

    out = dict(_drawn_inputs(seed))
    spreads = {'L0_conv_logit_scale': (2.3025851249694824, 0.2),
     'L1_attn_bproj': (0.0, 0.1),
     'L1_ffn_gate_b': (0.0, 0.627),
     'L1_ffn_b1': (0.0, 0.8),
     'L1_ffn_b2': (0.0, 0.348)}
    factors = {'L0_conv_bk': 2.821,
     'L0_conv_cpb_w1': 8.0,
     'L0_conv_cpb_b1': 8.0,
     'L0_conv_cpb_w2': 8.0,
     'L1_attn_Wqkv': 4.657,
     'L1_attn_Wproj': 4.591,
     'L1_ffn_W1': 6.697,
     'L1_ffn_W2': 6.056}
    for name, (base, spread) in spreads.items():
        noise = np.random.default_rng([zlib.crc32(name.encode()), seed]).standard_normal(out[name].shape)
        drawn = base * np.exp(spread * noise) if base else spread * noise
        out[name] = jnp.asarray(drawn.astype(out[name].dtype))
    for name, factor in factors.items():
        out[name] = (out[name] * factor).astype(out[name].dtype)
    return out
```

```python
from contextlib import ExitStack

import concourse.bass as bass
import numpy as np
from concourse import mybir

P = 128
IMAGES, SIDE, D = 32, 32, 128
TOKENS = SIDE * SIDE
TILES = TOKENS // P
ROWS = P // SIDE
HALF = TOKENS // 2
WS, SHIFT = 8, 4
WTOK = WS * WS
WINDOWS = TOKENS // WTOK
HA, DA = 8, 16
PAIRS = HA // 2
HB, DB = 4, 32
RADIUS = 32
E, HID = 8, 256
CH = HID // P
GROUP = 4
VA = 2 * DA + 2
VB = DB + 1
REL = 2 * WS - 1
GATE_PARTS = 3

F32 = mybir.dt.float32
BF16 = mybir.dt.bfloat16
ALU = mybir.AluOpType
ACT = mybir.ActivationFunctionType
AX_X = mybir.AxisListType.X
EXP_LN_SET = "natural_log_exp_and_others"

NORM_SHIFT = 20
LN2 = float(np.log(2.0))
NORM_CAP = 1e12
MASKED = -1e30

CONST = {}


def _columns():
    at = 0
    for name, width in (("identity", P), ("group_mean", P), ("head_ones", P), ("head_mask_a", HA), ("head_mask_b", HB),
                        ("tri", E * E), ("mask_a", 4 * WTOK), ("mask_b", P)):
        CONST[name] = (at, at + width)
        at += width
    return at


CONST_WIDTH = _columns()


def shape_constants():
    c = np.zeros((P, CONST_WIDTH), np.float32)

    def put(name, value):
        a, _ = CONST[name]
        value = np.asarray(value, np.float32)
        c[:value.shape[0], a:a + value.shape[1]] = value

    ch = np.arange(P)
    put("identity", np.eye(P))
    put("group_mean", (ch[:, None] // GROUP == ch[None] // GROUP) / GROUP)
    put("head_ones", ch[:, None] // DA == ch[None] // DA)
    put("head_mask_a", ch[:, None] // DA == np.arange(HA)[None])
    put("head_mask_b", ch[:, None] // DB == np.arange(HB)[None])
    e = np.arange(E)
    put("tri", np.broadcast_to((e[None] < e[:, None]).reshape(1, -1), (P, E * E)))
    img = np.zeros((SIDE, SIDE), np.int32)
    cuts = (slice(0, -WS), slice(-WS, -SHIFT), slice(-SHIFT, None))
    for a, hs in enumerate(cuts):
        for b, ws in enumerate(cuts):
            img[hs, ws] = 3 * a + b
    win = img.reshape(SIDE // WS, WS, SIDE // WS, WS).transpose(0, 2, 1, 3).reshape(SIDE // WS, SIDE // WS, WTOK)
    for bottom in range(2):
        for right in range(2):
            pair = win[3 * bottom, 2 * right:2 * right + 2]
            m = np.where(pair[:, :, None] != pair[:, None, :], -100.0, 0.0).reshape(P, WTOK)
            a = CONST["mask_a"][0] + (2 * bottom + right) * WTOK
            c[:, a:a + WTOK] = m
    n = SIDE * (ch // SIDE) + (ch % SIDE + SHIFT) % SIDE
    d = n[:, None] - n[None]
    put("mask_b", np.where((d >= 0) & (d <= RADIUS), 0.0, MASKED))
    r = np.arange(-(WS - 1), WS, dtype=np.float32)
    tbl = np.stack(np.meshgrid(r, r, indexing="ij"), axis=-1) / (WS - 1) * 8.0
    tbl = (np.sign(tbl) * np.log2(np.abs(tbl) + 1.0) / np.log2(8.0)).reshape(-1, 2)
    table = tbl[::-1].T.astype(np.float32)
    q = ch % WTOK
    unfold = np.stack([(np.arange(WS)[:, None] == WS - 1 - q[None] % WS) & (WS - 1 - q[None] // WS == py)
                       for py in range(WS)], axis=1).astype(np.float32).reshape(WS, WS * P)
    return c, table, unfold


def expert_selectors():
    s = np.zeros((GATE_PARTS * E, E, P), np.float32)
    for e in range(E):
        s[e::E, e] = 1.0
    return s.reshape(GATE_PARTS * E, E * P)


def count(image, per, k):
    if isinstance(image, int):
        image, k = (image, k) if 0 <= image < IMAGES else ((0, 0) if image < 0 else (IMAGES, 0))
        v = image * per + k
        return v if v > 0 else None
    return image * per + k


def hybrid_kernel(nc, x, wq, bq, wk, bk, wv, bv, wo, bo, logit_scale, cpb_w1, cpb_b1, cpb_w2,
                  w_qkv, w_proj, b_proj, gate_w, gate_b, w1, b1, w2, b2, consts, rel_table, unfold, selectors, out):
    scratch = nc.dram_tensor("rel_bias_scratch", [HA, REL * REL], F32)
    x_rolled = x.rearrange("a (t r) c d -> a r c t d", r=ROWS)
    out_rolled = out.rearrange("a (t r) c d -> a r c t d", r=ROWS)
    col_pieces = (((0, SIDE - SHIFT), (SHIFT, SIDE)), ((SIDE - SHIFT, SIDE), (0, SHIFT)))
    IO_DMAS = ROWS * len(col_pieces)

    with ExitStack() as ctx:
        def sb(name, shape, dt=F32):
            return ctx.enter_context(nc.sbuf_tensor(name, shape, dt))

        def bank(name):
            return ctx.enter_context(nc.psum_tensor(name, [P, HALF], F32))

        def sem(name):
            return ctx.enter_context(nc.semaphore(name))

        k = sb("k_consts", [P, CONST_WIDTH])

        def const(name, rows=P):
            a, b = CONST[name]
            return k[0:rows, a:b]

        ident = const("identity")
        sel = sb("expert_sel", [GATE_PARTS * E, E * P], BF16)
        ident16 = sb("ident16", [P, P], BF16)
        wq_s, wk_s, wv_s, wo_s = (sb(n, [P, P]) for n in ("wq_s", "wk_s", "wv_s", "wo_s"))
        wqkv_s = sb("wqkv_s", [P, 3 * P])
        wp_s = sb("wp_s", [P, P])
        gw_s = sb("gw_s", [P, E])
        w1_s = sb("w1_s", [P, E, HID])
        w2_s = sb("w2_s", [P, E, CH, P])
        b1_s = sb("b1_s", [P, E * CH])
        b2_s = sb("b2_s", [GATE_PARTS * E, P])
        b2_p = sb("b2_p", [GATE_PARTS * E, GATE_PARTS, P], BF16)
        b2_r = sb("b2_r", [GATE_PARTS * E, 2, P])
        cols = sb("cols", [P, 8])
        row_a = sb("row_a", [P, P])
        row_b = sb("row_b", [P, P])
        bo_s = sb("bo_s", [P, P])
        gb_s = sb("gb_s", [P, E])
        cw1_s = sb("cw1_s", [2, HID])
        cb1_s = sb("cb1_s", [P, CH])
        cw2_s = sb("cw2_s", [P, CH, HA])
        bias_a = sb("bias_a", [P, 4, HA, WTOK])
        eps5 = sb("eps5", [P, 4])

        pad = sb("pad", [P, 2])

        xin = sb("xin", [P, TILES, D])
        x_res = sb("x_res", [P, TILES, D])
        xn_a = sb("xn_a", [P, TOKENS])
        gstat = sb("gstat", [P, 24])
        qk_a = sb("qk_a", [P, 4, HALF])
        sq_a = sb("sq_a", [P, 4, HALF])
        xraw = sq_a[:, 0:2, :].rearrange("p a n -> p (a n)")
        km_a = sb("km_a", [P, HA, TOKENS])
        hid_s = km_a[:, 0, 0:CH * REL * REL].rearrange("p (c n) -> p c n", c=CH)
        rel_s = km_a[0:HA, 1, 0:REL * REL]
        tab_s = km_a[0:2, 1, HALF:HALF + REL * REL]
        unf_s = km_a[0:WS, 2, 0:HA * REL * WS].rearrange("p (y w) -> p y w", w=WS)
        fold_s = km_a[0:WS, 3, :]
        v_a = sb("v_a", [P, TILES + 1, PAIRS, 2, VA])
        ot_a = sb("ot_a", [P, TOKENS])
        t1 = sb("t1", [P, TILES, D])
        t1b = sb("t1b", [P, TILES, D])
        st_b = sb("st_b", [P, TILES, 6])
        mv_b = sb("mv_b", [P, TILES, 2])
        rs_b = sb("rs_b", [P, 3, TILES])
        xn_b = sb("xn_b", [P, TILES, D])
        xt_b = sb("xt_b", [P, TOKENS])
        q_b = sb("q_b", [P, TOKENS])
        k_b = xn_b[:, :, :].rearrange("p t d -> p (t d)")
        km_b = sb("km_b", [P, HB, TOKENS])
        v_b = sb("v_b", [P, TILES, HB, VB])
        ot_b = sb("ot_b", [P, TOKENS])
        t2 = sb("t2", [P, TILES, D])
        st_c = sb("st_c", [P, TILES, 6])
        mv_c = sb("mv_c", [P, TILES, 2])
        rs_c = sb("rs_c", [P, 3, TILES])
        xn_c = sb("xn_c", [P, TILES, D])
        xt_c = sb("xt_c", [P, TOKENS])
        lg = sb("lg", [P, TILES, E])
        pr = sb("pr", [P, TILES, E])
        col_c = sb("col_c", [P, 3, TILES])
        rank_c = sb("rank_c", [P, TILES, E])
        cw = sb("cw", [P, 3, TILES, E])
        cw3 = sb("cw3", [P, TILES, GATE_PARTS, E], BF16)
        cwt = sb("cwt", [GATE_PARTS * E, TOKENS], BF16)
        hid = sb("hid", [P, 8, HALF])
        cmp_c = [hid[:, 4 + n, :].rearrange("p (t e f) -> p t e f", t=TILES, e=E) for n in range(2)]
        y_s = sb("y_s", [P, HALF])
        s_sb = [sb("s_sb_a", [P, HA, WTOK]), sb("s_sb_b", [P, HB, P])]
        mx_s = [sb("mx_a", [P, HA]), sb("mx_b", [P, HB])]
        p_sb = [sb("p_sb_a", [P, 4, P]), sb("p_sb_b", [P, 4, P])]
        pt_sb = [sb("pt_sb_a", [P, 4, P]), sb("pt_sb_b", [P, 4, P])]
        rc_s = [sb("rc_a", [P, HA]), sb("rc_b", [P, HB])]
        on_s = [sb("on_a", [P, D]), sb("on_b", [P, D])]

        Z = [bank("bank_z0"), bank("bank_z1")]
        Y, W, SA, SB, T, O = (bank(n) for n in ("bank_y", "bank_w", "bank_sa", "bank_sb", "bank_t", "bank_o"))

        loaded = sem("loaded")
        setup = sem("setup")
        setup_act = sem("setup_act")
        bias_io = sem("bias_io")
        ready = sem("ready")
        x_in, x_copied, res_ready = sem("x_in"), sem("x_copied"), sem("res_ready")
        gn = sem("gn")
        xt_a_ready = sem("xt_a_ready")
        qk_ready, qk_sb, sq_ready, ss_ready, ln_ready, rn_ready, qn_ready, km_ready, av_ready, av_sb = (
            sem(n) for n in ("qk_ready", "qk_sb", "sq_ready", "ss_ready", "ln_ready", "rn_ready", "qn_ready",
                             "km_ready", "av_ready", "av_sb"))
        outa_ready, outb_ready = sem("outa_ready"), sem("outb_ready")
        ln_b, ln_c = sem("ln_b"), sem("ln_c")
        t1b_ready = sem("t1b_ready")
        bqk_ready, bqk_sb, bkm_ready, bv_ready, bv_sb = (
            sem(n) for n in ("bqk_ready", "bqk_sb", "bkm_ready", "bv_ready", "bv_sb"))
        gate = sem("gate")
        two = ("a", "b")
        s_ready, s_added, s_max, s_sub, p_ready, pt_ready, pt_copied, o_ready, o_rc, o_norm, ot_ready, ot_copied = (
            [sem(f"{n}_{w}") for w in two] for n in ("s_ready", "s_added", "s_max", "s_sub", "p_ready", "pt_ready",
                                                     "pt_copied", "o_ready", "o_rc", "o_norm", "ot_ready", "ot_copied"))
        web_ready, z_ready, gelu_ready, hw_ready, y_done, y_copied, yt_ready, fin_ready, stored = (
            sem(n) for n in ("web_ready", "z_ready", "gelu_ready", "hw_ready", "y_done", "y_copied", "yt_ready",
                             "fin_ready", "stored"))

        STEPS = TILES + 1
        LN_STEPS, GN_STEPS, GATE_STEPS = 33, 18, 21
        UNITS = 4 * TILES

        def need(eng, s, image, per, kth):
            v = count(image, per, kth)
            if v is not None:
                eng.wait_ge(s, v)

        def schedule(eng, body):
            for i in range(3):
                body(i, True, i >= 1, i >= 2)
            with eng.Fori(3, IMAGES) as i:
                body(i, True, True, True)
            for i in range(IMAGES, IMAGES + 2):
                body(i, False, i <= IMAGES, True)

        def unit(t, m):
            return t // 4, 2 * (t % 4) + m // 2, m % 2

        block = ctx.enter_context(nc.Block())

        loads = [(k[:], consts), (tab_s, rel_table), (fold_s, unfold), (sel[:], selectors), (wq_s[:], wq), (wk_s[:], wk), (wv_s[:], wv), (wo_s[:], wo),
                 (wqkv_s[:], w_qkv), (wp_s[:], w_proj), (gw_s[:], gate_w),
                 (w1_s[:], w1.rearrange("e p n -> p e n")),
                 (w2_s[:], w2.rearrange("e (c p) n -> p e c n", p=P)), (b1_s[:], b1),
                 (cols[:, 0:1], bq), (cols[:, 1:2], bk), (cols[:, 2:3], bv), (cols[:, 3:4], logit_scale),
                 (row_b[:], b_proj.to_broadcast([P, P])), (bo_s[:], bo.to_broadcast([P, P])),
                 (gb_s[:], gate_b.to_broadcast([P, E])), (cw1_s[:], cpb_w1), (cb1_s[:], cpb_b1),
                 (cw2_s[:], cpb_w2.rearrange("(c p) n -> p c n", p=P))]
        loads += [(b2_s[E * g:E * g + E, :], b2) for g in range(GATE_PARTS)]

        @block.sync
        def _(sp):
            for dst, src in loads:
                sp.dma_start(dst, src).then_inc(loaded, 16)

            def load_image(i):
                for r in range(ROWS):
                    for (p0, p1), (c0, c1) in col_pieces:
                        sp.dma_start(xin[SIDE * r + p0:SIDE * r + p1, :, :], x_rolled[i, r, c0:c1, :, :]).then_inc(x_in, 16)

            def store_image(c):
                for r in range(ROWS):
                    for (p0, p1), (c0, c1) in col_pieces:
                        sp.dma_start(out_rolled[c, r, c0:c1, :, :], xn_c[SIDE * r + p0:SIDE * r + p1, :, :]).then_inc(stored, 16)

            load_image(0)
            sp.wait_ge(setup, 9)
            sp.dma_start(scratch.ap(), rel_s).then_inc(bias_io, 16)
            sp.wait_ge(bias_io, 16)
            unfolded = bass.AP(scratch, 0, [[1, WS], [REL, HA * REL], [1, WS]])
            sp.dma_start(unf_s, unfolded).then_inc(bias_io, 16)

            def body(i, do_a, do_b, do_c):
                a, b, c = i, i - 1, i - 2
                if do_a:
                    need(sp, x_in, a, 16 * IO_DMAS, 16 * IO_DMAS)
                    need(sp, ln_b, b, LN_STEPS, 2)
                    sp.dma_start(x_res[:], xin[:]).then_inc(x_copied, 16)
                if not isinstance(i, int) or i < IMAGES:
                    need(sp, xt_a_ready, a, 2, 2)
                    need(sp, x_copied, a, 16, 16)
                    if isinstance(i, int):
                        if i + 1 < IMAGES:
                            load_image(i + 1)
                    else:
                        load_image(i + 1)
                if do_c:
                    need(sp, fin_ready, c, 2, 2)
                    store_image(c)

            for i in range(3):
                body(i, True, i >= 1, i >= 2)
            with sp.Fori(3, IMAGES - 1) as i:
                body(i, True, True, True)
            for i in range(IMAGES - 1, IMAGES + 2):
                body(i, i < IMAGES, i <= IMAGES, True)
            sp.wait_ge(stored, 16 * IO_DMAS * IMAGES)

        @block.tensor
        def _(pe):
            mm, tr = pe.matmul, pe.transpose
            pe.wait_ge(loaded, 16 * len(loads))
            for c in range(CH):
                last = mm(Z[c][:, 0:REL * REL], cw1_s[:, c * P:(c + 1) * P], tab_s, start=True, stop=True)
            last.then_inc(setup, 1)
            pe.wait_ge(setup, 3)
            for c in range(CH):
                last = mm(Y[0:HA, 0:REL * REL], cw2_s[:, c, :], hid_s[:, c, :], start=(c == 0), stop=(c == CH - 1))
            last.then_inc(setup, 1)
            mm(W[:, 0:P], cols[:, 2:3].to_broadcast([P, P]), wo_s[:], start=True, stop=True).then_inc(setup, 1)
            pe.wait_ge(bias_io, 32)
            for py in range(WS):
                last = mm(SA[:, :].rearrange("p (h n) -> p h n", h=HA), fold_s[:, py * P:py * P + P],
                          unf_s.rearrange("p (h y) w -> p h (y w)", h=HA)[:, :, py * WS:py * WS + WTOK],
                          start=(py == 0), stop=(py == WS - 1))
            last.then_inc(setup, 1)
            pe.wait_ge(ready, 3)

            def tokens(j):
                return slice(P * j, P * j + P)

            def rolled(t):
                return (t - SHIFT // ROWS) % TILES

            def window(w):
                return slice(WTOK * w, WTOK * w + WTOK)

            q_flat = qk_a[:, 0:2, :].rearrange("p a n -> p (a n)")

            def prepare(a, b, c, do_a, do_b, do_c):
                if do_a:
                    need(pe, x_in, a, 16 * IO_DMAS, 16 * IO_DMAS)
                    need(pe, gelu_ready, c - 1, UNITS, UNITS)
                    need(pe, bv_sb, b - 1, 2, 2)
                    for h in range(2):
                        for j in range(4):
                            tile = (4 * h + j + SHIFT // ROWS) % TILES
                            last = tr(Z[h][:, P * j:P * j + P], xin[:, tile, :], ident)
                        last.then_inc(xt_a_ready, 1)
                if do_c:
                    need(pe, ot_copied[1], c, TILES, TILES)
                    need(pe, y_copied, c - 1, 2, 2)
                    need(pe, hw_ready, c - 1, UNITS, UNITS)
                    for h, dst in enumerate((Y, W)):
                        for j in range(4):
                            t = 4 * h + j
                            last = mm(dst[:, P * j:P * j + P], ot_b[:, tokens(t)], wp_s[:], start=True, stop=True)
                        last.then_inc(outb_ready, 1)
                if do_b:
                    need(pe, ot_copied[0], b, TILES, TILES)
                    need(pe, s_added[0], b, TILES, TILES)
                    need(pe, s_added[1], b - 1, TILES, TILES)
                    for h, dst in enumerate((SA, SB)):
                        for j in range(4):
                            t = 4 * h + j
                            last = mm(dst[:, P * j:P * j + P], ot_a[:, tokens(rolled(t))], wo_s[:], start=True, stop=True)
                        last.then_inc(outa_ready, 1)
                if do_a:
                    need(pe, gn, a, GN_STEPS, 5)
                    need(pe, o_norm[0], b, TILES, TILES)
                    need(pe, o_norm[1], b - 1, TILES, TILES)
                    mm(O[:, 0:2], const("group_mean"), gstat[:, 12:14], start=True, stop=True).then_inc(gn, 1)
                    need(pe, gn, a, GN_STEPS, 9)
                    mm(O[:, 2:3], const("group_mean"), gstat[:, 17:18], start=True, stop=True).then_inc(gn, 1)
                if do_c:
                    need(pe, ln_c, c, LN_STEPS, 29)
                    for h, dst in enumerate((Y, W)):
                        for j in range(4):
                            last = tr(dst[:, P * j:P * j + P], xn_c[:, 4 * h + j, :], ident)
                        last.then_inc(ln_c, 1)
                if do_b:
                    need(pe, ln_b, b, LN_STEPS, 29)
                    need(pe, gn, a, GN_STEPS, 11)
                    need(pe, ot_copied[0], b, TILES, TILES)
                    need(pe, ot_copied[1], b - 1, TILES, TILES)
                    need(pe, fin_ready, c - 1, 2, 2)
                    for h, dst in enumerate((T, O)):
                        for j in range(4):
                            last = tr(dst[:, P * j:P * j + P], xn_b[:, 4 * h + j, :], ident)
                        last.then_inc(ln_b, 1)
                if do_a:
                    need(pe, gn, a, GN_STEPS, GN_STEPS)
                    need(pe, ln_b, b, LN_STEPS, 2)
                    for n, (w, dst) in enumerate(((wq_s, Z[0]), (wq_s, Z[1]), (wk_s, SA), (wk_s, SB))):
                        h = n % 2
                        mm(dst[:, :], w[:], xn_a[:, HALF * h:HALF * h + HALF], start=True, stop=True).then_inc(qk_ready, 1)
                if do_c:
                    need(pe, ln_c, c, LN_STEPS, 33)
                    for t in range(TILES):
                        last = mm(W[:, E * t:E * t + E], xt_c[:, tokens(t)], gw_s[:], start=True, stop=True)
                    last.then_inc(gate, 1)
                if do_b:
                    need(pe, ln_b, b, LN_STEPS, 33)
                    for n, (w0, dst) in enumerate(((0, Z[0]), (0, Z[1]), (P, SA), (P, SB))):
                        h = n % 2
                        need(pe, qk_sb, a, 4, n + 1)
                        mm(dst[:, :], wqkv_s[:, w0:w0 + P], xt_b[:, HALF * h:HALF * h + HALF],
                           start=True, stop=True).then_inc(bqk_ready, 1)
                if do_a:
                    for n, dst in enumerate((Y, T, O, Y)):
                        need(pe, sq_ready, a, 4, n + 1)
                        if n == 0:
                            need(pe, ln_c, c, LN_STEPS, 32)
                        if n == 1:
                            need(pe, ln_b, b, LN_STEPS, 33)
                        if n == 3:
                            need(pe, ln_ready, a, 4, 1)
                        mm(dst[:, :], const("head_ones"), sq_a[:, n, :], start=True, stop=True).then_inc(ss_ready, 1)
                if do_b:
                    for h, dst in enumerate(Z):
                        need(pe, bqk_sb, b, 4, h + 1)
                        for j in range(4):
                            last = mm(dst[:, P * j:P * j + P], xt_b[:, tokens(4 * h + j)], wqkv_s[:, 2 * P:3 * P],
                                      start=True, stop=True)
                        last.then_inc(bv_ready, 1)
                if do_a:
                    for g, dst in enumerate((SA, SB, T, O)):
                        need(pe, bqk_sb, b, 4, 3 + g if g < 2 else 4)
                        need(pe, qk_sb, a, 4, 4)
                        if g >= 2:
                            need(pe, ln_ready, a, 4, g)
                        for j in range(4):
                            for half in range(2):
                                last = mm(dst[WTOK * half:WTOK * half + WTOK, P * j:P * j + P],
                                          xn_a[:, window(4 * g + j)], wv_s[:], start=True, stop=True)
                        last.then_inc(av_ready, 1)
                if do_c:
                    need(pe, gate, c, GATE_STEPS, 19)
                    wt = W[:, :].bitcast(BF16)
                    for t in range(TILES):
                        last = tr(wt[0:GATE_PARTS * E, tokens(t)], cw3[:, t, :, :].rearrange("p g e -> p (g e)"), ident16[:])
                    last.then_inc(gate, 1)

            def expert_bias(c, half):
                need(pe, gate, c, GATE_STEPS, 21)
                if half == 0:
                    need(pe, ln_ready, c + 2, 4, 4)
                    need(pe, ln_c, c, LN_STEPS, 32)
                else:
                    need(pe, y_copied, c, 2, 1)
                for g in range(GATE_PARTS):
                    mm(Y[:, :], b2_p[:, g, :], cwt[:, HALF * half:HALF * half + HALF], start=(g == 0), stop=False)

            def scores(t, w, a, b, c):
                if w == 0:
                    need(pe, km_ready, a, HA, HA)
                    need(pe, av_sb, a, 8, 8)
                    if t > 0:
                        need(pe, s_added[0], a, TILES, t)
                    for j in range(2):
                        last = mm(SA[WTOK * j:WTOK * j + WTOK, :], q_flat[:, window(2 * t + j)], km_a[:, :, window(2 * t + j)],
                                  start=True, stop=True)
                else:
                    need(pe, bkm_ready, b, HB, HB)
                    need(pe, bqk_sb, b, 4, 4)
                    need(pe, av_sb, b + 1, 8, 8)
                    if t > 0:
                        need(pe, s_added[1], b, TILES, t)
                    last = mm(SB[:, :], q_b[:, tokens(t)], km_b[:, :, tokens(t)], start=True, stop=True)
                last.then_inc(s_ready[w], 1)

            def transposed_probs(t, w, n, other, c):
                need(pe, p_ready[w], n, TILES, t + 1)
                if w == 0:
                    if t == 0:
                        need(pe, av_sb, n, 8, 8)
                        need(pe, ln_b, other, LN_STEPS, 33)
                    else:
                        need(pe, ot_copied[0], n, TILES, t)
                        need(pe, ot_copied[1], other, TILES, t)
                else:
                    need(pe, pt_copied[0], other, TILES, t + 1)
                    if t == 0:
                        need(pe, ln_b, n, LN_STEPS, 33)
                    else:
                        need(pe, ot_copied[1], n, TILES, t)
                if t >= 5:
                    need(pe, fin_ready, c, 2, 1)
                for j in range(4):
                    last = tr(T[:, P * j:P * j + P], p_sb[w][:, j, :], ident)
                last.then_inc(pt_ready[w], 1)

            def weighted_values(t, w, n, other):
                need(pe, pt_copied[w], n, TILES, t + 1)
                if w == 0:
                    if t == 0:
                        need(pe, av_sb, n, 8, 8)
                        need(pe, ln_b, other, LN_STEPS, 33)
                    else:
                        need(pe, o_norm[0], n, TILES, t)
                        need(pe, o_norm[1], other, TILES, t)
                    flat = v_a[:, :, :, :, :].rearrange("p t j w c -> p (t j w c)")
                    for j in range(PAIRS):
                        at = (t * PAIRS + j) * 2 * VA
                        last = mm(O[:, P * j:P * j + P], pt_sb[0][:, j, :], flat[:, at:at + P], start=True, stop=True)
                else:
                    need(pe, bv_sb, n, 2, 2)
                    need(pe, o_norm[0], other, TILES, t + 1)
                    if t == 0:
                        need(pe, ln_b, n, LN_STEPS, 33)
                    else:
                        need(pe, o_norm[1], n, TILES, t)
                    flat = v_b[:, :, :, :].rearrange("p t h c -> p t (h c)")
                    for h in range(HB):
                        at = 0 if h < HB - 1 else HB * VB - P
                        last = mm(O[:, P * h:P * h + P], pt_sb[1][:, h, :], flat[:, t, at:at + P], start=True, stop=True)
                last.then_inc(o_ready[w], 1)

            def transposed_out(t, w, n, other):
                need(pe, o_norm[w], n, TILES, t + 1)
                need(pe, pt_copied[0], n if w == 0 else other, TILES, t + 1)
                need(pe, pt_copied[1], other if w == 0 else n, TILES, t + 1)
                if w == 1:
                    need(pe, ot_copied[0], other, TILES, t + 1)
                tr(T[:, 0:P], on_s[w][:], ident).then_inc(ot_ready[w], 1)

            def spread_weights(t, j, c):
                e, half = 2 * (t % 4) + j, t // 4
                if t == 0 and j == 0:
                    need(pe, gate, c, GATE_STEPS, 21)
                    need(pe, ln_c, c, LN_STEPS, 33)
                else:
                    need(pe, hw_ready, c, UNITS, 4 * t + 2 * j)
                mm(W[:, :], sel[:, e * P:(e + 1) * P], cwt[:, HALF * half:HALF * half + HALF],
                   start=True, stop=True).then_inc(web_ready, 1)

            def hidden(t, m, b, c):
                half, e, ch = unit(t, m)
                if 4 * t + m < 2:
                    need(pe, bv_sb, b, 2, 2)
                    need(pe, qk_sb, b + 1, 4, 4)
                else:
                    need(pe, gelu_ready, c, UNITS, 4 * t + m - 1)
                mm(Z[m % 2][:, :], w1_s[:, e, ch * P:(ch + 1) * P], xt_c[:, HALF * half:HALF * half + HALF],
                   start=True, stop=True).then_inc(z_ready, 1)

            def expert_out(t, m, c):
                half, e, ch = unit(t, m)
                if t % 4 == 0 and m == 0:
                    expert_bias(c, half)
                need(pe, hw_ready, c, UNITS, 4 * t + m + 1)
                mm(Y[:, :], w2_s[:, e, ch, :], hid[:, 4 * (t % 2) + m, :], start=False,
                   stop=(t % 4 == 3 and m == 3)).then_inc(y_done, 1)

            def transposed_y(half, b, c, t):
                need(pe, y_copied, c, 2, half + 1)
                need(pe, ot_copied[0], b + 1, TILES, t)
                need(pe, ot_copied[1], b, TILES, t)
                for j in range(4):
                    last = tr(T[:, P * j:P * j + P], y_s[:, P * j:P * j + P], ident)
                last.then_inc(yt_ready, 1)

            def body(i, do_a, do_b, do_c):
                a, b, c = i, i - 1, i - 2
                prepare(a, b, c, do_a, do_b, do_c)
                for t in range(STEPS):
                    now, before = t < TILES, t > 0
                    if do_a and now:
                        scores(t, 0, a, b, c)
                    if do_b and now:
                        scores(t, 1, a, b, c)
                    if do_c and now:
                        spread_weights(t, 0, c)
                        hidden(t, 0, b, c)
                        hidden(t, 1, b, c)
                    if do_a and before:
                        transposed_probs(t - 1, 0, a, b, c)
                    if do_c and before:
                        expert_out(t - 1, 0, c)
                    if do_c and now:
                        hidden(t, 2, b, c)
                    if do_b and before:
                        transposed_probs(t - 1, 1, b, a, c)
                    if do_c and before:
                        expert_out(t - 1, 1, c)
                    if do_c and now:
                        hidden(t, 3, b, c)
                    if do_a and before:
                        weighted_values(t - 1, 0, a, b)
                    if do_c and now:
                        spread_weights(t, 1, c)
                    if do_c and before:
                        expert_out(t - 1, 2, c)
                    if do_b and before:
                        weighted_values(t - 1, 1, b, a)
                    if do_c and before:
                        expert_out(t - 1, 3, c)
                    if do_a and before:
                        transposed_out(t - 1, 0, a, b)
                    if do_b and before:
                        transposed_out(t - 1, 1, b, a)
                    if do_c and t in (5, 8):
                        transposed_y(t // 8, b, c, t)

            schedule(pe, body)

        @block.scalar
        def _(act):
            func = act.activation
            act.preload_act_table_set(EXP_LN_SET)
            act.wait_ge(setup, 4)
            func(rel_s, Y[0:HA, 0:REL * REL], ACT.Exp, scale=-1.0).then_inc(setup_act, 1)
            act.wait_ge(loaded, 16 * len(loads))
            act.wait_ge(setup, 13)
            func(cols[:, 5:6], cols[:, 4:5], ACT.Exp).then_inc(setup_act, 1)
            act.wait_ge(setup_act, 2)

            def group_norm(a):
                for h in range(2):
                    need(act, xt_a_ready, a, 2, h + 1)
                    if h == 1:
                        need(act, gn, a, GN_STEPS, 1)
                    need(act, qn_ready, a - 1, 4, 4)
                    func(xraw[:, HALF * h:HALF * h + HALF], Z[h][:, :], ACT.Copy).then_inc(gn, 1)
                need(act, gn, a, GN_STEPS, 11)
                func(gstat[:, 19:20], gstat[:, 18:19], ACT.Ln, bias=eps5[:, 0:1]).then_inc(gn, 1)
                need(act, gn, a, GN_STEPS, 12)
                func(gstat[:, 20:21], gstat[:, 19:20], ACT.Exp, scale=-0.5).then_inc(gn, 1)

            def layer_rstd(s, n, mv, rs):
                need(act, s, n, LN_STEPS, 18)
                func(rs[:, 0, :], mv[:, :, 1], ACT.Ln, bias=eps5[:, 0:1]).then_inc(s, 1)
                need(act, s, n, LN_STEPS, 19)
                func(rs[:, 1, :], rs[:, 0, :], ACT.Exp, scale=-0.5).then_inc(s, 1)

            def layer_copy(s, n, banks, dst):
                for h, src in enumerate(banks):
                    need(act, s, n, LN_STEPS, 31 + h)
                    func(dst[:, HALF * h:HALF * h + HALF], src[:, :], ACT.Copy).then_inc(s, 1)

            def body(i, do_a, do_b, do_c):
                a, b, c = i, i - 1, i - 2
                act.preload_act_table_set(EXP_LN_SET)
                if do_a:
                    group_norm(a)
                if do_c:
                    layer_rstd(ln_c, c, mv_c, rs_c)
                if do_b:
                    layer_rstd(ln_b, b, mv_b, rs_b)
                if do_c:
                    layer_copy(ln_c, c, (Y, W), xt_c)
                if do_b:
                    layer_copy(ln_b, b, (T, O), xt_b)
                if do_a:
                    for n, src in enumerate((*Z, SA, SB)):
                        need(act, qk_ready, a, 4, n + 1)
                        need(act, s_ready[0], a - 1, TILES, TILES)
                        func(qk_a[:, n, :], src[:, :], ACT.Identity, bias=cols[:, n // 2:n // 2 + 1]).then_inc(qk_sb, 1)
                if do_b:
                    for n, src in enumerate((*Z, SA, SB)):
                        need(act, bqk_ready, b, 4, n + 1)
                        dst = (q_b, k_b)[n // 2]
                        need(act, s_ready[1], b - 1, TILES, TILES)
                        func(dst[:, HALF * (n % 2):HALF * (n % 2) + HALF], src[:, :], ACT.Copy).then_inc(bqk_sb, 1)
                if do_c:
                    need(act, gate, c, GATE_STEPS, 4)
                    func(pr[:, :, :], lg[:, :, :], ACT.Exp).then_inc(gate, 1)
                if do_a:
                    for n, src in enumerate((Y, T, O, Y)):
                        need(act, ss_ready, a, 4, n + 1)
                        func(sq_a[:, n, :], src[:, :], ACT.Ln, bias=eps5[:, 1:2], scale=2.0 ** NORM_SHIFT).then_inc(ln_ready, 1)
                        need(act, ln_ready, a, 4, n + 1)
                        func(sq_a[:, n, :], sq_a[:, n, :], ACT.Exp, scale=-0.5,
                             bias=eps5[:, 2 + n // 2:3 + n // 2]).then_inc(rn_ready, 1)
                if do_b:
                    for h, src in enumerate(Z):
                        need(act, bv_ready, b, 2, h + 1)
                        need(act, o_ready[1], b - 1, TILES, TILES)
                        func(v_b[:, 4 * h:4 * h + 4, :, 0:DB], src[:, :].rearrange("p (t h c) -> p t h c", t=4, h=HB),
                             ACT.Copy).then_inc(bv_sb, 1)
                if do_c:
                    need(act, gate, c, GATE_STEPS, 20)
                    func(cwt[:, :], W[:, :].bitcast(BF16)[0:GATE_PARTS * E, :], ACT.Copy).then_inc(gate, 1)
                for t in range(STEPS):
                    now, before = t < TILES, t > 0

                    def gelu(m):
                        _, e, ch = unit(t, m)
                        need(act, z_ready, c, UNITS, 4 * t + m + 1)
                        if t >= 2:
                            need(act, y_done, c, UNITS, 4 * (t - 2) + m + 1)
                        else:
                            need(act, y_done, c - 1, UNITS, UNITS)
                        func(hid[:, 4 * (t % 2) + m, :], Z[m % 2][:, :], ACT.Gelu,
                             bias=b1_s[:, CH * e + ch:CH * e + ch + 1]).then_inc(gelu_ready, 1)

                    def probs_copy(w, n):
                        need(act, pt_ready[w], n, TILES, t)
                        if t >= 2:
                            need(act, o_ready[w], n, TILES, t - 1)
                        else:
                            need(act, o_ready[w], n - 1, TILES, TILES)
                        func(pt_sb[w][:, :, :].rearrange("p j n -> p (j n)"), T[:, :], ACT.Copy).then_inc(pt_copied[w], 1)

                    def probs(w, n):
                        need(act, s_sub[w], n, TILES, t + 1)
                        need(act, pt_ready[w], n, TILES, t)
                        func(p_sb[w][:, :, :].rearrange("p j n -> p (j n)"), s_sb[w][:, :, :].rearrange("p h n -> p (h n)"),
                             ACT.Exp, scale=1.0 if w == 0 else float(DB) ** -0.5).then_inc(p_ready[w], 1)

                    def out_copy(w, n):
                        need(act, ot_ready[w], n, TILES, t)
                        if w == 0:
                            need(act, outa_ready, n - 1, 2, 2)
                            y0, x0 = WS * ((t - 1) // 2), 2 * WS * ((t - 1) % 2)
                            dst = ot_a[:, :].rearrange("p (y x) -> p y x", x=SIDE)[:, y0:y0 + WS, x0:x0 + 2 * WS]
                            func(dst.rearrange("p y (w x) -> p w y x", w=2),
                                 T[:, 0:P].rearrange("p (w y x) -> p w y x", w=2, y=WS), ACT.Copy).then_inc(ot_copied[0], 1)
                        else:
                            need(act, outb_ready, n - 1, 2, 2)
                            func(ot_b[:, P * (t - 1):P * t], T[:, 0:P], ACT.Copy).then_inc(ot_copied[1], 1)

                    if do_c and now:
                        gelu(0)
                        gelu(1)
                    if do_a and before:
                        probs_copy(0, a)
                    if do_c and now:
                        gelu(2)
                    if do_b and before:
                        probs_copy(1, b)
                    if do_c and now:
                        gelu(3)
                    if now:
                        act.preload_act_table_set(EXP_LN_SET)
                        if do_a:
                            probs(0, a)
                        if do_b:
                            probs(1, b)
                    if do_a and before:
                        out_copy(0, a)
                    if do_b and before:
                        out_copy(1, b)
                    if do_c and t in (4, 8):
                        need(act, y_done, c, UNITS, 4 * t)
                        need(act, yt_ready, c, 2, t // 8)
                        func(y_s[:, :], Y[:, :], ACT.Copy).then_inc(y_copied, 1)

            schedule(act, body)

        @block.gpsimd
        def _(pool):
            pool.memset(v_a[:, :, :, :, :], 0.0).then_inc(setup_act, 1)
            pool.wait_ge(ready, 3)

            def body(i, do_a, do_b, do_c):
                a, b, c = i, i - 1, i - 2
                if do_b:
                    need(pool, ln_b, b, LN_STEPS, 2)
                    need(pool, ln_c, c, LN_STEPS, 2)
                    pool.tensor_tensor(t1b[:, :, :], t1[:, :, :], row_b[:, None, :].to_broadcast([P, TILES, D]),
                                       ALU.add).then_inc(t1b_ready, 1)
                if do_a:
                    need(pool, x_copied, a, 16, 16)
                    pool.tensor_tensor(x_res[:, :, :], x_res[:, :, :], row_a[:, None, :].to_broadcast([P, TILES, D]),
                                       ALU.add).then_inc(res_ready, 1)
                    for n in range(4):
                        need(pool, qk_sb, a, 4, n + 1)
                        need(pool, qn_ready, a - 1, 4, 4)
                        pool.tensor_tensor(sq_a[:, n, :], qk_a[:, n, :], qk_a[:, n, :], ALU.mult).then_inc(sq_ready, 1)
                for t in range(TILES):
                    for w, n, on, s, m, width in ((0, a, do_a, s_sb[0], mx_s[0], WTOK), (1, b, do_b, s_sb[1], mx_s[1], P)):
                        if on:
                            need(pool, s_max[w], n, TILES, t + 1)
                            h = (HA, HB)[w]
                            pool.tensor_tensor(s[:, :, :], s[:, :, :], m[:, :, None].to_broadcast([P, h, width]),
                                               ALU.subtract).then_inc(s_sub[w], 1)

            schedule(pool, body)

        @block.vector
        def _(dve):
            tt, ts, stt = dve.tensor_tensor, dve.tensor_scalar, dve.scalar_tensor_tensor
            dve.wait_ge(loaded, 16 * len(loads))
            dve.wait_ge(setup, 1)
            for c in range(CH):
                ts(hid_s[:, c, :], Z[c][:, 0:REL * REL], cb1_s[:, c:c + 1], 0.0, ALU.add, ALU.max).then_inc(setup, 1)
            dve.wait_ge(setup, 5)
            dve.wait_ge(setup_act, 2)
            tt(row_a[:], W[:, 0:P], bo_s[:], ALU.add).then_inc(setup, 1)
            ts(rel_s, rel_s, 1.0, None, ALU.add).then_inc(setup, 1)
            dve.wait_ge(setup, 7)
            dve.reciprocal(rel_s, rel_s).then_inc(setup, 1)
            dve.wait_ge(setup, 8)
            ts(rel_s, rel_s, 16.0, None, ALU.mult).then_inc(setup, 1)
            dve.wait_ge(setup, 10)
            for kind in range(4):
                a = CONST["mask_a"][0] + kind * WTOK
                last = tt(bias_a[:, kind, :, :], SA[:, :].rearrange("p (h n) -> p h n", h=HA),
                          k[:, None, a:a + WTOK].to_broadcast([P, HA, WTOK]), ALU.add)
            last.then_inc(setup, 1)
            dve.tensor_copy(ident16[:], ident).then_inc(setup, 1)
            ts(cols[:, 4:5], cols[:, 3:4], float(np.log(100.0)), None, ALU.min).then_inc(setup, 1)
            dve.wait_ge(setup, 13)
            dve.memset(eps5[:, 0:1], 1e-5)
            dve.memset(eps5[:, 1:2], 2.0 ** -64)
            ts(eps5[:, 2:3], cols[:, 4:5], NORM_SHIFT * LN2 / 2, None, ALU.add)
            dve.memset(eps5[:, 3:4], NORM_SHIFT * LN2 / 2)
            dve.wait_ge(setup_act, 3)
            ts(cols[:, 6:7], cols[:, 5:6], NORM_CAP, None, ALU.mult)
            dve.memset(v_b[:, :, :, DB:VB], 1.0)
            dve.memset(v_a[0:WTOK, :, :, :, 2 * DA:2 * DA + 1], 1.0)
            dve.memset(v_a[WTOK:P, :, :, :, 2 * DA + 1:VA], 1.0)
            dve.tensor_copy(b2_p[:, 0, :], b2_s[:]).then_inc(setup, 1)
            dve.wait_ge(setup, 14)
            tt(b2_r[:, 0, :], b2_s[:], b2_p[:, 0, :], ALU.subtract).then_inc(setup, 1)
            dve.wait_ge(setup, 15)
            dve.tensor_copy(b2_p[:, 1, :], b2_r[:, 0, :]).then_inc(setup, 1)
            dve.wait_ge(setup, 16)
            tt(b2_r[:, 1, :], b2_r[:, 0, :], b2_p[:, 1, :], ALU.subtract).then_inc(setup, 1)
            dve.wait_ge(setup, 17)
            dve.tensor_copy(b2_p[:, 2, :], b2_r[:, 1, :]).then_inc(ready, 3)

            def residual(s, n, banks, old, new):
                for h, src in enumerate(banks):
                    tt(new[:, 4 * h:4 * h + 4, :].rearrange("p t d -> p (t d)"), src[:, :],
                       old[:, 4 * h:4 * h + 4, :].rearrange("p t d -> p (t d)"), ALU.add).then_inc(s, 1)

            def layer_norm_stats(s, n, tok, st, mv):
                need(dve, s, n, LN_STEPS, 2)
                for t in range(TILES):
                    dve.bn_stats(st[:, t, :], tok[:, t, :]).then_inc(s, 1)
                need(dve, s, n, LN_STEPS, 10)
                dve.memset(pad[:, 0:1], 0.0)
                for t in range(TILES):
                    dve.bn_aggr(mv[:, t, :], st[:, t, :]).then_inc(s, 1)

            def layer_norm_apply(s, n, tok, mv, rs, xn):
                need(dve, s, n, LN_STEPS, 20)
                stt(rs[:, 2, :], mv[:, :, 0], -1.0, rs[:, 1, :], ALU.mult, ALU.mult).then_inc(s, 1)
                need(dve, s, n, LN_STEPS, 21)
                for t in range(TILES):
                    ts(xn[:, t, :], tok[:, t, :], rs[:, 1, t:t + 1], rs[:, 2, t:t + 1], ALU.mult, ALU.add).then_inc(s, 1)

            def group_norm_stats(a):
                for h in range(2):
                    need(dve, gn, a, GN_STEPS, 2)
                    dve.bn_stats(gstat[:, 6 * h:6 * h + 6], xraw[:, HALF * h:HALF * h + HALF]).then_inc(gn, 1)
                need(dve, gn, a, GN_STEPS, 4)
                dve.memset(pad[:, 1:2], 0.0)
                dve.bn_aggr(gstat[:, 12:14], gstat[:, 0:12]).then_inc(gn, 1)
                need(dve, gn, a, GN_STEPS, 6)
                dve.tensor_copy(gstat[:, 14:16], O[:, 0:2]).then_inc(gn, 1)
                need(dve, gn, a, GN_STEPS, 7)
                tt(gstat[:, 16:17], gstat[:, 12:13], gstat[:, 14:15], ALU.subtract).then_inc(gn, 1)
                need(dve, gn, a, GN_STEPS, 8)
                tt(gstat[:, 17:18], gstat[:, 16:17], gstat[:, 16:17], ALU.mult).then_inc(gn, 1)
                need(dve, gn, a, GN_STEPS, 10)
                tt(gstat[:, 18:19], O[:, 2:3], gstat[:, 15:16], ALU.add).then_inc(gn, 1)

            def group_norm_apply(a):
                need(dve, gn, a, GN_STEPS, 13)
                stt(gstat[:, 21:22], gstat[:, 14:15], -1.0, gstat[:, 20:21], ALU.mult, ALU.mult).then_inc(gn, 1)
                need(dve, gn, a, GN_STEPS, 14)
                for wi in range(SIDE // WS):
                    span = slice(WS * SIDE * wi, WS * SIDE * (wi + 1))
                    ts(xn_a[:, span].rearrange("p (w y x) -> p y w x", y=WS, x=WS),
                       xraw[:, span].rearrange("p (y w x) -> p y w x", y=WS, x=WS),
                       gstat[:, 20:21], gstat[:, 21:22], ALU.mult, ALU.add).then_inc(gn, 1)

            def gate_weights(c):
                def step(n):
                    need(dve, gate, c, GATE_STEPS, n)

                pb = pr[:, :, :]
                shape = [P, TILES, E, E]
                ge, gt = cmp_c
                step(1)
                tt(lg[:, :, :], W[:, 0:TILES * E].rearrange("p (t e) -> p t e", e=E),
                   gb_s[:, None, :].to_broadcast([P, TILES, E]), ALU.add).then_inc(gate, 1)
                step(2)
                dve.tensor_reduce(col_c[:, 0, :], lg[:, :, :], AX_X, ALU.max).then_inc(gate, 1)
                step(3)
                tt(lg[:, :, :], lg[:, :, :], col_c[:, 0, :, None].to_broadcast([P, TILES, E]), ALU.subtract).then_inc(gate, 1)
                step(5)
                dve.tensor_reduce(col_c[:, 1, :], pb, AX_X, ALU.add).then_inc(gate, 1)
                step(6)
                dve.reciprocal(col_c[:, 2, :], col_c[:, 1, :]).then_inc(gate, 1)
                step(7)
                tt(pb, pb, col_c[:, 2, :, None].to_broadcast([P, TILES, E]), ALU.mult).then_inc(gate, 1)
                step(8)
                other, own = pr[:, :, None, :].to_broadcast(shape), pr[:, :, :, None].to_broadcast(shape)
                tt(ge, other, own, ALU.is_equal).then_inc(gate, 1)
                tt(gt, other, own, ALU.is_gt).then_inc(gate, 1)
                step(10)
                flat0 = ge.rearrange("p t e f -> p t (e f)")
                flat1 = gt.rearrange("p t e f -> p t (e f)")
                tt(flat0, flat0, const("tri")[:, None, :].to_broadcast([P, TILES, E * E]), ALU.mult).then_inc(gate, 1)
                step(11)
                tt(flat1, flat1, flat0, ALU.add).then_inc(gate, 1)
                step(12)
                dve.tensor_reduce(rank_c[:, :, :], gt, AX_X, ALU.add).then_inc(gate, 1)
                step(13)
                stt(cw[:, 0, :, :], rank_c[:, :, :], 2.0, pb, ALU.is_lt, ALU.mult).then_inc(gate, 1)
                step(14)
                dve.tensor_copy(cw3[:, :, 0, :], cw[:, 0, :, :]).then_inc(gate, 1)
                step(15)
                tt(cw[:, 1, :, :], cw[:, 0, :, :], cw3[:, :, 0, :], ALU.subtract).then_inc(gate, 1)
                step(16)
                dve.tensor_copy(cw3[:, :, 1, :], cw[:, 1, :, :]).then_inc(gate, 1)
                step(17)
                tt(cw[:, 2, :, :], cw[:, 1, :, :], cw3[:, :, 1, :], ALU.subtract).then_inc(gate, 1)
                step(18)
                dve.tensor_copy(cw3[:, :, 2, :], cw[:, 2, :, :]).then_inc(gate, 1)

            def body(i, do_a, do_b, do_c):
                a, b, c = i, i - 1, i - 2
                if do_a:
                    group_norm_stats(a)
                if do_c:
                    need(dve, outb_ready, c, 2, 2)
                    need(dve, t1b_ready, c, 1, 1)
                    need(dve, fin_ready, c - 1, 2, 2)
                    residual(ln_c, c, (Y, W), t1b, t2)
                if do_b:
                    need(dve, outa_ready, b, 2, 2)
                    need(dve, res_ready, b, 1, 1)
                    need(dve, t1b_ready, b - 1, 1, 1)
                    need(dve, ln_b, b - 1, LN_STEPS, LN_STEPS)
                    residual(ln_b, b, (SA, SB), x_res, t1)
                if do_c:
                    layer_norm_stats(ln_c, c, t2, st_c, mv_c)
                if do_b:
                    layer_norm_stats(ln_b, b, t1, st_b, mv_b)
                if do_a:
                    group_norm_apply(a)
                if do_c:
                    need(dve, stored, c - 1, 16 * IO_DMAS, 16 * IO_DMAS)
                    layer_norm_apply(ln_c, c, t2, mv_c, rs_c, xn_c)
                if do_b:
                    layer_norm_apply(ln_b, b, t1, mv_b, rs_b, xn_b)
                if do_c:
                    gate_weights(c)
                if do_b:
                    for h in range(HB):
                        need(dve, bqk_sb, b, 4, 4)
                        m = CONST["head_mask_b"][0] + h
                        ts(km_b[:, h, :], k_b, k[:, m:m + 1], None, ALU.mult).then_inc(bkm_ready, 1)
                if do_a:
                    for n in range(4):
                        need(dve, rn_ready, a, 4, n + 1)
                        cap = cols[:, 6:7] if n < 2 else NORM_CAP
                        stt(qk_a[:, n, :], sq_a[:, n, :], cap, qk_a[:, n, :], ALU.min, ALU.mult).then_inc(qn_ready, 1)
                    for h in range(HA):
                        need(dve, qn_ready, a, 4, 4)
                        m = CONST["head_mask_a"][0] + h
                        ts(km_a[:, h, :], qk_a[:, 2:4, :].rearrange("p a n -> p (a n)"), k[:, m:m + 1], None,
                           ALU.mult).then_inc(km_ready, 1)
                    for g, src in enumerate((SA, SB, T, O)):
                        need(dve, av_ready, a, 4, g + 1)
                        need(dve, o_ready[0], a - 1, TILES, TILES)
                        for par in range(2):
                            ps = slice(WTOK * par, WTOK * par + WTOK)
                            v = src[ps, :].rearrange("p (t w j e c) -> p t j w e c", t=2, w=2, j=PAIRS, e=2)
                            for pair in range(2):
                                last = dve.tensor_copy(v_a[ps, 2 * g + pair, :, :, DA * par:DA * par + DA],
                                                       v[:, pair, :, :, par, :])
                            last.then_inc(av_sb, 1)

                for t in range(STEPS):
                    now, before = t < TILES, t > 0

                    def biased(w, n):
                        need(dve, s_ready[w], n, TILES, t + 1)
                        if t > 0:
                            need(dve, p_ready[w], n, TILES, t)
                        else:
                            need(dve, p_ready[w], n - 1, TILES, TILES)
                        if w == 0:
                            kind = 2 * (t // 6) + t % 2
                            tt(s_sb[0][:, :, :].rearrange("p h n -> p (h n)"), SA[:, :],
                               bias_a[:, kind, :, :].rearrange("p h n -> p (h n)"), ALU.add).then_inc(s_added[0], 1)
                        else:
                            tt(s_sb[1][:, :, :], SB[:, :].rearrange("p (h n) -> p h n", h=HB),
                               const("mask_b")[:, None, :].to_broadcast([P, HB, P]), ALU.add).then_inc(s_added[1], 1)
                        need(dve, s_added[w], n, TILES, t + 1)
                        dve.tensor_reduce(mx_s[w][:], s_sb[w][:, :, :], AX_X, ALU.max).then_inc(s_max[w], 1)

                    def weigh(m):
                        slot = hid[:, 4 * (t % 2) + m, :]
                        need(dve, gelu_ready, c, UNITS, 4 * t + m + 1)
                        need(dve, web_ready, c, 2 * TILES, 2 * t + m // 2 + 1)
                        tt(slot, slot, W[:, :], ALU.mult).then_inc(hw_ready, 1)

                    def normalised(w, n):
                        need(dve, o_ready[w], n, TILES, t)
                        if w == 0:
                            o = O[:, :].rearrange("p (j n) -> p j n", j=PAIRS)
                            for win in range(2):
                                ps = slice(WTOK * win, WTOK * win + WTOK)
                                last = dve.reciprocal(rc_s[0][ps, :].rearrange("p (j e) -> p j e", e=2),
                                                      o[ps, :, VA * win + 2 * DA:VA * win + VA])
                            last.then_inc(o_rc[0], 1)
                            need(dve, o_rc[0], n, TILES, t)
                            if t >= 2:
                                need(dve, ot_ready[0], n, TILES, t - 1)
                            for win in range(2):
                                ps = slice(WTOK * win, WTOK * win + WTOK)
                                last = tt(on_s[0][ps, :].rearrange("p (j e c) -> p j e c", j=PAIRS, e=2),
                                          o[ps, :, VA * win:VA * win + 2 * DA].rearrange("p j (e c) -> p j e c", e=2),
                                          rc_s[0][ps, :].rearrange("p (j e) -> p j e", e=2)[:, :, :, None].to_broadcast(
                                              [WTOK, PAIRS, 2, DA]), ALU.mult)
                            last.then_inc(o_norm[0], 1)
                        else:
                            o = O[:, :]
                            three = o[:, 0:(HB - 1) * (P + VB)].rearrange("p (h n) -> p h n", h=HB - 1)
                            end = (HB - 1) * (P + VB) - (HB * VB - P)
                            dve.reciprocal(rc_s[1][:, 0:HB - 1], three[:, :, DB])
                            dve.reciprocal(rc_s[1][:, HB - 1:HB], o[:, end + DB:end + VB]).then_inc(o_rc[1], 1)
                            need(dve, o_rc[1], n, TILES, t)
                            if t >= 2:
                                need(dve, ot_ready[1], n, TILES, t - 1)
                            tt(on_s[1][:, 0:(HB - 1) * DB].rearrange("p (h c) -> p h c", c=DB), three[:, :, 0:DB],
                               rc_s[1][:, 0:HB - 1, None].to_broadcast([P, HB - 1, DB]), ALU.mult)
                            ts(on_s[1][:, (HB - 1) * DB:], o[:, end:end + DB], rc_s[1][:, HB - 1:HB], None,
                               ALU.mult).then_inc(o_norm[1], 1)

                    if do_a and now:
                        biased(0, a)
                    if do_b and now:
                        biased(1, b)
                    if do_c and now:
                        weigh(0)
                        weigh(1)
                    if do_a and before:
                        normalised(0, a)
                    if do_c and now:
                        weigh(2)
                        weigh(3)
                    if do_b and before:
                        normalised(1, b)
                    if do_c and t in (5, 8):
                        half = t // 8
                        need(dve, yt_ready, c, 2, half + 1)
                        tt(xn_c[:, 4 * half:4 * half + 4, :].rearrange("p t d -> p (t d)"), T[:, :],
                           t2[:, 4 * half:4 * half + 4, :].rearrange("p t d -> p (t d)"), ALU.add).then_inc(fin_ready, 1)

            schedule(dve, body)


_INPUTS = ["x", "wq", "bq", "wk", "bk", "wv", "bv", "wo", "bo", "logit_scale", "cpb_w1", "cpb_b1", "cpb_w2",
           "w_qkv", "w_proj", "b_proj", "gate_w", "gate_b", "w1", "b1", "w2", "b2", "consts", "rel_table", "unfold", "selectors"]


def kernel(x, L0_conv_Wq, L0_conv_bq, L0_conv_Wk, L0_conv_bk, L0_conv_Wv, L0_conv_bv, L0_conv_Wo, L0_conv_bo,
           L0_conv_logit_scale, L0_conv_cpb_w1, L0_conv_cpb_b1, L0_conv_cpb_w2, L1_attn_Wqkv, L1_attn_Wproj,
           L1_attn_bproj, L1_ffn_gate_w, L1_ffn_gate_b, L1_ffn_W1, L1_ffn_b1, L1_ffn_W2, L1_ffn_b2):
    import ml_dtypes
    import concourse.bacc as bacc
    from concourse.bass_utils import run_bass_kernel_spmd

    col, row = (lambda v: np.asarray(v).reshape(-1, 1)), (lambda v: np.asarray(v).reshape(1, -1))
    arrays = dict(zip(_INPUTS, [
        x, np.asarray(L0_conv_Wq).T, col(L0_conv_bq), np.asarray(L0_conv_Wk).T, col(L0_conv_bk),
        np.asarray(L0_conv_Wv).T, col(L0_conv_bv), np.asarray(L0_conv_Wo).T, row(L0_conv_bo),
        col(np.repeat(np.asarray(L0_conv_logit_scale).reshape(-1), DA)),
        np.asarray(L0_conv_cpb_w1).T, np.asarray(L0_conv_cpb_b1).reshape(CH, P).T, np.asarray(L0_conv_cpb_w2).T,
        L1_attn_Wqkv, L1_attn_Wproj, row(L1_attn_bproj), L1_ffn_gate_w, row(L1_ffn_gate_b),
        L1_ffn_W1, np.asarray(L1_ffn_b1).reshape(E * CH, P).T, L1_ffn_W2, L1_ffn_b2,
        *shape_constants(), expert_selectors().astype(ml_dtypes.bfloat16)]))
    nc = bacc.Bacc("TRN2", target_bir_lowering=False, num_devices=1)
    feeds, args = {}, []
    for name in _INPUTS:
        v = np.ascontiguousarray(arrays[name])
        feeds[f"in_{name}_dram"] = v
        args.append(nc.dram_tensor(f"in_{name}_dram", v.shape, mybir.dt.from_np(v.dtype), kind="ExternalInput").ap())
    args.append(nc.dram_tensor("out_0_dram", (IMAGES, SIDE, SIDE, D), F32, kind="ExternalOutput").ap())
    hybrid_kernel(nc, *args)
    return run_bass_kernel_spmd(nc, [feeds], core_ids=[0]).results[0]["out_0_dram"]
```

```python
from contextlib import ExitStack

import concourse.bass as bass
import numpy as np
from concourse import mybir

P = 128
IMAGES, SIDE, D = 32, 32, 128
TOKENS = SIDE * SIDE
TILES = TOKENS // P
ROWS = P // SIDE
HALF = TOKENS // 2
WS, SHIFT = 8, 4
WTOK = WS * WS
WINDOWS = TOKENS // WTOK
HA, DA = 8, 16
PAIRS = HA // 2
HB, DB = 4, 32
RADIUS = 32
E, HID = 8, 256
CH = HID // P
GROUP = 4
GATE_N, GATE_STRIDE = 96, 56
REL = 2 * WS - 1
GATE_PARTS = 3

F32 = mybir.dt.float32
F32R = mybir.dt.float32r
BF16 = mybir.dt.bfloat16
ALU = mybir.AluOpType
ACT = mybir.ActivationFunctionType
AX_X = mybir.AxisListType.X
EXP_LN_SET = "natural_log_exp_and_others"
GELU_SET = "gelu_and_others"

NORM_SHIFT = 20
LN2 = float(np.log(2.0))
NORM_CAP = 1e12
MASKED = -1e30

CONST = {}


def _columns():
    at = 0
    for name, width in (("identity", P), ("group_mean", P), ("head_ones", P), ("head_mask_a", HA), ("head_mask_b", HB),
                        ("tri", E * E), ("mask_a", 4 * WTOK), ("mask_b", P), ("ones_a", DB), ("ones_b", DB)):
        CONST[name] = (at, at + width)
        at += width
    return at


CONST_WIDTH = _columns()


def shape_constants():
    c = np.zeros((P, CONST_WIDTH), np.float32)

    def put(name, value):
        a, _ = CONST[name]
        value = np.asarray(value, np.float32)
        c[:value.shape[0], a:a + value.shape[1]] = value

    ch = np.arange(P)
    put("identity", np.eye(P))
    put("group_mean", (ch[:, None] // GROUP == ch[None] // GROUP) / GROUP)
    put("head_ones", ch[:, None] // DA == ch[None] // DA)
    put("head_mask_a", ch[:, None] // DA == np.arange(HA)[None])
    put("head_mask_b", ch[:, None] // DB == np.arange(HB)[None])
    put("ones_a", ch[:, None] // WTOK == np.arange(DB)[None] // DA)
    put("ones_b", np.ones((P, DB)))
    e = np.arange(E)
    put("tri", np.broadcast_to((e[None] < e[:, None]).reshape(1, -1), (P, E * E)))
    img = np.zeros((SIDE, SIDE), np.int32)
    cuts = (slice(0, -WS), slice(-WS, -SHIFT), slice(-SHIFT, None))
    for a, hs in enumerate(cuts):
        for b, ws in enumerate(cuts):
            img[hs, ws] = 3 * a + b
    win = img.reshape(SIDE // WS, WS, SIDE // WS, WS).transpose(0, 2, 1, 3).reshape(SIDE // WS, SIDE // WS, WTOK)
    for bottom in range(2):
        for right in range(2):
            pair = win[3 * bottom, 2 * right:2 * right + 2]
            m = np.where(pair[:, :, None] != pair[:, None, :], -100.0, 0.0).reshape(P, WTOK)
            a = CONST["mask_a"][0] + (2 * bottom + right) * WTOK
            c[:, a:a + WTOK] = m
    n = SIDE * (ch // SIDE) + (ch % SIDE + SHIFT) % SIDE
    d = n[:, None] - n[None]
    put("mask_b", np.where((d >= 0) & (d <= RADIUS), 0.0, MASKED))
    r = np.arange(-(WS - 1), WS, dtype=np.float32)
    tbl = np.stack(np.meshgrid(r, r, indexing="ij"), axis=-1) / (WS - 1) * 8.0
    tbl = (np.sign(tbl) * np.log2(np.abs(tbl) + 1.0) / np.log2(8.0)).reshape(-1, 2)
    table = tbl[::-1].T.astype(np.float32)
    q = ch % WTOK
    unfold = np.stack([(np.arange(WS)[:, None] == WS - 1 - q[None] % WS) & (WS - 1 - q[None] // WS == py)
                       for py in range(WS)], axis=1).astype(np.float32).reshape(WS, WS * P)
    return c, table, unfold


def expert_selectors():
    s = np.zeros((GATE_PARTS * E, E, P), np.float32)
    for e in range(E):
        s[e::E, e] = 1.0
    return s.reshape(GATE_PARTS * E, E * P)


def count(image, per, k):
    if isinstance(image, int):
        image, k = (image, k) if 0 <= image < IMAGES else ((0, 0) if image < 0 else (IMAGES, 0))
        v = image * per + k
        return v if v > 0 else None
    return image * per + k


def hybrid_kernel(nc, x, wq, bq, wk, bk, wv, bv, wo, bo, logit_scale, cpb_w1, cpb_b1, cpb_w2,
                  w_qkv, w_proj, b_proj, gate_w, gate_b, w1, b1, w2, b2, consts, rel_table, unfold, selectors, out):
    scratch = nc.dram_tensor("rel_bias_scratch", [HA, REL * REL], F32)
    x_rolled = x.rearrange("a (t r) c d -> a r c t d", r=ROWS)
    out_rolled = out.rearrange("a (t r) c d -> a r c t d", r=ROWS)
    col_pieces = (((0, SIDE - SHIFT), (SHIFT, SIDE)), ((SIDE - SHIFT, SIDE), (0, SHIFT)))
    IO_DMAS = ROWS * len(col_pieces)

    with ExitStack() as ctx:
        def sb(name, shape, dt=F32):
            return ctx.enter_context(nc.sbuf_tensor(name, shape, dt))

        def bank(name):
            return ctx.enter_context(nc.psum_tensor(name, [P, HALF], F32))

        def sem(name):
            return ctx.enter_context(nc.semaphore(name))

        k = sb("k_consts", [P, CONST_WIDTH])

        def const(name, rows=P):
            a, b = CONST[name]
            return k[0:rows, a:b]

        ident = const("identity")
        sel = sb("expert_sel", [GATE_PARTS * E, E * P], BF16)
        ident16 = sb("ident16", [P, P], BF16)
        wq_s, wk_s, wv_s, wo_s = (sb(n, [P, P]) for n in ("wq_s", "wk_s", "wv_s", "wo_s"))
        wqkv_s = sb("wqkv_s", [P, 3 * P])
        wp_s = sb("wp_s", [P, P])
        gw_s = sb("gw_s", [P, GATE_N])
        w1_h = sb("w1_h", [P, E * HID], F32R)
        w1_l = sb("w1_l", [P, E * HID], F32R)
        w2_h = sb("w2_h", [P, E * CH * P], F32R)
        w2_l = sb("w2_l", [P, E * CH * P], F32R)
        b1_s = sb("b1_s", [P, E * CH])
        b2_s = sb("b2_s", [GATE_PARTS * E, P])
        b2_p = sb("b2_p", [GATE_PARTS * E, GATE_PARTS, P], BF16)
        b2_r = sb("b2_r", [GATE_PARTS * E, 2, P])
        cols = sb("cols", [P, 8])
        row_a = sb("row_a", [P, P])
        row_b = sb("row_b", [P, P])
        bo_s = sb("bo_s", [P, P])
        gb_s = sb("gb_s", [P, E])
        cw1_s = sb("cw1_s", [2, HID])
        cb1_s = sb("cb1_s", [P, CH])
        cw2_s = sb("cw2_s", [P, CH, HA])
        bias_a = sb("bias_a", [P, 4, HA, WTOK])
        eps5 = sb("eps5", [P, 4])

        pad = sb("pad", [P, 2])

        xin = sb("xin", [P, TILES, D])
        x_res = sb("x_res", [P, TILES, D])
        xn_a = sb("xn_a", [P, TOKENS])
        gstat = sb("gstat", [P, 24])
        qk_a = sb("qk_a", [P, 4, HALF])
        sq_a = sb("sq_a", [P, 4, HALF])
        xraw = sq_a[:, 0:2, :].rearrange("p a n -> p (a n)")
        w1_s = sq_a[:, :, :].rearrange("p a n -> p (a n)")
        w2_s = qk_a[:, :, :].rearrange("p a n -> p (a n)")
        km_a = sb("km_a", [P, 2, HA, P])
        v_a = sb("v_a", [P, WINDOWS, P])
        ot_a = sb("ot_a", [P, TOKENS])
        t1 = sb("t1", [P, TILES, D])
        st_b = sb("st_b", [P, TILES, 6])
        mv_b = sb("mv_b", [P, TILES, 2])
        rs_b = sb("rs_b", [P, 3, TILES])
        xt_b = sb("xt_b", [P, TOKENS])
        q_b = sb("q_b", [P, TOKENS])
        k_b = sb("k_b", [P, TOKENS])
        km_b = sb("km_b", [P, 2, HB, P])
        v_b = sb("v_b", [P, TOKENS])
        ot_b = sb("ot_b", [P, TOKENS])
        t2 = sb("t2", [P, TILES, D])
        st_c = sb("st_c", [P, TILES, 6])
        mv_c = sb("mv_c", [P, TILES, 2])
        rs_c = sb("rs_c", [P, 3, TILES])
        xn_c = sb("xn_c", [P, TILES, D])
        xh_c = sb("xh_c", [P, TOKENS], F32R)
        xl_c = sb("xl_c", [P, TOKENS], F32R)
        lg = sb("lg", [P, TILES, E])
        pr = sb("pr", [P, TILES, E])
        col_c = sb("col_c", [P, 3, TILES])
        rank_c = sb("rank_c", [P, TILES, E])
        cw = sb("cw", [P, 3, TILES, E])
        cw3 = sb("cw3", [P, TILES, GATE_PARTS, E], BF16)
        cwt = sb("cwt", [GATE_PARTS * E, TOKENS], BF16)
        hid = sb("hid", [P, 8, HALF])
        hid_h = sb("hid_h", [P, 8, HALF], F32R)
        hid_l = sb("hid_l", [P, 4, HALF], F32R)
        xt_c = hid[:, 0:2, :].rearrange("p a n -> p (a n)")
        xn_b = hid[:, 2:4, :].rearrange("p a (t d) -> p (a t) d", d=D)
        cmp_c = [hid[:, 4 + n, :].rearrange("p (t e f) -> p t e f", t=TILES, e=E) for n in range(2)]
        y_s = sb("y_s", [P, HALF])
        hid_s = hid[:, 0:2, 0:REL * REL]
        rel_s = hid[0:HA, 2, 0:REL * REL]
        tab_s = hid[0:2, 3, 0:REL * REL]
        unf_s = hid[0:WS, 4:6, :].rearrange("p a n -> p (a n)")[:, 0:HA * REL * WS].rearrange("p (y w) -> p y w", w=WS)
        fold_s = hid[0:WS, 6:8, :].rearrange("p a n -> p (a n)")
        s_sb = [sb("s_sb_a", [P, HA, WTOK]), sb("s_sb_b", [P, HB, P])]
        mx_s = [sb("mx_a", [P, HA]), sb("mx_b", [P, HB])]
        p_sb = [sb("p_sb_a", [P, 4, P]), sb("p_sb_b", [P, 4, P])]
        pt_sb = [sb("pt_sb_a", [P, 4, P]), sb("pt_sb_b", [P, 4, P])]
        sum_inv = sb("sum_inv", [P, 2 * P])

        Z = [bank("bank_z0"), bank("bank_z1")]
        Y, W, SA, SB, T, O = (bank(n) for n in ("bank_y", "bank_w", "bank_sa", "bank_sb", "bank_t", "bank_o"))

        loaded = sem("loaded")
        setup = sem("setup")
        setup_act = sem("setup_act")
        w_split = sem("w_split")
        xs_ready = sem("xs_ready")
        bias_io = sem("bias_io")
        ready = sem("ready")
        x_in, x_copied, res_ready = sem("x_in"), sem("x_copied"), sem("res_ready")
        gn = sem("gn")
        xt_a_ready = sem("xt_a_ready")
        qk_ready, qk_sb, sq_ready, ss_ready, ln_ready, rn_ready, qn_ready, km_ready, av_ready, av_sb = (
            sem(n) for n in ("qk_ready", "qk_sb", "sq_ready", "ss_ready", "ln_ready", "rn_ready", "qn_ready",
                             "km_ready", "av_ready", "av_sb"))
        outa_ready, outb_ready = sem("outa_ready"), sem("outb_ready")
        ln_b, ln_c = sem("ln_b"), sem("ln_c")
        t1b_ready = sem("t1b_ready")
        bqk_ready, bqk_sb, bkm_ready, bv_ready, bv_sb = (
            sem(n) for n in ("bqk_ready", "bqk_sb", "bkm_ready", "bv_ready", "bv_sb"))
        gate = sem("gate")
        two = ("a", "b")
        s_ready, s_added, s_max, s_sub, p_ready, pt_ready, pt_copied, o_ready, o_norm = (
            [sem(f"{n}_{w}") for w in two] for n in ("s_ready", "s_added", "s_max", "s_sub", "p_ready", "pt_ready",
                                                     "pt_copied", "o_ready", "o_norm"))
        web_ready, z_ready, gelu_ready, hw_ready, hi_ready, lo_pool, lo_dve, y_done, y_copied, yt_ready, fin_ready, stored = (
            sem(n) for n in ("web_ready", "z_ready", "gelu_ready", "hw_ready", "hi_ready", "lo_pool", "lo_dve", "y_done", "y_copied", "yt_ready",
                             "fin_ready", "stored"))

        sum_logs, sums_inverted = sem("sum_logs"), sem("sums_inverted")

        STEPS = TILES + 1
        LN_STEPS, GN_STEPS, GATE_STEPS = 33, 18, 21
        DVE_LOW = 3
        UNITS = 4 * TILES

        def need(eng, s, image, per, kth):
            v = count(image, per, kth)
            if v is not None:
                eng.wait_ge(s, v)

        def schedule(eng, body):
            def peeled(i):
                body(i, i < IMAGES, 1 <= i <= IMAGES, i >= 2, i + 1 < IMAGES)

            for i in range(3):
                peeled(i)
            with eng.Fori(3, IMAGES - 1) as i:
                body(i, True, True, True, True)
            for i in range(IMAGES - 1, IMAGES + 2):
                peeled(i)

        def unit(t, m):
            return t // 4, 2 * (t % 4) + m // 2, m % 2

        def low_part(c, t, m):
            if m == DVE_LOW:
                return lo_dve, c, TILES, t + 1
            return lo_pool, c, 3 * TILES, 3 * t + m + 1

        block = ctx.enter_context(nc.Block())

        loads = [(k[:], consts), (tab_s, rel_table), (fold_s, unfold), (sel[:], selectors), (wq_s[:], wq), (wk_s[:], wk), (wv_s[:], wv), (wo_s[:], wo),
                 (wqkv_s[:], w_qkv), (wp_s[:], w_proj), (gw_s[:, 0:E], gate_w),
                 (w1_s.rearrange("p (e n) -> p e n", e=E), w1.rearrange("e p n -> p e n")),
                 (w2_s.rearrange("p (e c n) -> p e c n", e=E, c=CH), w2.rearrange("e (c p) n -> p e c n", p=P)), (b1_s[:], b1),
                 (cols[:, 0:1], bq), (cols[:, 1:2], bk), (cols[:, 2:3], bv), (cols[:, 3:4], logit_scale),
                 (row_b[:], b_proj.to_broadcast([P, P])), (bo_s[:], bo.to_broadcast([P, P])),
                 (gb_s[:], gate_b.to_broadcast([P, E])), (cw1_s[:], cpb_w1), (cb1_s[:], cpb_b1),
                 (cw2_s[:], cpb_w2.rearrange("(c p) n -> p c n", p=P))]
        loads += [(b2_s[E * g:E * g + E, :], b2) for g in range(GATE_PARTS)]

        @block.sync
        def _(sp):
            for dst, src in loads:
                sp.dma_start(dst, src).then_inc(loaded, 16)

            def load_image(i):
                for r in range(ROWS):
                    for (p0, p1), (c0, c1) in col_pieces:
                        sp.dma_start(xin[SIDE * r + p0:SIDE * r + p1, :, :], x_rolled[i, r, c0:c1, :, :]).then_inc(x_in, 16)

            def store_image(c):
                for r in range(ROWS):
                    for (p0, p1), (c0, c1) in col_pieces:
                        sp.dma_start(out_rolled[c, r, c0:c1, :, :], xn_c[SIDE * r + p0:SIDE * r + p1, :, :]).then_inc(stored, 16)

            load_image(0)
            sp.wait_ge(setup, 9)
            sp.dma_start(scratch.ap(), rel_s).then_inc(bias_io, 16)
            sp.wait_ge(bias_io, 16)
            unfolded = bass.AP(scratch, 0, [[1, WS], [REL, HA * REL], [1, WS]])
            sp.dma_start(unf_s, unfolded).then_inc(bias_io, 16)

            def body(i, do_a, do_b, do_c, do_next):
                a, b, c = i, i - 1, i - 2
                if do_a:
                    need(sp, x_in, a, 16 * IO_DMAS, 16 * IO_DMAS)
                    need(sp, ln_b, b, LN_STEPS, 2)
                    sp.dma_start(x_res[:], xin[:]).then_inc(x_copied, 16)
                if do_next:
                    need(sp, xt_a_ready, a, 2, 2)
                    need(sp, x_copied, a, 16, 16)
                    load_image(i + 1)
                if do_c:
                    need(sp, fin_ready, c, 2, 2)
                    store_image(c)

            schedule(sp, body)
            sp.wait_ge(stored, 16 * IO_DMAS * IMAGES)

        @block.tensor
        def _(pe):
            mm, tr = pe.matmul, pe.transpose
            pe.wait_ge(loaded, 16 * len(loads))
            for c in range(CH):
                last = mm(Z[c][:, 0:REL * REL], cw1_s[:, c * P:(c + 1) * P], tab_s, start=True, stop=True)
            last.then_inc(setup, 1)
            pe.wait_ge(setup, 3)
            for c in range(CH):
                last = mm(Y[0:HA, 0:REL * REL], cw2_s[:, c, :], hid_s[:, c, :], start=(c == 0), stop=(c == CH - 1))
            last.then_inc(setup, 1)
            mm(W[:, 0:P], cols[:, 2:3].to_broadcast([P, P]), wo_s[:], start=True, stop=True).then_inc(setup, 1)
            pe.wait_ge(bias_io, 32)
            for py in range(WS):
                last = mm(SA[:, :].rearrange("p (h n) -> p h n", h=HA), fold_s[:, py * P:py * P + P],
                          unf_s.rearrange("p (h y) w -> p h (y w)", h=HA)[:, :, py * WS:py * WS + WTOK],
                          start=(py == 0), stop=(py == WS - 1))
            last.then_inc(setup, 1)
            pe.wait_ge(ready, 3)

            def tokens(j):
                return slice(P * j, P * j + P)

            def rolled(t):
                return (t - SHIFT // ROWS) % TILES

            def window(w):
                return slice(WTOK * w, WTOK * w + WTOK)

            q_flat = qk_a[:, 0:2, :].rearrange("p a n -> p (a n)")

            def image_half(f, h, free):
                need(pe, x_in, f, 16 * IO_DMAS, 16 * IO_DMAS)
                free()
                for j in range(4):
                    tile = (4 * h + j + SHIFT // ROWS) % TILES
                    last = tr(T[:, P * j:P * j + P], xin[:, tile, :], ident)
                last.then_inc(xt_a_ready, 1)

            def group_stats(f, step, free):
                need(pe, gn, f, GN_STEPS, step - 1)
                free()
                if step == 6:
                    mm(O[:, 0:2], const("group_mean"), gstat[:, 12:14], start=True, stop=True).then_inc(gn, 1)
                else:
                    mm(O[:, 2:3], const("group_mean"), gstat[:, 17:18], start=True, stop=True).then_inc(gn, 1)

            def prepare(a, b, c, do_a, do_b, do_c):
                if do_c:
                    need(pe, o_norm[1], c, TILES, TILES)
                    need(pe, y_copied, c - 1, 2, 2)
                    need(pe, hw_ready, c - 1, UNITS, UNITS)
                    for h, dst in enumerate((Y, W)):
                        for j in range(4):
                            t = 4 * h + j
                            last = mm(dst[:, P * j:P * j + P], ot_b[:, tokens(t)], wp_s[:], start=True, stop=True)
                        last.then_inc(outb_ready, 1)
                if do_b:
                    need(pe, o_norm[0], b, TILES, TILES)
                    need(pe, s_added[0], b, TILES, TILES)
                    need(pe, s_added[1], b - 1, TILES, TILES)
                    for h, dst in enumerate((SA, SB)):
                        for j in range(4):
                            t = 4 * h + j
                            last = mm(dst[:, P * j:P * j + P], ot_a[:, tokens(rolled(t))], wo_s[:], start=True, stop=True)
                        last.then_inc(outa_ready, 1)
                if do_a:
                    need(pe, gn, a, GN_STEPS, GN_STEPS)
                    need(pe, gelu_ready, c - 1, UNITS, UNITS)
                    need(pe, bqk_sb, b - 1, 4, 4)
                    need(pe, o_norm[0], b, TILES, TILES)
                    need(pe, o_norm[1], b - 1, TILES, TILES)
                    need(pe, pt_copied[0], b, TILES, TILES)
                    need(pe, pt_copied[1], b - 1, TILES, TILES)
                    need(pe, fin_ready, c - 1, 2, 2)
                    for n, (w, dst) in enumerate(((wq_s, Z[0]), (wq_s, Z[1]), (wk_s, T), (wk_s, O))):
                        h = n % 2
                        mm(dst[:, :], w[:], xn_a[:, HALF * h:HALF * h + HALF], start=True, stop=True).then_inc(qk_ready, 1)
                    for g, dst in enumerate((*Z, T, O)):
                        need(pe, qk_sb, a, 4, g + 1)
                        for j in range(4):
                            for half in range(2):
                                last = mm(dst[WTOK * half:WTOK * half + WTOK, P * j:P * j + P],
                                          xn_a[:, window(4 * g + j)], wv_s[:], start=True, stop=True)
                        last.then_inc(av_ready, 1)
                    for n, dst in enumerate((*Z, T, O)):
                        need(pe, sq_ready, a, 4, n + 1)
                        need(pe, av_sb, a, 8, 2 * n + 2)
                        mm(dst[:, :], const("head_ones"), sq_a[:, n, :], start=True, stop=True).then_inc(ss_ready, 1)
                if do_c:
                    need(pe, ln_c, c, LN_STEPS, 29)
                    for h, dst in enumerate((Y, W)):
                        for j in range(4):
                            last = tr(dst[:, P * j:P * j + P], xn_c[:, 4 * h + j, :], ident)
                        last.then_inc(ln_c, 1)
                if do_b:
                    need(pe, ln_b, b, LN_STEPS, 29)
                    for h, dst in enumerate((SA, SB)):
                        for j in range(4):
                            last = tr(dst[:, P * j:P * j + P], xn_b[:, 4 * h + j, :], ident)
                        last.then_inc(ln_b, 1)
                if do_c:
                    need(pe, ln_c, c, LN_STEPS, 33)
                    need(pe, xs_ready, c, 4, 2)
                    for t in range(TILES):
                        at = GATE_STRIDE * t
                        last = mm(W[:, at:at + GATE_N], xt_c[:, tokens(t)], gw_s[:], start=True, stop=True)
                    last.then_inc(gate, 1)
                if do_b:
                    need(pe, ln_b, b, LN_STEPS, 33)
                    for n, (w0, dst) in enumerate(((0, SA), (0, SB), (P, Z[0]), (P, Z[1]))):
                        h = n % 2
                        if n >= 2:
                            need(pe, ln_ready, a, 4, n - 1)
                            need(pe, gelu_ready, c - 1, UNITS, UNITS)
                        mm(dst[:, :], wqkv_s[:, w0:w0 + P], xt_b[:, HALF * h:HALF * h + HALF],
                           start=True, stop=True).then_inc(bqk_ready, 1)
                    for h, dst in enumerate((T, O)):
                        need(pe, ln_ready, a, 4, 3 + h)
                        if h == 0:
                            need(pe, pt_copied[0], b, TILES, TILES)
                            need(pe, pt_copied[1], b - 1, TILES, TILES)
                            need(pe, fin_ready, c - 1, 2, 2)
                        else:
                            need(pe, o_norm[0], b, TILES, TILES)
                            need(pe, o_norm[1], b - 1, TILES, TILES)
                        for j in range(4):
                            last = mm(dst[:, P * j:P * j + P], xt_b[:, tokens(4 * h + j)], wqkv_s[:, 2 * P:3 * P],
                                      start=True, stop=True)
                        last.then_inc(bv_ready, 1)

            def gate_rows(c):
                need(pe, gate, c, GATE_STEPS, 19)
                wt = W[:, :].bitcast(BF16)
                for t in range(TILES):
                    last = tr(wt[0:GATE_PARTS * E, tokens(t)], cw3[:, t, :, :].rearrange("p g e -> p (g e)"), ident16[:])
                last.then_inc(gate, 1)

            def expert_bias(c, half):
                need(pe, gate, c, GATE_STEPS, 21)
                if half == 0:
                    need(pe, xs_ready, c, 4, 4)
                else:
                    need(pe, y_copied, c, 2, 1)
                for g in range(GATE_PARTS):
                    mm(Y[:, :], b2_p[:, g, :], cwt[:, HALF * half:HALF * half + HALF], start=(g == 0), stop=False)

            def scores(t, w, a, b):
                if w == 0:
                    need(pe, km_ready, a, TILES, t + 1)
                    need(pe, s_added[0], a, TILES, t)
                    if t == 0:
                        need(pe, bqk_sb, b, 4, 1)
                        need(pe, ln_b, b, LN_STEPS, 33)
                    for j in range(2):
                        last = mm(SA[WTOK * j:WTOK * j + WTOK, :], q_flat[:, window(2 * t + j)],
                                  km_a[:, t % 2, :, WTOK * j:WTOK * j + WTOK], start=True, stop=True)
                else:
                    need(pe, bkm_ready, b, TILES, t + 1)
                    need(pe, s_added[1], b, TILES, t)
                    if t == 0:
                        need(pe, bqk_sb, b, 4, 4)
                    last = mm(SB[:, :], q_b[:, tokens(t)], km_b[:, t % 2, :, :], start=True, stop=True)
                last.then_inc(s_ready[w], 1)

            def bank_t_free(t, use, a, b, c, all_on):
                extra = {3: (gn, a + 1, GN_STEPS, 1), 4: (gn, a + 1, GN_STEPS, 2), 5: (fin_ready, c, 2, 1)}
                probs_a, probs_b = (pt_copied[0], a, TILES, t), (pt_copied[1], b, TILES, t)
                last_probs = [(pt_copied[1], b, TILES, t - 1), (pt_copied[0], a, TILES, t - 1)]
                if use == "probs_a":
                    waits = [extra[t - 1]] if t - 1 in extra else last_probs[:1]
                elif use == "probs_b":
                    waits = [probs_a]
                else:
                    waits = [probs_b]
                if t == 1:
                    waits = waits + [(bv_sb, b, 2, 1), (ln_ready, a, 4, 3)]
                elif not all_on:
                    waits = waits + last_probs + [probs_a] * (use == "extra") + [extra[k] for k in extra if k < t]
                for s, n, per, kth in waits:
                    need(pe, s, n, per, kth)

            def transposed_probs(t, w, n, free):
                need(pe, p_ready[w], n, TILES, t + 1)
                free()
                for j in range(4):
                    last = tr(T[:, P * j:P * j + P], p_sb[w][:, j, :], ident)
                last.then_inc(pt_ready[w], 1)

            def weighted_values(t, a, b, do_a, do_b, stats_read):
                if do_a:
                    need(pe, pt_copied[0], a, TILES, t + 1)
                if do_b:
                    need(pe, pt_copied[1], b, TILES, t + 1)
                need(pe, o_norm[0], a, TILES, t)
                need(pe, o_norm[1], b, TILES, t)
                if t == 0:
                    need(pe, av_sb, a, 8, 8)
                    need(pe, ln_ready, a, 4, 4)
                    need(pe, bv_sb, b, 2, 2)
                stats_read()
                if do_a:
                    for win in range(2):
                        queries = slice(WTOK * win, WTOK * win + WTOK)
                        for j in range(PAIRS):
                            mm(O[DB * j:DB * j + DB, queries], v_a[:, 2 * t + win, DB * j:DB * j + DB],
                               pt_sb[0][:, j, queries], start=True, stop=True)
                    for j in range(PAIRS):
                        last = mm(O[DB * j:DB * j + DB, 2 * P:3 * P], const("ones_a"), pt_sb[0][:, j, :], start=True, stop=True)
                    last.then_inc(o_ready[0], 1)
                if do_b:
                    for h in range(HB):
                        mm(O[DB * h:DB * h + DB, P:2 * P], v_b[:, P * t + DB * h:P * t + DB * h + DB], pt_sb[1][:, h, :],
                           start=True, stop=True)
                    for h in range(HB):
                        last = mm(O[DB * h:DB * h + DB, 3 * P:4 * P], const("ones_b"), pt_sb[1][:, h, :], start=True, stop=True)
                    last.then_inc(o_ready[1], 1)

            def spread_weights(t, j, c):
                e, half = 2 * (t % 4) + j, t // 4
                if t == 0 and j == 0:
                    need(pe, gate, c, GATE_STEPS, 21)
                else:
                    need(pe, hw_ready, c, UNITS, 4 * t + 2 * j)
                mm(W[:, :], sel[:, e * P:(e + 1) * P], cwt[:, HALF * half:HALF * half + HALF],
                   start=True, stop=True).then_inc(web_ready, 1)

            def hidden(t, m, b, c):
                half, e, ch = unit(t, m)
                if 4 * t + m < 2:
                    need(pe, xs_ready, c, 4, 4)
                    need(pe, bqk_sb, b, 4, 3 + m)
                    need(pe, ln_ready, b + 1, 4, 1 + m)
                else:
                    need(pe, gelu_ready, c, UNITS, 4 * t + m - 1)
                w = slice(HID * e + P * ch, HID * e + P * ch + P)
                x = slice(HALF * half, HALF * half + HALF)
                mm(Z[m % 2][:, :], w1_h[:, w], xh_c[:, x], start=True, stop=False)
                mm(Z[m % 2][:, :], w1_h[:, w], xl_c[:, x], start=False, stop=False)
                mm(Z[m % 2][:, :], w1_l[:, w], xh_c[:, x], start=False, stop=True).then_inc(z_ready, 1)

            def expert_out(t, m, c):
                half, e, ch = unit(t, m)
                if t % 4 == 0 and m == 0:
                    expert_bias(c, half)
                w, slot = slice(P * (CH * e + ch), P * (CH * e + ch) + P), 4 * (t % 2) + m
                need(pe, hi_ready, c, UNITS, 4 * t + m + 1)
                mm(Y[:, :], w2_h[:, w], hid_h[:, slot, :], start=False, stop=False)
                mm(Y[:, :], w2_l[:, w], hid_h[:, slot, :], start=False, stop=False)
                need(pe, *low_part(c, t, m))
                mm(Y[:, :], w2_h[:, w], hid_l[:, m, :], start=False, stop=(t % 4 == 3 and m == 3)).then_inc(y_done, 1)

            def transposed_y(half, c, free):
                need(pe, y_copied, c, 2, half + 1)
                free()
                for j in range(4):
                    last = tr(T[:, P * j:P * j + P], y_s[:, P * j:P * j + P], ident)
                last.then_inc(yt_ready, 1)

            for h in range(2):
                image_half(0, h, lambda: need(pe, gn, 0, GN_STEPS, h))
            group_stats(0, 6, lambda: None)
            group_stats(0, 10, lambda: None)

            def body(i, do_a, do_b, do_c, do_next):
                a, b, c = i, i - 1, i - 2
                all_on = do_a and do_b and do_c and do_next
                prepare(a, b, c, do_a, do_b, do_c)
                for t in range(STEPS):
                    now, before = t < TILES, t > 0

                    def t_free(use):
                        return lambda: bank_t_free(t, use, a, b, c, all_on)

                    def o_free():
                        need(pe, o_norm[1], b, TILES, t - 1)
                        need(pe, o_norm[0], a, TILES, t - 1)

                    def stats_read():
                        if do_next and t in (6, 7):
                            need(pe, gn, a + 1, GN_STEPS, 7 if t == 6 else 11)

                    if do_c and t == 0:
                        hidden(0, 0, b, c)
                        hidden(0, 1, b, c)
                    if do_a and now:
                        scores(t, 0, a, b)
                    if do_b and now:
                        scores(t, 1, a, b)
                    if do_c and t == 0:
                        gate_rows(c)
                    if do_next and t in (6, 7):
                        group_stats(a + 1, 6 if t == 6 else 10, o_free)
                    if do_c and now:
                        spread_weights(t, 0, c)
                        if t > 0:
                            hidden(t, 0, b, c)
                            hidden(t, 1, b, c)
                    if do_a and before:
                        transposed_probs(t - 1, 0, a, t_free("probs_a"))
                    if do_c and before:
                        expert_out(t - 1, 0, c)
                    if do_c and now:
                        hidden(t, 2, b, c)
                    if do_b and before:
                        transposed_probs(t - 1, 1, b, t_free("probs_b"))
                    if do_c and before:
                        expert_out(t - 1, 1, c)
                    if do_c and now:
                        hidden(t, 3, b, c)
                    if do_next and t in (3, 4):
                        image_half(a + 1, t - 3, t_free("extra"))
                    if do_c and t == 5:
                        transposed_y(0, c, t_free("extra"))
                    if (do_a or do_b) and before:
                        weighted_values(t - 1, a, b, do_a, do_b, stats_read)
                    if do_c and now:
                        spread_weights(t, 1, c)
                    if do_c and before:
                        expert_out(t - 1, 2, c)
                    if do_c and before:
                        expert_out(t - 1, 3, c)

                def last_y_free():
                    need(pe, pt_copied[0], a, TILES, TILES)
                    need(pe, pt_copied[1], b, TILES, TILES)
                    need(pe, fin_ready, c, 2, 1)

                if do_c:
                    transposed_y(1, c, last_y_free)

            schedule(pe, body)

        @block.scalar
        def _(act):
            func = act.activation
            act.preload_act_table_set(EXP_LN_SET)
            act.wait_ge(setup, 4)
            func(rel_s, Y[0:HA, 0:REL * REL], ACT.Exp, scale=-1.0).then_inc(setup_act, 1)
            act.wait_ge(loaded, 16 * len(loads))
            act.wait_ge(setup, 13)
            func(cols[:, 5:6], cols[:, 4:5], ACT.Exp).then_inc(setup_act, 1)
            act.wait_ge(setup_act, 2)

            def image_copy(f, h):
                need(act, xt_a_ready, f, 2, h + 1)
                need(act, qn_ready, f - 1, 4, 4)
                func(xraw[:, HALF * h:HALF * h + HALF], T[:, :], ACT.Copy).then_inc(gn, 1)

            def group_rstd(f):
                need(act, gn, f, GN_STEPS, 11)
                func(gstat[:, 19:20], gstat[:, 18:19], ACT.Ln, bias=eps5[:, 0:1]).then_inc(gn, 1)
                need(act, gn, f, GN_STEPS, 12)
                func(gstat[:, 20:21], gstat[:, 19:20], ACT.Exp, scale=-0.5).then_inc(gn, 1)

            def layer_rstd(s, n, mv, rs):
                need(act, s, n, LN_STEPS, 18)
                func(rs[:, 0, :], mv[:, :, 1], ACT.Ln, bias=eps5[:, 0:1]).then_inc(s, 1)
                need(act, s, n, LN_STEPS, 19)
                func(rs[:, 1, :], rs[:, 0, :], ACT.Exp, scale=-0.5).then_inc(s, 1)

            def layer_copy(s, n, banks, dst):
                for h, src in enumerate(banks):
                    need(act, s, n, LN_STEPS, 31 + h)
                    func(dst[:, HALF * h:HALF * h + HALF], src[:, :], ACT.Copy).then_inc(s, 1)

            act.preload_act_table_set(EXP_LN_SET)
            act.wait_ge(ready, 3)
            for h in range(2):
                image_copy(0, h)
            group_rstd(0)

            def body(i, do_a, do_b, do_c, do_next):
                a, b, c = i, i - 1, i - 2
                if do_a:
                    need(act, s_ready[0], a - 1, TILES, TILES)
                    need(act, km_ready, a - 1, TILES, TILES)
                    for n, src in enumerate((*Z, T, O)):
                        need(act, qk_ready, a, 4, n + 1)
                        func(qk_a[:, n, :], src[:, :], ACT.Identity, bias=cols[:, n // 2:n // 2 + 1]).then_inc(qk_sb, 1)
                if do_c:
                    layer_rstd(ln_c, c, mv_c, rs_c)
                if do_a:
                    need(act, o_ready[0], a - 1, TILES, TILES)
                    for g, src in enumerate((*Z, T, O)):
                        need(act, av_ready, a, 4, g + 1)
                        for par in range(2):
                            ps = slice(WTOK * par, WTOK * par + WTOK)
                            v = src[ps, :].rearrange("p (w j e c) -> p w j e c", w=4, j=PAIRS, e=2)
                            dst = v_a[ps, 4 * g:4 * g + 4, :].rearrange("p w (j e c) -> p w j e c", j=PAIRS, e=2)
                            func(dst[:, :, :, par, :], v[:, :, :, par, :], ACT.Copy).then_inc(av_sb, 1)
                if do_b:
                    layer_rstd(ln_b, b, mv_b, rs_b)
                if do_a:
                    for n, src in enumerate((*Z, T, O)):
                        need(act, ss_ready, a, 4, n + 1)
                        func(sq_a[:, n, :], src[:, :], ACT.Ln, bias=eps5[:, 1:2], scale=2.0 ** NORM_SHIFT).then_inc(ln_ready, 1)
                if do_c:
                    layer_copy(ln_c, c, (Y, W), xt_c)
                    need(act, z_ready, c - 1, UNITS, UNITS)
                    for h in (1, 0):
                        src = (Y, W)[h]
                        func(xh_c[:, HALF * h:HALF * h + HALF], src[:, :], ACT.Copy).then_inc(xs_ready, 1)
                if do_a:
                    for n in range(4):
                        need(act, ln_ready, a, 4, n + 1)
                        func(sq_a[:, n, :], sq_a[:, n, :], ACT.Exp, scale=-0.5,
                             bias=eps5[:, 2 + n // 2:3 + n // 2]).then_inc(rn_ready, 1)
                if do_b:
                    need(act, s_ready[1], b - 1, TILES, TILES)
                    need(act, bkm_ready, b - 1, TILES, TILES)
                    for n, src in enumerate((SA, SB, *Z)):
                        need(act, bqk_ready, b, 4, n + 1)
                        dst = (q_b, k_b)[n // 2]
                        func(dst[:, HALF * (n % 2):HALF * (n % 2) + HALF], src[:, :], ACT.Copy).then_inc(bqk_sb, 1)
                if do_c:
                    need(act, gate, c, GATE_STEPS, 4)
                    func(pr[:, :, :], lg[:, :, :], ACT.Exp).then_inc(gate, 1)
                    act.preload_act_table_set(GELU_SET)
                if do_b:
                    for h, src in enumerate((T, O)):
                        need(act, bv_ready, b, 2, h + 1)
                        need(act, o_ready[1], b - 1, TILES, TILES)
                        func(v_b[:, HALF * h:HALF * h + HALF], src[:, :], ACT.Copy).then_inc(bv_sb, 1)
                for t in range(STEPS):
                    now, before = t < TILES, t > 0

                    def gelu(m):
                        _, e, ch = unit(t, m)
                        need(act, z_ready, c, UNITS, 4 * t + m + 1)
                        if t >= 2:
                            need(act, *low_part(c, t - 2, m))
                        else:
                            need(act, *low_part(c - 1, TILES - 2 + t, m))
                        func(hid[:, 4 * (t % 2) + m, :], Z[m % 2][:, :], ACT.Gelu,
                             bias=b1_s[:, CH * e + ch:CH * e + ch + 1]).then_inc(gelu_ready, 1)

                    def probs_copy(w, n):
                        need(act, pt_ready[w], n, TILES, t)
                        if t >= 2:
                            need(act, o_ready[w], n, TILES, t - 1)
                        else:
                            need(act, o_ready[w], n - 1, TILES, TILES)
                        func(pt_sb[w][:, :, :].rearrange("p j n -> p (j n)"), T[:, :], ACT.Copy).then_inc(pt_copied[w], 1)

                    def probs(w, n):
                        need(act, s_sub[w], n, TILES, t + 1)
                        need(act, pt_ready[w], n, TILES, t)
                        func(p_sb[w][:, :, :].rearrange("p j n -> p (j n)"), s_sb[w][:, :, :].rearrange("p h n -> p (h n)"),
                             ACT.Exp, scale=1.0 if w == 0 else float(DB) ** -0.5).then_inc(p_ready[w], 1)

                    if do_c and now:
                        gelu(0)
                        gelu(1)
                    if do_c and t == 0:
                        need(act, gate, c, GATE_STEPS, 20)
                        func(cwt[:, :], W[:, :].bitcast(BF16)[0:GATE_PARTS * E, :], ACT.Copy).then_inc(gate, 1)
                    if do_a and before:
                        probs_copy(0, a)
                    if do_c and now:
                        gelu(2)
                    if do_b and before:
                        probs_copy(1, b)
                    if do_c and now:
                        gelu(3)
                    if do_next and t in (3, 4):
                        image_copy(a + 1, t - 3)
                    if now:
                        act.preload_act_table_set(EXP_LN_SET)
                    if (do_a or do_b) and before:
                        need(act, o_ready[0], a, TILES, t)
                        need(act, o_ready[1], b, TILES, t)
                        need(act, o_norm[0], a, TILES, t - 1)
                        need(act, o_norm[1], b, TILES, t - 1)
                        lo, hi = (0 if do_a else P), (2 * P if do_b else P)
                        func(sum_inv[:, lo:hi], O[:, 2 * P + lo:2 * P + hi], ACT.Ln).then_inc(sum_logs, 1)
                        act.wait_ge(sum_logs, i * TILES + t)
                        func(sum_inv[:, lo:hi], sum_inv[:, lo:hi], ACT.Exp, scale=-1.0).then_inc(sums_inverted, 1)
                    if now:
                        if do_a:
                            probs(0, a)
                        if do_b:
                            probs(1, b)
                        if do_c and t < TILES - 1:
                            act.preload_act_table_set(GELU_SET)
                    if do_next and t == 7:
                        group_rstd(a + 1)
                    if do_c and t == 4:
                        need(act, y_done, c, UNITS, 4 * t)
                        func(y_s[:, :], Y[:, :], ACT.Copy).then_inc(y_copied, 1)
                if do_c:
                    need(act, y_done, c, UNITS, UNITS)
                    need(act, yt_ready, c, 2, 1)
                    func(y_s[:, :], Y[:, :], ACT.Copy).then_inc(y_copied, 1)

            schedule(act, body)

        @block.gpsimd
        def _(pool):
            pool.memset(v_a[:, :, :], 0.0).then_inc(setup_act, 1)
            pool.wait_ge(ready, 3)

            def low_hidden(eng, c, t, m):
                slot = 4 * (t % 2) + m
                need(eng, hi_ready, c, UNITS, 4 * t + m + 1)
                if t > 0:
                    need(eng, y_done, c, UNITS, 4 * (t - 1) + m + 1)
                eng.tensor_tensor(hid_l[:, m, :], hid[:, slot, :], hid_h[:, slot, :].bitcast(F32),
                                  ALU.subtract).then_inc(low_part(c, t, m)[0], 1)

            def masked_keys(w, n, t):
                need(pool, s_ready[w], n, TILES, t - 1)
                if t < 2:
                    need(pool, s_ready[w], n - 1, TILES, TILES)
                if w == 0:
                    need(pool, qn_ready, n, 4, 3 + t // 4)
                    keys, mask, dst, s = qk_a[:, 2 + t // 4, P * (t % 4):P * (t % 4) + P], const("head_mask_a"), km_a, km_ready
                else:
                    need(pool, bqk_sb, n, 4, 3 + t // 4)
                    keys, mask, dst, s = k_b[:, P * t:P * t + P], const("head_mask_b"), km_b, bkm_ready
                shape = [P, (HA, HB)[w], P]
                pool.tensor_tensor(dst[:, t % 2, :, :], keys[:, None, :].to_broadcast(shape),
                                   mask[:, :, None].to_broadcast(shape), ALU.mult).then_inc(s, 1)

            def body(i, do_a, do_b, do_c, do_next):
                a, b, c = i, i - 1, i - 2
                if do_a:
                    for n in range(4):
                        need(pool, qk_sb, a, 4, n + 1)
                        if n < 2:
                            need(pool, gn, a, GN_STEPS, GN_STEPS)
                        pool.tensor_tensor(sq_a[:, n, :], qk_a[:, n, :], qk_a[:, n, :], ALU.mult).then_inc(sq_ready, 1)
                if do_b:
                    need(pool, ln_b, b, LN_STEPS, 29)
                    pool.tensor_tensor(t1[:, :, :], t1[:, :, :], row_b[:, None, :].to_broadcast([P, TILES, D]),
                                       ALU.add).then_inc(t1b_ready, 1)
                if do_b:
                    masked_keys(1, b, 0)
                if do_a:
                    masked_keys(0, a, 0)
                for t in range(TILES):
                    if t + 1 < TILES:
                        if do_a:
                            masked_keys(0, a, t + 1)
                        if do_b:
                            masked_keys(1, b, t + 1)
                    for w, n, on, s, m, width in ((0, a, do_a, s_sb[0], mx_s[0], WTOK), (1, b, do_b, s_sb[1], mx_s[1], P)):
                        if on:
                            need(pool, s_max[w], n, TILES, t + 1)
                            h = (HA, HB)[w]
                            pool.tensor_tensor(s[:, :, :], s[:, :, :], m[:, :, None].to_broadcast([P, h, width]),
                                               ALU.subtract).then_inc(s_sub[w], 1)
                    if do_c:
                        for chunk in range(4):
                            if chunk != DVE_LOW:
                                low_hidden(pool, c, t, chunk)
                    if t == 1 and do_a:
                        need(pool, x_copied, a, 16, 16)
                        pool.tensor_tensor(x_res[:, :, :], x_res[:, :, :], row_a[:, None, :].to_broadcast([P, TILES, D]),
                                           ALU.add).then_inc(res_ready, 1)

            schedule(pool, body)

        @block.vector
        def _(dve):
            tt, ts, stt = dve.tensor_tensor, dve.tensor_scalar, dve.scalar_tensor_tensor
            dve.memset(gw_s[:, E:], 0.0)
            dve.wait_ge(loaded, 16 * len(loads))
            dve.tensor_copy(w1_h[:], w1_s).then_inc(w_split, 1)
            dve.tensor_copy(w2_h[:], w2_s).then_inc(w_split, 1)
            dve.wait_ge(w_split, 2)
            tt(w1_l[:], w1_s, w1_h[:].bitcast(F32), ALU.subtract).then_inc(w_split, 1)
            tt(w2_l[:], w2_s, w2_h[:].bitcast(F32), ALU.subtract).then_inc(w_split, 1)
            dve.wait_ge(setup, 1)
            for c in range(CH):
                ts(hid_s[:, c, :], Z[c][:, 0:REL * REL], cb1_s[:, c:c + 1], 0.0, ALU.add, ALU.max).then_inc(setup, 1)
            dve.wait_ge(setup, 5)
            dve.wait_ge(setup_act, 2)
            tt(row_a[:], W[:, 0:P], bo_s[:], ALU.add).then_inc(setup, 1)
            ts(rel_s, rel_s, 1.0, None, ALU.add).then_inc(setup, 1)
            dve.wait_ge(setup, 7)
            dve.reciprocal(rel_s, rel_s).then_inc(setup, 1)
            dve.wait_ge(setup, 8)
            ts(rel_s, rel_s, 16.0, None, ALU.mult).then_inc(setup, 1)
            dve.wait_ge(setup, 10)
            for kind in range(4):
                a = CONST["mask_a"][0] + kind * WTOK
                last = tt(bias_a[:, kind, :, :], SA[:, :].rearrange("p (h n) -> p h n", h=HA),
                          k[:, None, a:a + WTOK].to_broadcast([P, HA, WTOK]), ALU.add)
            last.then_inc(setup, 1)
            dve.tensor_copy(ident16[:], ident).then_inc(setup, 1)
            ts(cols[:, 4:5], cols[:, 3:4], float(np.log(100.0)), None, ALU.min).then_inc(setup, 1)
            dve.wait_ge(setup, 13)
            dve.memset(eps5[:, 0:1], 1e-5)
            dve.memset(eps5[:, 1:2], 2.0 ** -64)
            ts(eps5[:, 2:3], cols[:, 4:5], NORM_SHIFT * LN2 / 2, None, ALU.add)
            dve.memset(eps5[:, 3:4], NORM_SHIFT * LN2 / 2)
            dve.wait_ge(setup_act, 3)
            ts(cols[:, 6:7], cols[:, 5:6], NORM_CAP, None, ALU.mult)
            dve.tensor_copy(b2_p[:, 0, :], b2_s[:]).then_inc(setup, 1)
            dve.wait_ge(setup, 14)
            tt(b2_r[:, 0, :], b2_s[:], b2_p[:, 0, :], ALU.subtract).then_inc(setup, 1)
            dve.wait_ge(setup, 15)
            dve.tensor_copy(b2_p[:, 1, :], b2_r[:, 0, :]).then_inc(setup, 1)
            dve.wait_ge(setup, 16)
            tt(b2_r[:, 1, :], b2_r[:, 0, :], b2_p[:, 1, :], ALU.subtract).then_inc(setup, 1)
            dve.wait_ge(setup, 17)
            dve.wait_ge(w_split, 4)
            dve.tensor_copy(b2_p[:, 2, :], b2_r[:, 1, :]).then_inc(ready, 3)

            def residual(s, n, banks, old, new):
                for h, src in enumerate(banks):
                    tt(new[:, 4 * h:4 * h + 4, :].rearrange("p t d -> p (t d)"), src[:, :],
                       old[:, 4 * h:4 * h + 4, :].rearrange("p t d -> p (t d)"), ALU.add).then_inc(s, 1)

            def layer_norm_stats(s, n, tok, st, mv):
                need(dve, s, n, LN_STEPS, 2)
                for t in range(TILES):
                    dve.bn_stats(st[:, t, :], tok[:, t, :]).then_inc(s, 1)
                need(dve, s, n, LN_STEPS, 10)
                dve.memset(pad[:, 0:1], 0.0)
                for t in range(TILES):
                    dve.bn_aggr(mv[:, t, :], st[:, t, :]).then_inc(s, 1)

            def layer_norm_apply(s, n, tok, mv, rs, xn):
                need(dve, s, n, LN_STEPS, 20)
                stt(rs[:, 2, :], mv[:, :, 0], -1.0, rs[:, 1, :], ALU.mult, ALU.mult).then_inc(s, 1)
                need(dve, s, n, LN_STEPS, 21)
                for t in range(TILES):
                    ts(xn[:, t, :], tok[:, t, :], rs[:, 1, t:t + 1], rs[:, 2, t:t + 1], ALU.mult, ALU.add).then_inc(s, 1)

            def group_norm_stats(f):
                for h in range(2):
                    need(dve, gn, f, GN_STEPS, 2)
                    dve.bn_stats(gstat[:, 6 * h:6 * h + 6], xraw[:, HALF * h:HALF * h + HALF]).then_inc(gn, 1)
                need(dve, gn, f, GN_STEPS, 4)
                dve.memset(pad[:, 1:2], 0.0)
                dve.bn_aggr(gstat[:, 12:14], gstat[:, 0:12]).then_inc(gn, 1)

            def group_norm_means(f):
                need(dve, gn, f, GN_STEPS, 6)
                dve.tensor_copy(gstat[:, 14:16], O[:, 0:2]).then_inc(gn, 1)
                need(dve, gn, f, GN_STEPS, 7)
                tt(gstat[:, 16:17], gstat[:, 12:13], gstat[:, 14:15], ALU.subtract).then_inc(gn, 1)
                need(dve, gn, f, GN_STEPS, 8)
                tt(gstat[:, 17:18], gstat[:, 16:17], gstat[:, 16:17], ALU.mult).then_inc(gn, 1)

            def group_norm_variance(f):
                need(dve, gn, f, GN_STEPS, 10)
                tt(gstat[:, 18:19], O[:, 2:3], gstat[:, 15:16], ALU.add).then_inc(gn, 1)

            def group_norm_apply(a):
                need(dve, gn, a, GN_STEPS, 13)
                need(dve, av_ready, a - 1, 4, 4)
                stt(gstat[:, 21:22], gstat[:, 14:15], -1.0, gstat[:, 20:21], ALU.mult, ALU.mult).then_inc(gn, 1)
                need(dve, gn, a, GN_STEPS, 14)
                for wi in range(SIDE // WS):
                    span = slice(WS * SIDE * wi, WS * SIDE * (wi + 1))
                    ts(xn_a[:, span].rearrange("p (w y x) -> p y w x", y=WS, x=WS),
                       xraw[:, span].rearrange("p (y w x) -> p y w x", y=WS, x=WS),
                       gstat[:, 20:21], gstat[:, 21:22], ALU.mult, ALU.add).then_inc(gn, 1)

            def gate_weights(c, first):
                def step(n):
                    need(dve, gate, c, GATE_STEPS, n)

                pb = pr[:, :, :]
                shape = [P, TILES, E, E]
                ge, gt = cmp_c
                if first == 0:
                    step(1)
                    tt(lg[:, :, :], W[:, 0:TILES * GATE_STRIDE].rearrange("p (t n) -> p t n", t=TILES)[:, :, 0:E],
                       gb_s[:, None, :].to_broadcast([P, TILES, E]), ALU.add).then_inc(gate, 1)
                    step(2)
                    dve.tensor_reduce(col_c[:, 0, :], lg[:, :, :], AX_X, ALU.max).then_inc(gate, 1)
                    step(3)
                    tt(lg[:, :, :], lg[:, :, :], col_c[:, 0, :, None].to_broadcast([P, TILES, E]), ALU.subtract).then_inc(gate, 1)
                    return
                step(5)
                dve.tensor_reduce(col_c[:, 1, :], pb, AX_X, ALU.add).then_inc(gate, 1)
                step(6)
                dve.reciprocal(col_c[:, 2, :], col_c[:, 1, :]).then_inc(gate, 1)
                step(7)
                tt(pb, pb, col_c[:, 2, :, None].to_broadcast([P, TILES, E]), ALU.mult).then_inc(gate, 1)
                step(8)
                other, own = pr[:, :, None, :].to_broadcast(shape), pr[:, :, :, None].to_broadcast(shape)
                tt(ge, other, own, ALU.is_equal).then_inc(gate, 1)
                tt(gt, other, own, ALU.is_gt).then_inc(gate, 1)
                step(10)
                flat0 = ge.rearrange("p t e f -> p t (e f)")
                flat1 = gt.rearrange("p t e f -> p t (e f)")
                tt(flat0, flat0, const("tri")[:, None, :].to_broadcast([P, TILES, E * E]), ALU.mult).then_inc(gate, 1)
                step(11)
                tt(flat1, flat1, flat0, ALU.add).then_inc(gate, 1)
                step(12)
                dve.tensor_reduce(rank_c[:, :, :], gt, AX_X, ALU.add).then_inc(gate, 1)
                step(13)
                stt(cw[:, 0, :, :], rank_c[:, :, :], 2.0, pb, ALU.is_lt, ALU.mult).then_inc(gate, 1)
                step(14)
                dve.tensor_copy(cw3[:, :, 0, :], cw[:, 0, :, :]).then_inc(gate, 1)
                step(15)
                tt(cw[:, 1, :, :], cw[:, 0, :, :], cw3[:, :, 0, :], ALU.subtract).then_inc(gate, 1)
                step(16)
                dve.tensor_copy(cw3[:, :, 1, :], cw[:, 1, :, :]).then_inc(gate, 1)
                step(17)
                tt(cw[:, 2, :, :], cw[:, 1, :, :], cw3[:, :, 1, :], ALU.subtract).then_inc(gate, 1)
                step(18)
                dve.tensor_copy(cw3[:, :, 2, :], cw[:, 2, :, :]).then_inc(gate, 1)

            group_norm_stats(0)
            group_norm_means(0)
            group_norm_variance(0)
            group_norm_apply(0)

            def body(i, do_a, do_b, do_c, do_next):
                a, b, c = i, i - 1, i - 2
                if do_c:
                    need(dve, outb_ready, c, 2, 2)
                    need(dve, t1b_ready, c, 1, 1)
                    need(dve, fin_ready, c - 1, 2, 2)
                    residual(ln_c, c, (Y, W), t1, t2)
                    layer_norm_stats(ln_c, c, t2, st_c, mv_c)
                if do_b:
                    need(dve, outa_ready, b, 2, 2)
                    need(dve, res_ready, b, 1, 1)
                    need(dve, ln_c, c, LN_STEPS, 2)
                    need(dve, ln_b, b - 1, LN_STEPS, LN_STEPS)
                    residual(ln_b, b, (SA, SB), x_res, t1)
                if do_c:
                    need(dve, stored, c - 1, 16 * IO_DMAS, 16 * IO_DMAS)
                    layer_norm_apply(ln_c, c, t2, mv_c, rs_c, xn_c)
                if do_b:
                    layer_norm_stats(ln_b, b, t1, st_b, mv_b)
                    layer_norm_apply(ln_b, b, t1, mv_b, rs_b, xn_b)
                if do_b:
                    for h, src in enumerate((SA, SB)):
                        need(dve, ln_b, b, LN_STEPS, 31 + h)
                        need(dve, bv_ready, b - 1, 2, 2)
                        dve.tensor_copy(xt_b[:, HALF * h:HALF * h + HALF], src[:, :]).then_inc(ln_b, 1)
                if do_c:
                    need(dve, z_ready, c - 1, UNITS, UNITS)
                    for h in (1, 0):
                        need(dve, xs_ready, c, 4, 2)
                        need(dve, ln_c, c, LN_STEPS, 33)
                        span = slice(HALF * h, HALF * h + HALF)
                        tt(xl_c[:, span], xt_c[:, span], xh_c[:, span].bitcast(F32), ALU.subtract).then_inc(xs_ready, 1)
                    gate_weights(c, 0)
                if do_a:
                    for n in (2, 3, 0, 1):
                        need(dve, rn_ready, a, 4, 4)
                        cap = cols[:, 6:7] if n < 2 else NORM_CAP
                        stt(qk_a[:, n, :], sq_a[:, n, :], cap, qk_a[:, n, :], ALU.min, ALU.mult).then_inc(qn_ready, 1)
                if do_c:
                    gate_weights(c, 5)
                def final_add(half):
                    need(dve, yt_ready, c, 2, half + 1)
                    tt(xn_c[:, 4 * half:4 * half + 4, :].rearrange("p t d -> p (t d)"), T[:, :],
                       t2[:, 4 * half:4 * half + 4, :].rearrange("p t d -> p (t d)"), ALU.add).then_inc(fin_ready, 1)

                for t in range(STEPS):
                    now, before = t < TILES, t > 0

                    def biased(w, n):
                        need(dve, s_ready[w], n, TILES, t + 1)
                        if t > 0:
                            need(dve, p_ready[w], n, TILES, t)
                        else:
                            need(dve, p_ready[w], n - 1, TILES, TILES)
                        if w == 0:
                            kind = 2 * (t // 6) + t % 2
                            tt(s_sb[0][:, :, :].rearrange("p h n -> p (h n)"), SA[:, :],
                               bias_a[:, kind, :, :].rearrange("p h n -> p (h n)"), ALU.add).then_inc(s_added[0], 1)
                        else:
                            tt(s_sb[1][:, :, :], SB[:, :].rearrange("p (h n) -> p h n", h=HB),
                               const("mask_b")[:, None, :].to_broadcast([P, HB, P]), ALU.add).then_inc(s_added[1], 1)
                        need(dve, s_added[w], n, TILES, t + 1)
                        dve.tensor_reduce(mx_s[w][:], s_sb[w][:, :, :], AX_X, ALU.max).then_inc(s_max[w], 1)

                    def weigh(m):
                        slot = hid[:, 4 * (t % 2) + m, :]
                        need(dve, gelu_ready, c, UNITS, 4 * t + m + 1)
                        need(dve, web_ready, c, 2 * TILES, 2 * t + m // 2 + 1)
                        tt(slot, slot, W[:, :], ALU.mult).then_inc(hw_ready, 1)

                    def high_hidden(m):
                        slot = 4 * (t % 2) + m
                        need(dve, hw_ready, c, UNITS, 4 * t + m + 1)
                        if t >= 2:
                            need(dve, y_done, c, UNITS, 4 * (t - 2) + m + 1)
                        else:
                            need(dve, y_done, c - 1, UNITS, UNITS)
                        dve.tensor_copy(hid_h[:, slot, :], hid[:, slot, :]).then_inc(hi_ready, 1)

                    def low_hidden(m):
                        slot = 4 * (t % 2) + m
                        need(dve, hi_ready, c, UNITS, 4 * t + m + 1)
                        if t > 0:
                            need(dve, y_done, c, UNITS, 4 * (t - 1) + m + 1)
                        tt(hid_l[:, m, :], hid[:, slot, :], hid_h[:, slot, :].bitcast(F32),
                           ALU.subtract).then_inc(lo_dve, 1)

                    def normalised():
                        dve.wait_ge(sums_inverted, i * TILES + t)
                        if do_a:
                            need(dve, outa_ready, a - 1, 2, 2)
                            y0, x0 = WS * ((t - 1) // 2), 2 * WS * ((t - 1) % 2)
                            dst = ot_a[:, :].rearrange("p (y x) -> p y x", x=SIDE)[:, y0:y0 + WS, x0:x0 + 2 * WS]
                            tt(dst.rearrange("p y (w x) -> p w y x", w=2),
                               O[:, 0:P].rearrange("p (w y x) -> p w y x", w=2, y=WS),
                               sum_inv[:, 0:P].rearrange("p (w y x) -> p w y x", w=2, y=WS), ALU.mult).then_inc(o_norm[0], 1)
                        if do_b:
                            need(dve, outb_ready, b - 1, 2, 2)
                            tt(ot_b[:, P * (t - 1):P * t], O[:, P:2 * P], sum_inv[:, P:2 * P], ALU.mult).then_inc(o_norm[1], 1)

                    if do_next and t == 5:
                        group_norm_stats(a + 1)
                    if do_next and t == 6:
                        group_norm_means(a + 1)
                    if do_next and t == 7:
                        group_norm_variance(a + 1)
                    if do_next and t == 8:
                        group_norm_apply(a + 1)
                    if do_a and now:
                        biased(0, a)
                    if do_b and now:
                        biased(1, b)
                    if do_c and now:
                        weigh(0)
                        weigh(1)
                        high_hidden(0)
                        high_hidden(1)
                    if do_c and t == 5:
                        final_add(0)
                    if do_c and now:
                        weigh(2)
                        weigh(3)
                        high_hidden(2)
                        high_hidden(3)
                        low_hidden(DVE_LOW)
                    if (do_a or do_b) and before:
                        normalised()
                if do_c:
                    final_add(1)

            schedule(dve, body)


_INPUTS = ["x", "wq", "bq", "wk", "bk", "wv", "bv", "wo", "bo", "logit_scale", "cpb_w1", "cpb_b1", "cpb_w2",
           "w_qkv", "w_proj", "b_proj", "gate_w", "gate_b", "w1", "b1", "w2", "b2", "consts", "rel_table", "unfold", "selectors"]


def kernel(x, L0_conv_Wq, L0_conv_bq, L0_conv_Wk, L0_conv_bk, L0_conv_Wv, L0_conv_bv, L0_conv_Wo, L0_conv_bo,
           L0_conv_logit_scale, L0_conv_cpb_w1, L0_conv_cpb_b1, L0_conv_cpb_w2, L1_attn_Wqkv, L1_attn_Wproj,
           L1_attn_bproj, L1_ffn_gate_w, L1_ffn_gate_b, L1_ffn_W1, L1_ffn_b1, L1_ffn_W2, L1_ffn_b2):
    import ml_dtypes
    import concourse.bacc as bacc
    from concourse.bass_utils import run_bass_kernel_spmd

    col, row = (lambda v: np.asarray(v).reshape(-1, 1)), (lambda v: np.asarray(v).reshape(1, -1))
    arrays = dict(zip(_INPUTS, [
        x, np.asarray(L0_conv_Wq).T, col(L0_conv_bq), np.asarray(L0_conv_Wk).T, col(L0_conv_bk),
        np.asarray(L0_conv_Wv).T, col(L0_conv_bv), np.asarray(L0_conv_Wo).T, row(L0_conv_bo),
        col(np.repeat(np.asarray(L0_conv_logit_scale).reshape(-1), DA)),
        np.asarray(L0_conv_cpb_w1).T, np.asarray(L0_conv_cpb_b1).reshape(CH, P).T, np.asarray(L0_conv_cpb_w2).T,
        L1_attn_Wqkv, L1_attn_Wproj, row(L1_attn_bproj), L1_ffn_gate_w, row(L1_ffn_gate_b),
        L1_ffn_W1, np.asarray(L1_ffn_b1).reshape(E * CH, P).T, L1_ffn_W2, L1_ffn_b2,
        *shape_constants(), expert_selectors().astype(ml_dtypes.bfloat16)]))
    nc = bacc.Bacc("TRN2", target_bir_lowering=False, num_devices=1)
    feeds, args = {}, []
    for name in _INPUTS:
        v = np.ascontiguousarray(arrays[name])
        feeds[f"in_{name}_dram"] = v
        args.append(nc.dram_tensor(f"in_{name}_dram", v.shape, mybir.dt.from_np(v.dtype), kind="ExternalInput").ap())
    args.append(nc.dram_tensor("out_0_dram", (IMAGES, SIDE, SIDE, D), F32, kind="ExternalOutput").ap())
    hybrid_kernel(nc, *args)
    return run_bass_kernel_spmd(nc, [feeds], core_ids=[0]).results[0]["out_0_dram"]
```

```python
from contextlib import ExitStack

import concourse.bass as bass
import numpy as np
from concourse import mybir

P = 128
IMAGES, SIDE, D = 32, 32, 128
TOKENS = SIDE * SIDE
TILES = TOKENS // P
ROWS = P // SIDE
HALF = TOKENS // 2
WS, SHIFT = 8, 4
WTOK = WS * WS
WINDOWS = TOKENS // WTOK
HA, DA = 8, 16
PAIRS = HA // 2
HB, DB = 4, 32
RADIUS = 32
E, HID = 8, 256
CH = HID // P
GROUP = 4
GATE_N, GATE_STRIDE = 96, 56
REL = 2 * WS - 1
GATE_PARTS = 3

F32 = mybir.dt.float32
F32R = mybir.dt.float32r
BF16 = mybir.dt.bfloat16
ALU = mybir.AluOpType
ACT = mybir.ActivationFunctionType
AX_X = mybir.AxisListType.X
EXP_LN_SET = "natural_log_exp_and_others"
GELU_SET = "gelu_and_others"

NORM_SHIFT = 20
LN2 = float(np.log(2.0))
NORM_CAP = 1e12
MASKED = -1e30

CONST = {}


def _columns():
    at = 0
    for name, width in (("identity", P), ("group_mean", P), ("head_ones", P), ("head_mask_a", HA), ("head_mask_b", HB),
                        ("tri", E * E), ("mask_a", 4 * WTOK), ("mask_b", P), ("ones_a", DB), ("ones_b", DB)):
        CONST[name] = (at, at + width)
        at += width
    return at


CONST_WIDTH = _columns()


def shape_constants():
    c = np.zeros((P, CONST_WIDTH), np.float32)

    def put(name, value):
        a, _ = CONST[name]
        value = np.asarray(value, np.float32)
        c[:value.shape[0], a:a + value.shape[1]] = value

    ch = np.arange(P)
    put("identity", np.eye(P))
    put("group_mean", (ch[:, None] // GROUP == ch[None] // GROUP) / GROUP)
    put("head_ones", ch[:, None] // DA == ch[None] // DA)
    put("head_mask_a", ch[:, None] // DA == np.arange(HA)[None])
    put("head_mask_b", ch[:, None] // DB == np.arange(HB)[None])
    put("ones_a", ch[:, None] // WTOK == np.arange(DB)[None] // DA)
    put("ones_b", np.ones((P, DB)))
    e = np.arange(E)
    put("tri", np.broadcast_to((e[None] < e[:, None]).reshape(1, -1), (P, E * E)))
    img = np.zeros((SIDE, SIDE), np.int32)
    cuts = (slice(0, -WS), slice(-WS, -SHIFT), slice(-SHIFT, None))
    for a, hs in enumerate(cuts):
        for b, ws in enumerate(cuts):
            img[hs, ws] = 3 * a + b
    win = img.reshape(SIDE // WS, WS, SIDE // WS, WS).transpose(0, 2, 1, 3).reshape(SIDE // WS, SIDE // WS, WTOK)
    for bottom in range(2):
        for right in range(2):
            pair = win[3 * bottom, 2 * right:2 * right + 2]
            m = np.where(pair[:, :, None] != pair[:, None, :], -100.0, 0.0).reshape(P, WTOK)
            a = CONST["mask_a"][0] + (2 * bottom + right) * WTOK
            c[:, a:a + WTOK] = m
    n = SIDE * (ch // SIDE) + (ch % SIDE + SHIFT) % SIDE
    d = n[:, None] - n[None]
    put("mask_b", np.where((d >= 0) & (d <= RADIUS), 0.0, MASKED))
    r = np.arange(-(WS - 1), WS, dtype=np.float32)
    tbl = np.stack(np.meshgrid(r, r, indexing="ij"), axis=-1) / (WS - 1) * 8.0
    tbl = (np.sign(tbl) * np.log2(np.abs(tbl) + 1.0) / np.log2(8.0)).reshape(-1, 2)
    table = tbl[::-1].T.astype(np.float32)
    q = ch % WTOK
    unfold = np.stack([(np.arange(WS)[:, None] == WS - 1 - q[None] % WS) & (WS - 1 - q[None] // WS == py)
                       for py in range(WS)], axis=1).astype(np.float32).reshape(WS, WS * P)
    return c, table, unfold


def expert_selectors():
    s = np.zeros((GATE_PARTS * E, E, P), np.float32)
    for e in range(E):
        s[e::E, e] = 1.0
    return s.reshape(GATE_PARTS * E, E * P)


def count(image, per, k):
    if isinstance(image, int):
        image, k = (image, k) if 0 <= image < IMAGES else ((0, 0) if image < 0 else (IMAGES, 0))
        v = image * per + k
        return v if v > 0 else None
    return image * per + k


def hybrid_kernel(nc, x, wq, bq, wk, bk, wv, bv, wo, bo, logit_scale, cpb_w1, cpb_b1, cpb_w2,
                  w_qkv, w_proj, b_proj, gate_w, gate_b, w1, b1, w2, b2, consts, rel_table, unfold, selectors, out):
    scratch = nc.dram_tensor("rel_bias_scratch", [HA, REL * REL], F32)
    x_rolled = x.rearrange("a (t r) c d -> a r c t d", r=ROWS)
    out_rolled = out.rearrange("a (t r) c d -> a r c t d", r=ROWS)
    col_pieces = (((0, SIDE - SHIFT), (SHIFT, SIDE)), ((SIDE - SHIFT, SIDE), (0, SHIFT)))
    IO_DMAS = ROWS * len(col_pieces)

    with ExitStack() as ctx:
        def sb(name, shape, dt=F32):
            return ctx.enter_context(nc.sbuf_tensor(name, shape, dt))

        def bank(name):
            return ctx.enter_context(nc.psum_tensor(name, [P, HALF], F32))

        def sem(name):
            return ctx.enter_context(nc.semaphore(name))

        k = sb("k_consts", [P, CONST_WIDTH])

        def const(name, rows=P):
            a, b = CONST[name]
            return k[0:rows, a:b]

        ident = const("identity")
        sel = sb("expert_sel", [GATE_PARTS * E, E * P], BF16)
        ident16 = sb("ident16", [P, P], BF16)
        head_ones = sb("head_ones", [P, P], F32R)
        wq_s, wk_s, wv_s, wo_s = (sb(n, [P, P]) for n in ("wq_s", "wk_s", "wv_s", "wo_s"))
        wqkv_s = sb("wqkv_s", [P, 3 * P])
        wp_s = sb("wp_s", [P, P])
        gw_s = sb("gw_s", [P, GATE_N])
        w1_h = sb("w1_h", [P, E * HID], F32R)
        w1_l = sb("w1_l", [P, E * HID], F32R)
        w2_h = sb("w2_h", [P, E * CH * P], F32R)
        w2_l = sb("w2_l", [P, E * CH * P], F32R)
        b1_s = sb("b1_s", [P, E * CH])
        b2_s = sb("b2_s", [GATE_PARTS * E, P])
        b2_p = sb("b2_p", [GATE_PARTS * E, GATE_PARTS, P], BF16)
        b2_r = sb("b2_r", [GATE_PARTS * E, 2, P])
        cols = sb("cols", [P, 8])
        row_a = sb("row_a", [P, P])
        row_b = sb("row_b", [P, P])
        bo_s = sb("bo_s", [P, P])
        gb_s = sb("gb_s", [P, E])
        cw1_s = sb("cw1_s", [2, HID])
        cb1_s = sb("cb1_s", [P, CH])
        cw2_s = sb("cw2_s", [P, CH, HA])
        bias_a = sb("bias_a", [P, 4, HA, WTOK])
        eps5 = sb("eps5", [P, 4])

        pad = sb("pad", [P, 2])

        xin = sb("xin", [P, TILES, D])
        x_res = sb("x_res", [P, TILES, D])
        xn_a = sb("xn_a", [P, TOKENS])
        gstat = sb("gstat", [P, 24])
        qk_a = sb("qk_a", [P, 4, HALF])
        sq_a = sb("sq_a", [P, 4, HALF])
        xraw = sq_a[:, 0:2, :].rearrange("p a n -> p (a n)")
        w1_s = sq_a[:, :, :].rearrange("p a n -> p (a n)")
        w2_s = qk_a[:, :, :].rearrange("p a n -> p (a n)")
        km_a = sb("km_a", [P, 2, HA, P])
        v_a = sb("v_a", [P, WINDOWS, P])
        ot_a = sb("ot_a", [P, TOKENS])
        t1 = sb("t1", [P, TILES, D])
        st_b = sb("st_b", [P, TILES, 6])
        mv_b = sb("mv_b", [P, TILES, 2])
        rs_b = sb("rs_b", [P, 3, TILES])
        xt_b = sb("xt_b", [P, TOKENS])
        q_b = sb("q_b", [P, TOKENS])
        k_b = sb("k_b", [P, TOKENS])
        km_b = sb("km_b", [P, 2, HB, P])
        v_b = sb("v_b", [P, TOKENS])
        ot_b = sb("ot_b", [P, TOKENS])
        t2 = sb("t2", [P, TILES, D])
        st_c = sb("st_c", [P, TILES, 6])
        mv_c = sb("mv_c", [P, TILES, 2])
        rs_c = sb("rs_c", [P, 3, TILES])
        xn_c = sb("xn_c", [P, TILES, D])
        xh_c = sb("xh_c", [P, TOKENS], F32R)
        xl_c = sb("xl_c", [P, TOKENS], F32R)
        lg = sb("lg", [P, TILES, E])
        pr = sb("pr", [P, TILES, E])
        col_c = sb("col_c", [P, 3, TILES])
        rank_c = sb("rank_c", [P, TILES, E])
        cw = sb("cw", [P, 3, TILES, E])
        cw3 = sb("cw3", [P, TILES, GATE_PARTS, E], BF16)
        cwt = sb("cwt", [GATE_PARTS * E, TOKENS], BF16)
        hid = sb("hid", [P, 8, HALF])
        hid_h = sb("hid_h", [P, 8, HALF], F32R)
        hid_l = sb("hid_l", [P, 4, HALF], F32R)
        xt_c = hid[:, 0:2, :].rearrange("p a n -> p (a n)")
        xn_b = hid[:, 2:4, :].rearrange("p a (t d) -> p (a t) d", d=D)
        cmp_c = [hid[:, 4 + n, :].rearrange("p (t e f) -> p t e f", t=TILES, e=E) for n in range(2)]
        sq_h, sq_l = [hid_h[:, n, :] for n in range(4)], [hid_l[:, n, :] for n in range(4)]
        y_s = sb("y_s", [P, HALF])
        result = [xn_c[:, 0:4, :], hid[:, 6, :].rearrange("p (t d) -> p t d", d=D)]
        hid_s = hid[:, 0:2, 0:REL * REL]
        rel_s = hid[0:HA, 2, 0:REL * REL]
        tab_s = hid[0:2, 3, 0:REL * REL]
        unf_s = hid[0:WS, 4:6, :].rearrange("p a n -> p (a n)")[:, 0:HA * REL * WS].rearrange("p (y w) -> p y w", w=WS)
        fold_s = hid[0:WS, 6:8, :].rearrange("p a n -> p (a n)")
        s_sb = [sb("s_sb_a", [P, HA, WTOK]), sb("s_sb_b", [P, HB, P])]
        mx_s = [sb("mx_a", [P, HA]), sb("mx_b", [P, HB])]
        p_sb = [sb("p_sb_a", [P, 4, P]), sb("p_sb_b", [P, 4, P])]
        pt_sb = [sb("pt_sb_a", [P, 4, P]), sb("pt_sb_b", [P, 4, P])]
        sum_inv = sb("sum_inv", [P, 2 * P])

        Z = [bank("bank_z0"), bank("bank_z1")]
        Y, W, SA, SB, T, O = (bank(n) for n in ("bank_y", "bank_w", "bank_sa", "bank_sb", "bank_t", "bank_o"))

        loaded = sem("loaded")
        setup = sem("setup")
        setup_act = sem("setup_act")
        w_split = sem("w_split")
        xt_b_ready, xt_c_ready = sem("xt_b_ready"), sem("xt_c_ready")
        sq_high, sq_low = sem("sq_high"), sem("sq_low")
        xs_ready = sem("xs_ready")
        bias_io = sem("bias_io")
        ready = sem("ready")
        x_in, x_copied, res_ready = sem("x_in"), sem("x_copied"), sem("res_ready")
        gn = sem("gn")
        xt_a_ready = sem("xt_a_ready")
        qk_ready, qk_sb, sq_ready, ss_ready, ln_ready, rn_ready, qn_ready, km_ready, av_ready, av_sb = (
            sem(n) for n in ("qk_ready", "qk_sb", "sq_ready", "ss_ready", "ln_ready", "rn_ready", "qn_ready",
                             "km_ready", "av_ready", "av_sb"))
        outa_ready, outb_ready = sem("outa_ready"), sem("outb_ready")
        ln_b, ln_c = sem("ln_b"), sem("ln_c")
        t1b_ready = sem("t1b_ready")
        bqk_ready, bq_sb, bk_sb, bkm_ready, bv_ready, bv_sb = (
            sem(n) for n in ("bqk_ready", "bq_sb", "bk_sb", "bkm_ready", "bv_ready", "bv_sb"))
        gate = sem("gate")
        two = ("a", "b")
        s_ready, s_added, s_max, s_sub, p_ready, pt_ready, pt_copied, o_ready, o_norm = (
            [sem(f"{n}_{w}") for w in two] for n in ("s_ready", "s_added", "s_max", "s_sub", "p_ready", "pt_ready",
                                                     "pt_copied", "o_ready", "o_norm"))
        web_ready, z_ready, gelu_ready, hw_ready, hi_ready, lo_pool, lo_dve, y_done, y_copied, yt_ready, fin_ready = (
            sem(n) for n in ("web_ready", "z_ready", "gelu_ready", "hw_ready", "hi_ready", "lo_pool", "lo_dve", "y_done", "y_copied", "yt_ready",
                             "fin_ready"))
        stored = [sem("stored_0"), sem("stored_1")]

        sum_logs, sums_inverted = sem("sum_logs"), sem("sums_inverted")

        STEPS = TILES + 1
        LN_STEPS, GN_STEPS, GATE_STEPS = 31, 18, 21
        DVE_LOW = 3
        UNITS = 4 * TILES

        def need(eng, s, image, per, kth):
            v = count(image, per, kth)
            if v is not None:
                eng.wait_ge(s, v)

        def schedule(eng, body):
            def peeled(i):
                body(i, i < IMAGES, 1 <= i <= IMAGES, i >= 2, i + 1 < IMAGES)

            for i in range(3):
                peeled(i)
            with eng.Fori(3, IMAGES - 1) as i:
                body(i, True, True, True, True)
            for i in range(IMAGES - 1, IMAGES + 2):
                peeled(i)

        def unit(t, m):
            return t // 4, 2 * (t % 4) + m // 2, m % 2

        def low_part(c, t, m):
            if m == DVE_LOW:
                return lo_dve, c, TILES, t + 1
            return lo_pool, c, 3 * TILES, 3 * t + m + 1

        block = ctx.enter_context(nc.Block())

        loads = [(k[:], consts), (tab_s, rel_table), (fold_s, unfold), (sel[:], selectors), (wq_s[:], wq),
                 (wk_s[:], wk), (wv_s[:], wv), (wo_s[:], wo),
                 (wqkv_s[:], w_qkv), (wp_s[:], w_proj), (gw_s[:, 0:E], gate_w),
                 (w1_s.rearrange("p (e n) -> p e n", e=E), w1.rearrange("e p n -> p e n")),
                 (w2_s.rearrange("p (e c n) -> p e c n", e=E, c=CH), w2.rearrange("e (c p) n -> p e c n", p=P)), (b1_s[:], b1),
                 (cols[:, 0:1], bq), (cols[:, 1:2], bk), (cols[:, 2:3], bv), (cols[:, 3:4], logit_scale),
                 (row_b[:], b_proj.to_broadcast([P, P])), (bo_s[:], bo.to_broadcast([P, P])),
                 (gb_s[:], gate_b.to_broadcast([P, E])), (cw1_s[:], cpb_w1), (cb1_s[:], cpb_b1),
                 (cw2_s[:], cpb_w2.rearrange("(c p) n -> p c n", p=P))]
        loads += [(b2_s[E * g:E * g + E, :], b2) for g in range(GATE_PARTS)]

        @block.sync
        def _(sp):
            for dst, src in loads:
                sp.dma_start(dst, src).then_inc(loaded, 16)

            def load_image(i):
                for r in range(ROWS):
                    for (p0, p1), (c0, c1) in col_pieces:
                        sp.dma_start(xin[SIDE * r + p0:SIDE * r + p1, :, :], x_rolled[i, r, c0:c1, :, :]).then_inc(x_in, 16)

            def store_half(c, half):
                need(sp, fin_ready, c, 2, half + 1)
                for r in range(ROWS):
                    for (p0, p1), (c0, c1) in col_pieces:
                        sp.dma_start(out_rolled[c, r, c0:c1, 4 * half:4 * half + 4, :],
                                     result[half][SIDE * r + p0:SIDE * r + p1, :, :]).then_inc(stored[half], 16)

            load_image(0)
            sp.wait_ge(setup, 9)
            sp.dma_start(scratch.ap(), rel_s).then_inc(bias_io, 16)
            sp.wait_ge(bias_io, 16)
            unfolded = bass.AP(scratch, 0, [[1, WS], [REL, HA * REL], [1, WS]])
            sp.dma_start(unf_s, unfolded).then_inc(bias_io, 16)

            def body(i, do_a, do_b, do_c, do_next):
                a, b, c = i, i - 1, i - 2
                if not isinstance(i, int) or i >= 3:
                    store_half(c - 1, 1)
                if do_a:
                    need(sp, x_in, a, 16 * IO_DMAS, 16 * IO_DMAS)
                    need(sp, ln_b, b, LN_STEPS, 2)
                    sp.dma_start(x_res[:], xin[:]).then_inc(x_copied, 16)
                if do_next:
                    need(sp, xt_a_ready, a, 2, 2)
                    need(sp, x_copied, a, 16, 16)
                    load_image(i + 1)
                if do_c:
                    store_half(c, 0)

            schedule(sp, body)
            store_half(IMAGES - 1, 1)
            for half in range(2):
                sp.wait_ge(stored[half], 16 * IO_DMAS * IMAGES)

        @block.tensor
        def _(pe):
            mm, tr = pe.matmul, pe.transpose
            pe.wait_ge(loaded, 16 * len(loads))
            for c in range(CH):
                last = mm(Z[c][:, 0:REL * REL], cw1_s[:, c * P:(c + 1) * P], tab_s, start=True, stop=True)
            last.then_inc(setup, 1)
            pe.wait_ge(setup, 3)
            for c in range(CH):
                last = mm(Y[0:HA, 0:REL * REL], cw2_s[:, c, :], hid_s[:, c, :], start=(c == 0), stop=(c == CH - 1))
            last.then_inc(setup, 1)
            mm(W[:, 0:P], cols[:, 2:3].to_broadcast([P, P]), wo_s[:], start=True, stop=True).then_inc(setup, 1)
            pe.wait_ge(bias_io, 32)
            for py in range(WS):
                last = mm(SA[:, :].rearrange("p (h n) -> p h n", h=HA), fold_s[:, py * P:py * P + P],
                          unf_s.rearrange("p (h y) w -> p h (y w)", h=HA)[:, :, py * WS:py * WS + WTOK],
                          start=(py == 0), stop=(py == WS - 1))
            last.then_inc(setup, 1)
            pe.wait_ge(ready, 3)

            def tokens(j):
                return slice(P * j, P * j + P)

            def rolled(t):
                return (t - SHIFT // ROWS) % TILES

            def window(w):
                return slice(WTOK * w, WTOK * w + WTOK)

            q_flat = qk_a[:, 0:2, :].rearrange("p a n -> p (a n)")

            def image_half(f, h, free):
                need(pe, x_in, f, 16 * IO_DMAS, 16 * IO_DMAS)
                free()
                for j in range(4):
                    tile = (4 * h + j + SHIFT // ROWS) % TILES
                    last = tr(T[:, P * j:P * j + P], xin[:, tile, :], ident)
                last.then_inc(xt_a_ready, 1)

            def group_stats(f, step, free):
                need(pe, gn, f, GN_STEPS, step - 1)
                free()
                if step == 6:
                    mm(O[:, 0:2], const("group_mean"), gstat[:, 12:14], start=True, stop=True).then_inc(gn, 1)
                else:
                    mm(O[:, 2:3], const("group_mean"), gstat[:, 17:18], start=True, stop=True).then_inc(gn, 1)

            def queries(f, h):
                need(pe, gn, f, GN_STEPS, GN_STEPS)
                need(pe, gelu_ready, f - 3, UNITS, UNITS)
                mm(Z[h][:, :], wq_s[:], xn_a[:, HALF * h:HALF * h + HALF], start=True, stop=True).then_inc(qk_ready, 1)

            def window_values(a, g, dst):
                need(pe, qk_sb, a, 4, g + 1)
                for j in range(4):
                    for half in range(2):
                        last = mm(dst[WTOK * half:WTOK * half + WTOK, P * j:P * j + P],
                                  xn_a[:, window(4 * g + j)], wv_s[:], start=True, stop=True)
                last.then_inc(av_ready, 1)

            def banded_values(a, b, c):
                for h, dst in enumerate((T, O)):
                    need(pe, ln_ready, a, 4, 3 + h)
                    if h == 0:
                        need(pe, pt_copied[0], b, TILES, TILES)
                        need(pe, pt_copied[1], b - 1, TILES, TILES)
                        need(pe, fin_ready, c - 1, 2, 2)
                    else:
                        need(pe, o_norm[0], b, TILES, TILES)
                        need(pe, o_norm[1], b - 1, TILES, TILES)
                    for j in range(4):
                        last = mm(dst[:, P * j:P * j + P], xt_b[:, tokens(4 * h + j)], wqkv_s[:, 2 * P:3 * P],
                                  start=True, stop=True)
                    last.then_inc(bv_ready, 1)

            def squared_norms(a, n, dst):
                need(pe, sq_low, a, 4, n + 1)
                need(pe, av_sb, a, 8, 2 * n + 2)
                mm(dst[:, :], head_ones[:], sq_h[n], start=True, stop=False)
                mm(dst[:, :], head_ones[:], sq_l[n], start=False, stop=True).then_inc(ss_ready, 1)

            def banded_out(h, dst):
                for j in range(4):
                    last = mm(dst[:, P * j:P * j + P], ot_b[:, tokens(4 * h + j)], wp_s[:], start=True, stop=True)
                last.then_inc(outb_ready, 1)

            def prepare(i, do_a, do_b, do_c):
                a, b, c = i, i - 1, i - 2

                def last_y_free():
                    need(pe, pt_copied[0], b, TILES, TILES)
                    need(pe, pt_copied[1], b - 1, TILES, TILES)
                    need(pe, fin_ready, c - 1, 2, 1)

                if do_c:
                    need(pe, o_norm[1], c, TILES, TILES)
                    need(pe, hw_ready, c - 1, UNITS, UNITS)
                    banded_out(1, W)
                if 0 <= i - 3 or not isinstance(i, int):
                    transposed_y(1, c - 1, last_y_free)
                if do_c:
                    need(pe, y_copied, c - 1, 2, 2)
                    banded_out(0, Y)
                if do_b:
                    need(pe, o_norm[0], b, TILES, TILES)
                    need(pe, s_added[0], b, TILES, TILES)
                    need(pe, s_added[1], b - 1, TILES, TILES)
                    for h, dst in enumerate((SA, SB)):
                        for j in range(4):
                            t = 4 * h + j
                            last = mm(dst[:, P * j:P * j + P], ot_a[:, tokens(rolled(t))], wo_s[:], start=True, stop=True)
                        last.then_inc(outa_ready, 1)
                if do_a:
                    for g in range(2):
                        window_values(a, g, Z[g])
                    need(pe, pt_copied[0], b, TILES, TILES)
                    need(pe, pt_copied[1], b - 1, TILES, TILES)
                    need(pe, fin_ready, c - 1, 2, 2)
                    need(pe, o_norm[0], b, TILES, TILES)
                    need(pe, o_norm[1], b - 1, TILES, TILES)
                    for h, dst in enumerate((T, O)):
                        mm(dst[:, :], wk_s[:], xn_a[:, HALF * h:HALF * h + HALF], start=True, stop=True).then_inc(qk_ready, 1)
                    for n in range(2):
                        squared_norms(a, n, Z[n])
                    for g, dst in ((2, T), (3, O)):
                        window_values(a, g, dst)
                if do_c:
                    need(pe, ln_c, c, LN_STEPS, 29)
                    for h, dst in enumerate((Y, W)):
                        for j in range(4):
                            last = tr(dst[:, P * j:P * j + P], xn_c[:, 4 * h + j, :], ident)
                        last.then_inc(xt_c_ready, 1)
                if do_a:
                    for n, dst in ((2, T), (3, O)):
                        squared_norms(a, n, dst)
                if do_c:
                    need(pe, ln_c, c, LN_STEPS, 31)
                    need(pe, xs_ready, c, 4, 2)
                    for t in range(TILES):
                        at = GATE_STRIDE * t
                        last = mm(W[:, at:at + GATE_N], xt_c[:, tokens(t)], gw_s[:], start=True, stop=True)
                    last.then_inc(gate, 1)
                if do_b:
                    need(pe, ln_b, b, LN_STEPS, 29)
                    for h, dst in enumerate((SA, SB)):
                        for j in range(4):
                            last = tr(dst[:, P * j:P * j + P], xn_b[:, 4 * h + j, :], ident)
                        last.then_inc(xt_b_ready, 1)
                if do_b:
                    for n, (w0, dst) in enumerate(((0, SA), (0, SB), (P, Z[0]), (P, Z[1]))):
                        h = n % 2
                        need(pe, ln_b, b, LN_STEPS, 30 + h)
                        if n >= 2:
                            need(pe, ln_ready, a, 4, n - 1)
                            need(pe, gelu_ready, c - 1, UNITS, UNITS)
                        mm(dst[:, :], wqkv_s[:, w0:w0 + P], xt_b[:, HALF * h:HALF * h + HALF],
                           start=True, stop=True).then_inc(bqk_ready, 1)

            def gate_rows(c):
                need(pe, gate, c, GATE_STEPS, 19)
                wt = W[:, :].bitcast(BF16)
                for t in range(TILES):
                    last = tr(wt[0:GATE_PARTS * E, tokens(t)], cw3[:, t, :, :].rearrange("p g e -> p (g e)"), ident16[:])
                last.then_inc(gate, 1)

            def expert_bias(c, half):
                need(pe, gate, c, GATE_STEPS, 21)
                if half == 0:
                    need(pe, xs_ready, c, 4, 4)
                else:
                    need(pe, y_copied, c, 2, 1)
                for g in range(GATE_PARTS):
                    mm(Y[:, :], b2_p[:, g, :], cwt[:, HALF * half:HALF * half + HALF], start=(g == 0), stop=False)

            def scores(t, w, a, b):
                if w == 0:
                    need(pe, km_ready, a, TILES, t + 1)
                    need(pe, qn_ready, a, 4, 2 + 2 * (t // 4))
                    need(pe, s_added[0], a, TILES, t)
                    if t == 0:
                        need(pe, bq_sb, b, 2, 1)
                        need(pe, ln_b, b, LN_STEPS, 31)
                    for j in range(2):
                        last = mm(SA[WTOK * j:WTOK * j + WTOK, :], q_flat[:, window(2 * t + j)],
                                  km_a[:, t % 2, :, WTOK * j:WTOK * j + WTOK], start=True, stop=True)
                else:
                    need(pe, bkm_ready, b, TILES, t + 1)
                    need(pe, s_added[1], b, TILES, t)
                    if t == 0:
                        need(pe, bq_sb, b, 2, 2)
                        need(pe, bk_sb, b, 2, 2)
                    last = mm(SB[:, :], q_b[:, tokens(t)], km_b[:, t % 2, :, :], start=True, stop=True)
                last.then_inc(s_ready[w], 1)

            def bank_t_free(t, use, a, b, c, all_on):
                extra = {2: (gn, a + 1, GN_STEPS, 1), 3: (gn, a + 1, GN_STEPS, 2), 5: (fin_ready, c, 2, 1)}
                probs_a, probs_b = (pt_copied[0], a, TILES, t), (pt_copied[1], b, TILES, t)
                last_probs = [(pt_copied[1], b, TILES, t - 1), (pt_copied[0], a, TILES, t - 1)]
                if use == "probs_a":
                    waits = [extra[t - 1]] if t - 1 in extra else last_probs[:1]
                elif use == "probs_b":
                    waits = [probs_a]
                else:
                    waits = [probs_b]
                if t == 1:
                    waits = waits + [(bv_sb, b, 2, 1), (ln_ready, a, 4, 3)]
                elif not all_on:
                    waits = waits + last_probs + [probs_a] * (use == "extra") + [extra[k] for k in extra if k < t]
                for s, n, per, kth in waits:
                    need(pe, s, n, per, kth)

            def transposed_probs(t, w, n, free):
                need(pe, p_ready[w], n, TILES, t + 1)
                free()
                for j in range(4):
                    last = tr(T[:, P * j:P * j + P], p_sb[w][:, j, :], ident)
                last.then_inc(pt_ready[w], 1)

            def weighted_values(t, a, b, do_a, do_b, stats_read):
                if do_a:
                    need(pe, pt_copied[0], a, TILES, t + 1)
                if do_b:
                    need(pe, pt_copied[1], b, TILES, t + 1)
                need(pe, o_norm[0], a, TILES, t)
                need(pe, o_norm[1], b, TILES, t)
                if t == 0:
                    need(pe, av_sb, a, 8, 8)
                    need(pe, ln_ready, a, 4, 4)
                    need(pe, bv_sb, b, 2, 2)
                stats_read()
                if do_a:
                    for win in range(2):
                        queries = slice(WTOK * win, WTOK * win + WTOK)
                        for j in range(PAIRS):
                            mm(O[DB * j:DB * j + DB, queries], v_a[:, 2 * t + win, DB * j:DB * j + DB],
                               pt_sb[0][:, j, queries], start=True, stop=True)
                    for j in range(PAIRS):
                        last = mm(O[DB * j:DB * j + DB, 2 * P:3 * P], const("ones_a"), pt_sb[0][:, j, :], start=True, stop=True)
                    last.then_inc(o_ready[0], 1)
                if do_b:
                    for h in range(HB):
                        mm(O[DB * h:DB * h + DB, P:2 * P], v_b[:, P * t + DB * h:P * t + DB * h + DB], pt_sb[1][:, h, :],
                           start=True, stop=True)
                    for h in range(HB):
                        last = mm(O[DB * h:DB * h + DB, 3 * P:4 * P], const("ones_b"), pt_sb[1][:, h, :], start=True, stop=True)
                    last.then_inc(o_ready[1], 1)

            def spread_weights(t, j, c):
                e, half = 2 * (t % 4) + j, t // 4
                if t == 0 and j == 0:
                    need(pe, gate, c, GATE_STEPS, 21)
                else:
                    need(pe, hw_ready, c, UNITS, 4 * t + 2 * j)
                mm(W[:, :], sel[:, e * P:(e + 1) * P], cwt[:, HALF * half:HALF * half + HALF],
                   start=True, stop=True).then_inc(web_ready, 1)

            def hidden(t, m, b, c):
                half, e, ch = unit(t, m)
                if 4 * t + m < 2:
                    need(pe, xs_ready, c, 4, 4)
                    need(pe, bk_sb, b, 2, 1 + m)
                    need(pe, ln_ready, b + 1, 4, 1 + m)
                else:
                    need(pe, gelu_ready, c, UNITS, 4 * t + m - 1)
                w = slice(HID * e + P * ch, HID * e + P * ch + P)
                x = slice(HALF * half, HALF * half + HALF)
                mm(Z[m % 2][:, :], w1_h[:, w], xh_c[:, x], start=True, stop=False)
                mm(Z[m % 2][:, :], w1_h[:, w], xl_c[:, x], start=False, stop=False)
                mm(Z[m % 2][:, :], w1_l[:, w], xh_c[:, x], start=False, stop=True).then_inc(z_ready, 1)

            def expert_out(t, m, c):
                half, e, ch = unit(t, m)
                if t % 4 == 0 and m == 0:
                    expert_bias(c, half)
                w, slot = slice(P * (CH * e + ch), P * (CH * e + ch) + P), 4 * (t % 2) + m
                need(pe, hi_ready, c, UNITS, 4 * t + m + 1)
                mm(Y[:, :], w2_h[:, w], hid_h[:, slot, :], start=False, stop=False)
                mm(Y[:, :], w2_l[:, w], hid_h[:, slot, :], start=False, stop=False)
                need(pe, *low_part(c, t, m))
                mm(Y[:, :], w2_h[:, w], hid_l[:, m, :], start=False, stop=(t % 4 == 3 and m == 3)).then_inc(y_done, 1)

            def transposed_y(half, c, free):
                need(pe, y_copied, c, 2, half + 1)
                free()
                for j in range(4):
                    last = tr(T[:, P * j:P * j + P], y_s[:, P * j:P * j + P], ident)
                last.then_inc(yt_ready, 1)

            for h in range(2):
                image_half(0, h, lambda: need(pe, gn, 0, GN_STEPS, h))
            group_stats(0, 6, lambda: None)
            group_stats(0, 10, lambda: None)
            for h in range(2):
                queries(0, h)

            def body(i, do_a, do_b, do_c, do_next):
                a, b, c = i, i - 1, i - 2
                all_on = do_a and do_b and do_c and do_next
                prepare(i, do_a, do_b, do_c)
                for t in range(STEPS):
                    now, before = t < TILES, t > 0

                    def t_free(use):
                        return lambda: bank_t_free(t, use, a, b, c, all_on)

                    def o_free():
                        need(pe, o_norm[1], b, TILES, t - 1)
                        need(pe, o_norm[0], a, TILES, t - 1)

                    def stats_read():
                        if do_next and t in (5, 6):
                            need(pe, gn, a + 1, GN_STEPS, 7 if t == 5 else 11)

                    if do_c and t == 0:
                        hidden(0, 0, b, c)
                        hidden(0, 1, b, c)
                    if do_b and t == 0:
                        banded_values(a, b, c)
                    if do_a and now:
                        scores(t, 0, a, b)
                    if do_b and now:
                        scores(t, 1, a, b)
                    if do_c and t == 0:
                        gate_rows(c)
                    if do_c and t == 1:
                        spread_weights(0, 1, c)
                    if do_c and t == 0:
                        hidden(t, 2, b, c)
                        hidden(t, 3, b, c)
                    if do_c and t == 0:
                        spread_weights(t, 0, c)
                    if do_c and now and t > 0:
                        if t != 1:
                            spread_weights(t, 0, c)
                        hidden(t, 0, b, c)
                        hidden(t, 1, b, c)
                        if t == 1:
                            spread_weights(t, 0, c)
                    if do_next and t in (5, 6):
                        group_stats(a + 1, 6 if t == 5 else 10, o_free)
                    if do_c and t == TILES:
                        expert_out(t - 1, 0, c)
                    if do_a and before:
                        transposed_probs(t - 1, 0, a, t_free("probs_a"))
                    if do_c and 0 < t < TILES:
                        expert_out(t - 1, 0, c)
                    if do_c and now and t > 0:
                        hidden(t, 2, b, c)
                    if do_next and t == TILES:
                        queries(a + 1, 0)
                    if do_b and before:
                        transposed_probs(t - 1, 1, b, t_free("probs_b"))
                    if do_c and before:
                        expert_out(t - 1, 1, c)
                    if do_c and now and t > 0:
                        hidden(t, 3, b, c)
                    if do_next and t == TILES:
                        queries(a + 1, 1)
                    if do_next and t in (2, 3):
                        image_half(a + 1, t - 2, t_free("extra"))
                    if do_c and t == 5:
                        transposed_y(0, c, t_free("extra"))
                    if (do_a or do_b) and before:
                        weighted_values(t - 1, a, b, do_a, do_b, stats_read)
                    if do_c and now and t > 0:
                        spread_weights(t, 1, c)
                    if do_c and before:
                        expert_out(t - 1, 2, c)
                    if do_c and before:
                        expert_out(t - 1, 3, c)

            schedule(pe, body)
            last_c = IMAGES - 1
            transposed_y(1, last_c, lambda: need(pe, fin_ready, last_c, 2, 1))

        @block.scalar
        def _(act):
            func = act.activation
            act.preload_act_table_set(EXP_LN_SET)
            act.wait_ge(setup, 4)
            func(rel_s, Y[0:HA, 0:REL * REL], ACT.Exp, scale=-1.0).then_inc(setup_act, 1)
            act.wait_ge(loaded, 16 * len(loads))
            act.wait_ge(setup, 13)
            func(cols[:, 5:6], cols[:, 4:5], ACT.Exp).then_inc(setup_act, 1)
            act.wait_ge(setup_act, 2)

            def image_copy(f, h):
                need(act, xt_a_ready, f, 2, h + 1)
                need(act, qn_ready, f - 1, 4, 4)
                func(xraw[:, HALF * h:HALF * h + HALF], T[:, :], ACT.Copy).then_inc(gn, 1)

            def group_rstd(f):
                need(act, gn, f, GN_STEPS, 11)
                func(gstat[:, 19:20], gstat[:, 18:19], ACT.Ln, bias=eps5[:, 0:1]).then_inc(gn, 1)
                need(act, gn, f, GN_STEPS, 12)
                func(gstat[:, 20:21], gstat[:, 19:20], ACT.Exp, scale=-0.5).then_inc(gn, 1)

            def layer_rstd(s, n, mv, rs):
                need(act, s, n, LN_STEPS, 18)
                func(rs[:, 0, :], mv[:, :, 1], ACT.Ln, bias=eps5[:, 0:1]).then_inc(s, 1)
                need(act, s, n, LN_STEPS, 19)
                func(rs[:, 1, :], rs[:, 0, :], ACT.Exp, scale=-0.5).then_inc(s, 1)

            def layer_copy(s, n, banks, dst):
                for h, src in enumerate(banks):
                    need(act, xt_c_ready, n, 2, h + 1)
                    func(dst[:, HALF * h:HALF * h + HALF], src[:, :], ACT.Copy).then_inc(s, 1)

            def queries_keys(f, n, src):
                need(act, s_ready[0], f - 1, TILES, TILES)
                need(act, km_ready, f - 1, TILES, TILES)
                need(act, qk_ready, f, 4, n + 1)
                func(qk_a[:, n, :], src[:, :], ACT.Identity, bias=cols[:, n // 2:n // 2 + 1]).then_inc(qk_sb, 1)

            act.preload_act_table_set(EXP_LN_SET)
            act.wait_ge(ready, 3)
            for h in range(2):
                image_copy(0, h)
            group_rstd(0)
            for h in range(2):
                queries_keys(0, h, Z[h])

            def body(i, do_a, do_b, do_c, do_next):
                a, b, c = i, i - 1, i - 2
                def window_values(g, src):
                    need(act, av_ready, a, 4, g + 1)
                    for par in range(2):
                        ps = slice(WTOK * par, WTOK * par + WTOK)
                        v = src[ps, :].rearrange("p (w j e c) -> p w j e c", w=4, j=PAIRS, e=2)
                        dst = v_a[ps, 4 * g:4 * g + 4, :].rearrange("p w (j e c) -> p w j e c", j=PAIRS, e=2)
                        func(dst[:, :, :, par, :], v[:, :, :, par, :], ACT.Copy).then_inc(av_sb, 1)

                def high_squares(n):
                    need(act, sq_ready, a, 4, n + 1)
                    need(act, y_done, c - 1, UNITS, UNITS)
                    func(sq_h[n], sq_a[:, n, :], ACT.Copy).then_inc(sq_high, 1)

                if do_a:
                    for n in range(2):
                        high_squares(n)
                    need(act, o_ready[0], a - 1, TILES, TILES)
                    window_values(0, Z[0])
                if do_c:
                    layer_rstd(ln_c, c, mv_c, rs_c)
                if do_a:
                    window_values(1, Z[1])
                    for h, src in enumerate((T, O)):
                        queries_keys(a, 2 + h, src)
                    for g, src in ((2, T), (3, O)):
                        high_squares(g)
                        window_values(g, src)

                def log_norm(n, src):
                    need(act, ss_ready, a, 4, n + 1)
                    func(sq_a[:, n, :], src[:, :], ACT.Ln, bias=eps5[:, 1:2], scale=2.0 ** NORM_SHIFT).then_inc(ln_ready, 1)

                if do_c:
                    layer_copy(ln_c, c, (Y, W), xt_c)
                if do_b:
                    layer_rstd(ln_b, b, mv_b, rs_b)
                if do_c:
                    need(act, z_ready, c - 1, UNITS, UNITS)
                    for h in (1, 0):
                        src = (Y, W)[h]
                        func(xh_c[:, HALF * h:HALF * h + HALF], src[:, :], ACT.Copy).then_inc(xs_ready, 1)
                if do_a:
                    for n, src in enumerate((*Z, T, O)):
                        log_norm(n, src)
                if do_c:
                    need(act, gate, c, GATE_STEPS, 4)
                    func(pr[:, :, :], lg[:, :, :], ACT.Exp).then_inc(gate, 1)
                if do_a:
                    for n in (2, 0, 3, 1):
                        need(act, ln_ready, a, 4, n + 1)
                        func(sq_a[:, n, :], sq_a[:, n, :], ACT.Exp, scale=-0.5,
                             bias=eps5[:, 2 + n // 2:3 + n // 2]).then_inc(rn_ready, 1)
                if do_c:
                    act.preload_act_table_set(GELU_SET)
                if do_b:
                    need(act, bkm_ready, b - 1, TILES, TILES)
                    for h in range(2):
                        need(act, bqk_ready, b, 4, 3 + h)
                        func(k_b[:, HALF * h:HALF * h + HALF], Z[h][:, :], ACT.Copy).then_inc(bk_sb, 1)
                    need(act, s_ready[1], b - 1, TILES, TILES)
                    for h, src in enumerate((SA, SB)):
                        need(act, bqk_ready, b, 4, 1 + h)
                        func(q_b[:, HALF * h:HALF * h + HALF], src[:, :], ACT.Copy).then_inc(bq_sb, 1)
                for t in range(STEPS):
                    now, before = t < TILES, t > 0

                    def gelu(m):
                        _, e, ch = unit(t, m)
                        need(act, z_ready, c, UNITS, 4 * t + m + 1)
                        if t == 1 and m == 2:
                            need(act, stored[1], c - 1, 16 * IO_DMAS, 16 * IO_DMAS)
                        if t >= 2:
                            need(act, *low_part(c, t - 2, m))
                        else:
                            need(act, *low_part(c - 1, TILES - 2 + t, m))
                        func(hid[:, 4 * (t % 2) + m, :], Z[m % 2][:, :], ACT.Gelu,
                             bias=b1_s[:, CH * e + ch:CH * e + ch + 1]).then_inc(gelu_ready, 1)

                    def probs_copy(w, n):
                        need(act, pt_ready[w], n, TILES, t)
                        if t >= 2:
                            need(act, o_ready[w], n, TILES, t - 1)
                        else:
                            need(act, o_ready[w], n - 1, TILES, TILES)
                        func(pt_sb[w][:, :, :].rearrange("p j n -> p (j n)"), T[:, :], ACT.Copy).then_inc(pt_copied[w], 1)

                    def probs(w, n):
                        need(act, s_sub[w], n, TILES, t + 1)
                        need(act, pt_ready[w], n, TILES, t)
                        func(p_sb[w][:, :, :].rearrange("p j n -> p (j n)"), s_sb[w][:, :, :].rearrange("p h n -> p (h n)"),
                             ACT.Exp, scale=1.0 if w == 0 else float(DB) ** -0.5).then_inc(p_ready[w], 1)

                    if do_c and now:
                        gelu(0)
                        gelu(1)
                    if do_b and t == 0:
                        for h, src in enumerate((T, O)):
                            need(act, bv_ready, b, 2, h + 1)
                            need(act, o_ready[1], b - 1, TILES, TILES)
                            func(v_b[:, HALF * h:HALF * h + HALF], src[:, :], ACT.Copy).then_inc(bv_sb, 1)
                    if do_c and t == 0:
                        need(act, gate, c, GATE_STEPS, 20)
                        func(cwt[:, :], W[:, :].bitcast(BF16)[0:GATE_PARTS * E, :], ACT.Copy).then_inc(gate, 1)
                    if do_a and before:
                        probs_copy(0, a)
                    if do_next and t == TILES:
                        queries_keys(a + 1, 0, Z[0])
                    if do_c and now:
                        gelu(2)
                    if do_b and before:
                        probs_copy(1, b)
                    if do_next and t == TILES:
                        queries_keys(a + 1, 1, Z[1])
                    if do_c and now:
                        gelu(3)
                    if do_next and t in (2, 3):
                        image_copy(a + 1, t - 2)
                    if now:
                        act.preload_act_table_set(EXP_LN_SET)
                    if (do_a or do_b) and before:
                        need(act, o_ready[0], a, TILES, t)
                        need(act, o_ready[1], b, TILES, t)
                        need(act, o_norm[0], a, TILES, t - 1)
                        need(act, o_norm[1], b, TILES, t - 1)
                        lo, hi = (0 if do_a else P), (2 * P if do_b else P)
                        func(sum_inv[:, lo:hi], O[:, 2 * P + lo:2 * P + hi], ACT.Ln).then_inc(sum_logs, 1)
                        act.wait_ge(sum_logs, i * TILES + t)
                        func(sum_inv[:, lo:hi], sum_inv[:, lo:hi], ACT.Exp, scale=-1.0).then_inc(sums_inverted, 1)
                    if do_next and t == 6:
                        group_rstd(a + 1)
                    if now:
                        if do_a:
                            probs(0, a)
                        if do_b:
                            probs(1, b)
                        if do_c and t < TILES - 1:
                            act.preload_act_table_set(GELU_SET)
                    if do_c and t == 4:
                        need(act, y_done, c, UNITS, 4 * t)
                        func(y_s[:, :], Y[:, :], ACT.Copy).then_inc(y_copied, 1)
                if do_c:
                    need(act, y_done, c, UNITS, UNITS)
                    need(act, yt_ready, c, 2, 1)
                    func(y_s[:, :], Y[:, :], ACT.Copy).then_inc(y_copied, 1)

            schedule(act, body)

        @block.gpsimd
        def _(pool):
            pool.memset(v_a[:, :, :], 0.0).then_inc(setup_act, 1)
            pool.wait_ge(ready, 3)

            def low_hidden(eng, c, t, m):
                slot = 4 * (t % 2) + m
                need(eng, hi_ready, c, UNITS, 4 * t + m + 1)
                if t > 0:
                    need(eng, y_done, c, UNITS, 4 * (t - 1) + m + 1)
                eng.tensor_tensor(hid_l[:, m, :], hid[:, slot, :], hid_h[:, slot, :].bitcast(F32),
                                  ALU.subtract).then_inc(low_part(c, t, m)[0], 1)

            def masked_keys(w, n, t):
                need(pool, s_ready[w], n, TILES, t - 1)
                if t < 2:
                    need(pool, s_ready[w], n - 1, TILES, TILES)
                if w == 0:
                    need(pool, qn_ready, n, 4, 1 + 2 * (t // 4))
                    keys, mask, dst, s = qk_a[:, 2 + t // 4, P * (t % 4):P * (t % 4) + P], const("head_mask_a"), km_a, km_ready
                else:
                    need(pool, bk_sb, n, 2, 1 + t // 4)
                    keys, mask, dst, s = k_b[:, P * t:P * t + P], const("head_mask_b"), km_b, bkm_ready
                shape = [P, (HA, HB)[w], P]
                pool.tensor_tensor(dst[:, t % 2, :, :], keys[:, None, :].to_broadcast(shape),
                                   mask[:, :, None].to_broadcast(shape), ALU.mult).then_inc(s, 1)

            def body(i, do_a, do_b, do_c, do_next):
                a, b, c = i, i - 1, i - 2

                def squares(pair):
                    for n in pair:
                        need(pool, qk_sb, a, 4, n + 1)
                        if n < 2:
                            need(pool, gn, a, GN_STEPS, GN_STEPS)
                        pool.tensor_tensor(sq_a[:, n, :], qk_a[:, n, :], qk_a[:, n, :], ALU.mult).then_inc(sq_ready, 1)
                    for n in pair:
                        need(pool, sq_high, a, 4, n + 1)
                        pool.tensor_tensor(sq_l[n], sq_a[:, n, :], sq_h[n].bitcast(F32), ALU.subtract).then_inc(sq_low, 1)

                if do_a:
                    squares((0, 1))
                    squares((2, 3))
                if do_c:
                    need(pool, z_ready, c - 1, UNITS, UNITS)
                    for h in (1, 0):
                        need(pool, xs_ready, c, 4, 2)
                        span = slice(HALF * h, HALF * h + HALF)
                        pool.tensor_tensor(xl_c[:, span], xt_c[:, span], xh_c[:, span].bitcast(F32),
                                           ALU.subtract).then_inc(xs_ready, 1)
                if do_b:
                    need(pool, ln_b, b, LN_STEPS, 29)
                    pool.tensor_tensor(t1[:, :, :], t1[:, :, :], row_b[:, None, :].to_broadcast([P, TILES, D]),
                                       ALU.add).then_inc(t1b_ready, 1)
                if do_a:
                    masked_keys(0, a, 0)
                if do_b:
                    masked_keys(1, b, 0)
                for t in range(TILES):
                    if t + 1 < TILES:
                        if do_a:
                            masked_keys(0, a, t + 1)
                        if do_b:
                            masked_keys(1, b, t + 1)
                    for w, n, on, s, m, width in ((0, a, do_a, s_sb[0], mx_s[0], WTOK), (1, b, do_b, s_sb[1], mx_s[1], P)):
                        if on:
                            need(pool, s_max[w], n, TILES, t + 1)
                            h = (HA, HB)[w]
                            pool.tensor_tensor(s[:, :, :], s[:, :, :], m[:, :, None].to_broadcast([P, h, width]),
                                               ALU.subtract).then_inc(s_sub[w], 1)
                    if do_c:
                        for chunk in range(4):
                            if chunk != DVE_LOW:
                                low_hidden(pool, c, t, chunk)
                    if t == 1 and do_a:
                        need(pool, x_copied, a, 16, 16)
                        pool.tensor_tensor(x_res[:, :, :], x_res[:, :, :], row_a[:, None, :].to_broadcast([P, TILES, D]),
                                           ALU.add).then_inc(res_ready, 1)

            schedule(pool, body)

        @block.vector
        def _(dve):
            tt, ts, stt = dve.tensor_tensor, dve.tensor_scalar, dve.scalar_tensor_tensor
            dve.memset(gw_s[:, E:], 0.0)
            dve.wait_ge(loaded, 16 * len(loads))
            dve.tensor_copy(w1_h[:], w1_s).then_inc(w_split, 1)
            dve.tensor_copy(w2_h[:], w2_s).then_inc(w_split, 1)
            dve.wait_ge(w_split, 2)
            tt(w1_l[:], w1_s, w1_h[:].bitcast(F32), ALU.subtract).then_inc(w_split, 1)
            tt(w2_l[:], w2_s, w2_h[:].bitcast(F32), ALU.subtract).then_inc(w_split, 1)
            dve.wait_ge(setup, 1)
            for c in range(CH):
                ts(hid_s[:, c, :], Z[c][:, 0:REL * REL], cb1_s[:, c:c + 1], 0.0, ALU.add, ALU.max).then_inc(setup, 1)
            dve.wait_ge(setup, 5)
            dve.wait_ge(setup_act, 2)
            tt(row_a[:], W[:, 0:P], bo_s[:], ALU.add).then_inc(setup, 1)
            ts(rel_s, rel_s, 1.0, None, ALU.add).then_inc(setup, 1)
            dve.wait_ge(setup, 7)
            dve.reciprocal(rel_s, rel_s).then_inc(setup, 1)
            dve.wait_ge(setup, 8)
            ts(rel_s, rel_s, 16.0, None, ALU.mult).then_inc(setup, 1)
            dve.wait_ge(setup, 10)
            for kind in range(4):
                a = CONST["mask_a"][0] + kind * WTOK
                last = tt(bias_a[:, kind, :, :], SA[:, :].rearrange("p (h n) -> p h n", h=HA),
                          k[:, None, a:a + WTOK].to_broadcast([P, HA, WTOK]), ALU.add)
            last.then_inc(setup, 1)
            dve.tensor_copy(head_ones[:], const("head_ones"))
            dve.tensor_copy(ident16[:], ident).then_inc(setup, 1)
            ts(cols[:, 4:5], cols[:, 3:4], float(np.log(100.0)), None, ALU.min).then_inc(setup, 1)
            dve.wait_ge(setup, 13)
            dve.memset(eps5[:, 0:1], 1e-5)
            dve.memset(eps5[:, 1:2], 2.0 ** -64)
            ts(eps5[:, 2:3], cols[:, 4:5], NORM_SHIFT * LN2 / 2, None, ALU.add)
            dve.memset(eps5[:, 3:4], NORM_SHIFT * LN2 / 2)
            dve.wait_ge(setup_act, 3)
            ts(cols[:, 6:7], cols[:, 5:6], NORM_CAP, None, ALU.mult)
            dve.tensor_copy(b2_p[:, 0, :], b2_s[:]).then_inc(setup, 1)
            dve.wait_ge(setup, 14)
            tt(b2_r[:, 0, :], b2_s[:], b2_p[:, 0, :], ALU.subtract).then_inc(setup, 1)
            dve.wait_ge(setup, 15)
            dve.tensor_copy(b2_p[:, 1, :], b2_r[:, 0, :]).then_inc(setup, 1)
            dve.wait_ge(setup, 16)
            tt(b2_r[:, 1, :], b2_r[:, 0, :], b2_p[:, 1, :], ALU.subtract).then_inc(setup, 1)
            dve.wait_ge(setup, 17)
            dve.wait_ge(w_split, 4)
            dve.tensor_copy(b2_p[:, 2, :], b2_r[:, 1, :]).then_inc(ready, 3)

            def residual(s, n, banks, old, new):
                for h, src in enumerate(banks):
                    tt(new[:, 4 * h:4 * h + 4, :].rearrange("p t d -> p (t d)"), src[:, :],
                       old[:, 4 * h:4 * h + 4, :].rearrange("p t d -> p (t d)"), ALU.add).then_inc(s, 1)

            def layer_norm_stats(s, n, tok, st, mv):
                need(dve, s, n, LN_STEPS, 2)
                for t in range(TILES):
                    dve.bn_stats(st[:, t, :], tok[:, t, :]).then_inc(s, 1)
                need(dve, s, n, LN_STEPS, 10)
                dve.memset(pad[:, 0:1], 0.0)
                for t in range(TILES):
                    dve.bn_aggr(mv[:, t, :], st[:, t, :]).then_inc(s, 1)

            def layer_norm_apply(s, n, tok, mv, rs, xn):
                need(dve, s, n, LN_STEPS, 20)
                stt(rs[:, 2, :], mv[:, :, 0], -1.0, rs[:, 1, :], ALU.mult, ALU.mult).then_inc(s, 1)
                need(dve, s, n, LN_STEPS, 21)
                for t in range(TILES):
                    ts(xn[:, t, :], tok[:, t, :], rs[:, 1, t:t + 1], rs[:, 2, t:t + 1], ALU.mult, ALU.add).then_inc(s, 1)

            def group_norm_stats(f):
                for h in range(2):
                    need(dve, gn, f, GN_STEPS, 2)
                    dve.bn_stats(gstat[:, 6 * h:6 * h + 6], xraw[:, HALF * h:HALF * h + HALF]).then_inc(gn, 1)
                need(dve, gn, f, GN_STEPS, 4)
                dve.memset(pad[:, 1:2], 0.0)
                dve.bn_aggr(gstat[:, 12:14], gstat[:, 0:12]).then_inc(gn, 1)

            def group_norm_means(f):
                need(dve, gn, f, GN_STEPS, 6)
                dve.tensor_copy(gstat[:, 14:16], O[:, 0:2]).then_inc(gn, 1)
                need(dve, gn, f, GN_STEPS, 7)
                tt(gstat[:, 16:17], gstat[:, 12:13], gstat[:, 14:15], ALU.subtract).then_inc(gn, 1)
                need(dve, gn, f, GN_STEPS, 8)
                tt(gstat[:, 17:18], gstat[:, 16:17], gstat[:, 16:17], ALU.mult).then_inc(gn, 1)

            def group_norm_variance(f):
                need(dve, gn, f, GN_STEPS, 10)
                tt(gstat[:, 18:19], O[:, 2:3], gstat[:, 15:16], ALU.add).then_inc(gn, 1)

            def group_norm_apply(a):
                need(dve, gn, a, GN_STEPS, 13)
                need(dve, av_ready, a - 1, 4, 4)
                stt(gstat[:, 21:22], gstat[:, 14:15], -1.0, gstat[:, 20:21], ALU.mult, ALU.mult).then_inc(gn, 1)
                need(dve, gn, a, GN_STEPS, 14)
                for wi in range(SIDE // WS):
                    span = slice(WS * SIDE * wi, WS * SIDE * (wi + 1))
                    ts(xn_a[:, span].rearrange("p (w y x) -> p y w x", y=WS, x=WS),
                       xraw[:, span].rearrange("p (y w x) -> p y w x", y=WS, x=WS),
                       gstat[:, 20:21], gstat[:, 21:22], ALU.mult, ALU.add).then_inc(gn, 1)

            def gate_weights(c, first):
                def step(n):
                    need(dve, gate, c, GATE_STEPS, n)

                pb = pr[:, :, :]
                shape = [P, TILES, E, E]
                ge, gt = cmp_c
                if first == 0:
                    step(1)
                    tt(lg[:, :, :], W[:, 0:TILES * GATE_STRIDE].rearrange("p (t n) -> p t n", t=TILES)[:, :, 0:E],
                       gb_s[:, None, :].to_broadcast([P, TILES, E]), ALU.add).then_inc(gate, 1)
                    step(2)
                    dve.tensor_reduce(col_c[:, 0, :], lg[:, :, :], AX_X, ALU.max).then_inc(gate, 1)
                    step(3)
                    tt(lg[:, :, :], lg[:, :, :], col_c[:, 0, :, None].to_broadcast([P, TILES, E]), ALU.subtract).then_inc(gate, 1)
                    return
                step(5)
                dve.tensor_reduce(col_c[:, 1, :], pb, AX_X, ALU.add).then_inc(gate, 1)
                step(6)
                dve.reciprocal(col_c[:, 2, :], col_c[:, 1, :]).then_inc(gate, 1)
                step(7)
                tt(pb, pb, col_c[:, 2, :, None].to_broadcast([P, TILES, E]), ALU.mult).then_inc(gate, 1)
                step(8)
                other, own = pr[:, :, None, :].to_broadcast(shape), pr[:, :, :, None].to_broadcast(shape)
                tt(ge, other, own, ALU.is_equal).then_inc(gate, 1)
                tt(gt, other, own, ALU.is_gt).then_inc(gate, 1)
                step(10)
                flat0 = ge.rearrange("p t e f -> p t (e f)")
                flat1 = gt.rearrange("p t e f -> p t (e f)")
                tt(flat0, flat0, const("tri")[:, None, :].to_broadcast([P, TILES, E * E]), ALU.mult).then_inc(gate, 1)
                step(11)
                tt(flat1, flat1, flat0, ALU.add).then_inc(gate, 1)
                step(12)
                dve.tensor_reduce(rank_c[:, :, :], gt, AX_X, ALU.add).then_inc(gate, 1)
                step(13)
                stt(cw[:, 0, :, :], rank_c[:, :, :], 2.0, pb, ALU.is_lt, ALU.mult).then_inc(gate, 1)
                step(14)
                dve.tensor_copy(cw3[:, :, 0, :], cw[:, 0, :, :]).then_inc(gate, 1)
                step(15)
                tt(cw[:, 1, :, :], cw[:, 0, :, :], cw3[:, :, 0, :], ALU.subtract).then_inc(gate, 1)
                step(16)
                dve.tensor_copy(cw3[:, :, 1, :], cw[:, 1, :, :]).then_inc(gate, 1)
                step(17)
                tt(cw[:, 2, :, :], cw[:, 1, :, :], cw3[:, :, 1, :], ALU.subtract).then_inc(gate, 1)
                step(18)
                dve.tensor_copy(cw3[:, :, 2, :], cw[:, 2, :, :]).then_inc(gate, 1)

            group_norm_stats(0)
            group_norm_means(0)
            group_norm_variance(0)
            group_norm_apply(0)

            def final_add(c, half):
                need(dve, yt_ready, c, 2, half + 1)
                tt(result[half].rearrange("p t d -> p (t d)"), T[:, :],
                   t2[:, 4 * half:4 * half + 4, :].rearrange("p t d -> p (t d)"), ALU.add).then_inc(fin_ready, 1)

            def body(i, do_a, do_b, do_c, do_next):
                a, b, c = i, i - 1, i - 2
                if not isinstance(i, int) or i >= 3:
                    final_add(c - 1, 1)
                if do_c:
                    need(dve, outb_ready, c, 2, 2)
                    need(dve, t1b_ready, c, 1, 1)
                    need(dve, fin_ready, c - 1, 2, 2)
                    residual(ln_c, c, (Y, W), t1, t2)
                    layer_norm_stats(ln_c, c, t2, st_c, mv_c)
                if do_b:
                    need(dve, outa_ready, b, 2, 2)
                    need(dve, res_ready, b, 1, 1)
                    need(dve, ln_c, c, LN_STEPS, 2)
                    need(dve, ln_b, b - 1, LN_STEPS, LN_STEPS)
                    residual(ln_b, b, (SA, SB), x_res, t1)
                if do_c:
                    need(dve, stored[0], c - 1, 16 * IO_DMAS, 16 * IO_DMAS)
                    layer_norm_apply(ln_c, c, t2, mv_c, rs_c, xn_c)
                if do_b:
                    layer_norm_stats(ln_b, b, t1, st_b, mv_b)
                    layer_norm_apply(ln_b, b, t1, mv_b, rs_b, xn_b)
                if do_c:
                    gate_weights(c, 0)
                if do_b:
                    for h, src in enumerate((SA, SB)):
                        need(dve, xt_b_ready, b, 2, h + 1)
                        need(dve, bv_ready, b - 1, 2, 2)
                        dve.tensor_copy(xt_b[:, HALF * h:HALF * h + HALF], src[:, :]).then_inc(ln_b, 1)

                def unit_vectors(n):
                    need(dve, rn_ready, a, 4, 1 + (2, 0, 3, 1).index(n))
                    cap = cols[:, 6:7] if n < 2 else NORM_CAP
                    stt(qk_a[:, n, :], sq_a[:, n, :], cap, qk_a[:, n, :], ALU.min, ALU.mult).then_inc(qn_ready, 1)

                if do_a:
                    unit_vectors(2)
                    unit_vectors(0)
                if do_c:
                    gate_weights(c, 5)
                for t in range(STEPS):
                    now, before = t < TILES, t > 0

                    def biased(w, n):
                        need(dve, s_ready[w], n, TILES, t + 1)
                        if t > 0:
                            need(dve, p_ready[w], n, TILES, t)
                        else:
                            need(dve, p_ready[w], n - 1, TILES, TILES)
                        if w == 0:
                            kind = 2 * (t // 6) + t % 2
                            tt(s_sb[0][:, :, :].rearrange("p h n -> p (h n)"), SA[:, :],
                               bias_a[:, kind, :, :].rearrange("p h n -> p (h n)"), ALU.add).then_inc(s_added[0], 1)
                        else:
                            tt(s_sb[1][:, :, :], SB[:, :].rearrange("p (h n) -> p h n", h=HB),
                               const("mask_b")[:, None, :].to_broadcast([P, HB, P]), ALU.add).then_inc(s_added[1], 1)
                        need(dve, s_added[w], n, TILES, t + 1)
                        dve.tensor_reduce(mx_s[w][:], s_sb[w][:, :, :], AX_X, ALU.max).then_inc(s_max[w], 1)

                    def weigh(m):
                        slot = hid[:, 4 * (t % 2) + m, :]
                        need(dve, gelu_ready, c, UNITS, 4 * t + m + 1)
                        need(dve, web_ready, c, 2 * TILES, 2 * t + m // 2 + 1)
                        tt(slot, slot, W[:, :], ALU.mult).then_inc(hw_ready, 1)

                    def high_hidden(m):
                        slot = 4 * (t % 2) + m
                        need(dve, hw_ready, c, UNITS, 4 * t + m + 1)
                        if t >= 2:
                            need(dve, y_done, c, UNITS, 4 * (t - 2) + m + 1)
                        else:
                            need(dve, y_done, c - 1, UNITS, UNITS)
                        dve.tensor_copy(hid_h[:, slot, :], hid[:, slot, :]).then_inc(hi_ready, 1)

                    def low_hidden(m):
                        slot = 4 * (t % 2) + m
                        need(dve, hi_ready, c, UNITS, 4 * t + m + 1)
                        if t > 0:
                            need(dve, y_done, c, UNITS, 4 * (t - 1) + m + 1)
                        tt(hid_l[:, m, :], hid[:, slot, :], hid_h[:, slot, :].bitcast(F32),
                           ALU.subtract).then_inc(lo_dve, 1)

                    def normalised():
                        dve.wait_ge(sums_inverted, i * TILES + t)
                        if do_a:
                            need(dve, outa_ready, a - 1, 2, 2)
                            y0, x0 = WS * ((t - 1) // 2), 2 * WS * ((t - 1) % 2)
                            dst = ot_a[:, :].rearrange("p (y x) -> p y x", x=SIDE)[:, y0:y0 + WS, x0:x0 + 2 * WS]
                            tt(dst.rearrange("p y (w x) -> p w y x", w=2),
                               O[:, 0:P].rearrange("p (w y x) -> p w y x", w=2, y=WS),
                               sum_inv[:, 0:P].rearrange("p (w y x) -> p w y x", w=2, y=WS), ALU.mult).then_inc(o_norm[0], 1)
                        if do_b:
                            need(dve, outb_ready, b - 1, 2, 2)
                            tt(ot_b[:, P * (t - 1):P * t], O[:, P:2 * P], sum_inv[:, P:2 * P], ALU.mult).then_inc(o_norm[1], 1)

                    if do_next and t == 4:
                        group_norm_stats(a + 1)
                    if do_next and t == 5:
                        group_norm_means(a + 1)
                    if do_next and t == 6:
                        group_norm_variance(a + 1)
                    if do_next and t == 7:
                        group_norm_apply(a + 1)
                    if do_a and now:
                        biased(0, a)
                    if do_b and now:
                        biased(1, b)
                    if do_c and now:
                        weigh(0)
                        weigh(1)
                        high_hidden(0)
                        high_hidden(1)
                    if do_c and t == 5:
                        final_add(c, 0)
                    if do_c and now:
                        weigh(2)
                        weigh(3)
                        high_hidden(2)
                        high_hidden(3)
                        low_hidden(DVE_LOW)
                    if (do_a or do_b) and before:
                        normalised()
                    if do_a and t == 1:
                        unit_vectors(3)
                        unit_vectors(1)
            schedule(dve, body)
            final_add(IMAGES - 1, 1)


_INPUTS = ["x", "wq", "bq", "wk", "bk", "wv", "bv", "wo", "bo", "logit_scale", "cpb_w1", "cpb_b1", "cpb_w2",
           "w_qkv", "w_proj", "b_proj", "gate_w", "gate_b", "w1", "b1", "w2", "b2", "consts", "rel_table", "unfold", "selectors"]


def kernel(x, L0_conv_Wq, L0_conv_bq, L0_conv_Wk, L0_conv_bk, L0_conv_Wv, L0_conv_bv, L0_conv_Wo, L0_conv_bo,
           L0_conv_logit_scale, L0_conv_cpb_w1, L0_conv_cpb_b1, L0_conv_cpb_w2, L1_attn_Wqkv, L1_attn_Wproj,
           L1_attn_bproj, L1_ffn_gate_w, L1_ffn_gate_b, L1_ffn_W1, L1_ffn_b1, L1_ffn_W2, L1_ffn_b2):
    import ml_dtypes
    import concourse.bacc as bacc
    from concourse.bass_utils import run_bass_kernel_spmd

    col, row = (lambda v: np.asarray(v).reshape(-1, 1)), (lambda v: np.asarray(v).reshape(1, -1))
    arrays = dict(zip(_INPUTS, [
        x, np.asarray(L0_conv_Wq).T, col(L0_conv_bq), np.asarray(L0_conv_Wk).T, col(L0_conv_bk),
        np.asarray(L0_conv_Wv).T, col(L0_conv_bv), np.asarray(L0_conv_Wo).T, row(L0_conv_bo),
        col(np.repeat(np.asarray(L0_conv_logit_scale).reshape(-1), DA)),
        np.asarray(L0_conv_cpb_w1).T, np.asarray(L0_conv_cpb_b1).reshape(CH, P).T, np.asarray(L0_conv_cpb_w2).T,
        L1_attn_Wqkv, L1_attn_Wproj, row(L1_attn_bproj), L1_ffn_gate_w, row(L1_ffn_gate_b),
        L1_ffn_W1, np.asarray(L1_ffn_b1).reshape(E * CH, P).T, L1_ffn_W2, L1_ffn_b2,
        *shape_constants(), expert_selectors().astype(ml_dtypes.bfloat16)]))
    nc = bacc.Bacc("TRN2", target_bir_lowering=False, num_devices=1)
    feeds, args = {}, []
    for name in _INPUTS:
        v = np.ascontiguousarray(arrays[name])
        feeds[f"in_{name}_dram"] = v
        args.append(nc.dram_tensor(f"in_{name}_dram", v.shape, mybir.dt.from_np(v.dtype), kind="ExternalInput").ap())
    args.append(nc.dram_tensor("out_0_dram", (IMAGES, SIDE, SIDE, D), F32, kind="ExternalOutput").ap())
    hybrid_kernel(nc, *args)
    return run_bass_kernel_spmd(nc, [feeds], core_ids=[0]).results[0]["out_0_dram"]
```
